# Optimizing a Trainium2 kernel written in Bass

```python
import numpy as np
import jax
import jax.numpy as jnp

def _softmax(x, axis=-1):
    return jax.nn.softmax(x, axis=axis)

def _gelu(x):
    return jax.nn.gelu(x, approximate=True)

def _silu(x):
    return jax.nn.silu(x)

def _sigmoid(x):
    return jax.nn.sigmoid(x)

def _layernorm(x, axis=-1, eps=1e-05):
    m = jnp.mean(x, axis=axis, keepdims=True)
    v = jnp.var(x, axis=axis, keepdims=True)
    return (x - m) / jnp.sqrt(v + eps)

def _scatter_add(tgt, idx, src, axis=0):
    return tgt.at[idx].add(src)

def _segment_sum(src, seg, n):
    return jax.ops.segment_sum(src, seg, n)
kernel_name = 'mk_conv_seq_d2_conv_nchw192_r2_618e9b'

def setup_inputs(seed: int=0):
    np.random.seed(seed)
    _w = jnp.asarray

    def _rec_inputs():
        import jax
        import jax.numpy as jnp
        _gk = jax.random.key(seed)
        x = -0.0005963 + 1.001 * jax.random.normal(jax.random.fold_in(_gk, 1), (4, 96, 32, 32), jnp.float32)
        return x
    x = _rec_inputs()

    def _L0_conv_setup():
        import jax, jax.numpy as jnp
        import numpy as np
        D_MODEL = 96
        D_STATE = 16
        D_CONV = 4
        EXPAND = 2
        D_INNER = EXPAND * D_MODEL
        DT_RANK = (D_MODEL + 15) // 16
        B_SZ, H_IMG, W_IMG = (4, 32, 32)
        LN_EPS = 1e-05

        def _mamba(x, W_in, conv_w, conv_b, W_xproj, W_dt, b_dt, A_log, D, W_out):
            Bb, L, _ = x.shape
            xz = x @ W_in
            xr, z = jnp.split(xz, 2, axis=-1)
            xc = jnp.transpose(xr, (0, 2, 1))
            xc = jax.lax.conv_general_dilated(xc, conv_w[:, None, :], (1,), [(D_CONV - 1, 0)], dimension_numbers=('NCH', 'OIH', 'NCH'), feature_group_count=D_INNER)
            xr = jax.nn.silu(jnp.transpose(xc + conv_b[None, :, None], (0, 2, 1)))
            dbl = xr @ W_xproj
            dt = jax.nn.softplus(dbl[..., :DT_RANK] @ W_dt + b_dt)
            Bm = dbl[..., DT_RANK:DT_RANK + D_STATE]
            Cm = dbl[..., DT_RANK + D_STATE:]
            A = -jnp.exp(A_log)

            def step(h, inp):
                dt_t, B_t, C_t, x_t = inp
                h = jnp.exp(dt_t[:, :, None] * A) * h + (dt_t * x_t)[:, :, None] * B_t[:, None, :]
                y_t = jnp.einsum('ben,bn->be', h, C_t)
                return (h, y_t)
            h0 = jnp.zeros((Bb, D_INNER, D_STATE), x.dtype)
            xs = (dt.transpose(1, 0, 2), Bm.transpose(1, 0, 2), Cm.transpose(1, 0, 2), xr.transpose(1, 0, 2))
            _, ys = jax.lax.scan(step, h0, xs)
            y = ys.transpose(1, 0, 2) + xr * D
            y = y * jax.nn.silu(z)
            return y @ W_out
        key = jax.random.key(seed)
        ks = jax.random.split(key, 8)
        s = lambda k, shape, sc: jax.random.normal(k, shape, jnp.float32) * sc
        dt_bias = float(np.log(np.expm1(0.01)))
        return {'x': jax.random.normal(ks[0], (B_SZ, D_MODEL, H_IMG, W_IMG), jnp.float32), 'gamma': jnp.ones((D_MODEL,), jnp.float32), 'beta': jnp.zeros((D_MODEL,), jnp.float32), 'W_in': s(ks[1], (D_MODEL, 2 * D_INNER), 0.05), 'conv_w': s(ks[2], (D_INNER, D_CONV), 0.3), 'conv_b': jnp.zeros((D_INNER,), jnp.float32), 'W_xproj': s(ks[3], (D_INNER, DT_RANK + 2 * D_STATE), 0.05), 'W_dt': s(ks[4], (DT_RANK, D_INNER), 0.1), 'b_dt': jnp.full((D_INNER,), dt_bias, jnp.float32), 'A_log': jnp.log(jnp.tile(jnp.arange(1, D_STATE + 1, dtype=jnp.float32), (D_INNER, 1))), 'D': jnp.ones((D_INNER,), jnp.float32), 'W_out': s(ks[5], (D_INNER, D_MODEL), 0.05)}
    _L0_conv_all = _L0_conv_setup()
    _L0_conv_in = {k: v for k, v in _L0_conv_all.items() if k in ('gamma', 'beta', 'W_in', 'conv_w', 'conv_b', 'W_xproj', 'W_dt', 'b_dt', 'A_log', 'D', 'W_out')}
    del _L0_conv_all

    def _L1_conv_setup():
        import jax, jax.numpy as jnp
        import numpy as np
        DIM = 96
        HEADS = 6
        HD = DIM // HEADS
        WIN = 7
        K = WIN * WIN
        B, H, W = (4, 56, 56)
        EPS = 1e-05
        PAD = WIN // 2

        def _conv1x1(x, w, b):
            return jnp.einsum('bchw,oc->bohw', x, w) + b[None, :, None, None]
        key = jax.random.key(seed)
        ks = jax.random.split(key, 8)

        def n(k, shape, scale=0.02):
            return jax.random.normal(k, shape, dtype=jnp.float32) * scale
        return {'x': jax.random.normal(ks[0], (B, DIM, H, W), dtype=jnp.float32), 'bn_gamma': jnp.ones((DIM,), jnp.float32), 'bn_beta': jnp.zeros((DIM,), jnp.float32), 'qkv_w': n(ks[1], (3 * DIM, DIM)), 'qkv_b': jnp.zeros((3 * DIM,), jnp.float32), 'dm_w': n(ks[2], (K, 2 * HD, WIN, WIN)), 'dm_b': jnp.zeros((K,), jnp.float32), 'rel_bias': n(ks[3], (K, HEADS)), 'proj_w': n(ks[4], (DIM, DIM)), 'proj_b': jnp.zeros((DIM,), jnp.float32), 'c1_w': n(ks[5], (4 * DIM, DIM)), 'c1_b': jnp.zeros((4 * DIM,), jnp.float32), 'c2_w': n(ks[6], (DIM, 4 * DIM)), 'c2_b': jnp.zeros((DIM,), jnp.float32)}
    _L1_conv_all = _L1_conv_setup()
    _L1_conv_in = {k: v for k, v in _L1_conv_all.items() if k in ('bn_gamma', 'bn_beta', 'qkv_w', 'qkv_b', 'dm_w', 'dm_b', 'rel_bias', 'proj_w', 'proj_b', 'c1_w', 'c1_b', 'c2_w', 'c2_b')}
    del _L1_conv_all
    return {'x': x, 'L0_conv_gamma': _L0_conv_in['gamma'], 'L0_conv_beta': _L0_conv_in['beta'], 'L0_conv_W_in': _L0_conv_in['W_in'], 'L0_conv_conv_w': _L0_conv_in['conv_w'], 'L0_conv_conv_b': _L0_conv_in['conv_b'], 'L0_conv_W_xproj': _L0_conv_in['W_xproj'], 'L0_conv_W_dt': _L0_conv_in['W_dt'], 'L0_conv_b_dt': _L0_conv_in['b_dt'], 'L0_conv_A_log': _L0_conv_in['A_log'], 'L0_conv_D': _L0_conv_in['D'], 'L0_conv_W_out': _L0_conv_in['W_out'], 'L1_conv_bn_gamma': _L1_conv_in['bn_gamma'], 'L1_conv_bn_beta': _L1_conv_in['bn_beta'], 'L1_conv_qkv_w': _L1_conv_in['qkv_w'], 'L1_conv_qkv_b': _L1_conv_in['qkv_b'], 'L1_conv_dm_w': _L1_conv_in['dm_w'], 'L1_conv_dm_b': _L1_conv_in['dm_b'], 'L1_conv_rel_bias': _L1_conv_in['rel_bias'], 'L1_conv_proj_w': _L1_conv_in['proj_w'], 'L1_conv_proj_b': _L1_conv_in['proj_b'], 'L1_conv_c1_w': _L1_conv_in['c1_w'], 'L1_conv_c1_b': _L1_conv_in['c1_b'], 'L1_conv_c2_w': _L1_conv_in['c2_w'], 'L1_conv_c2_b': _L1_conv_in['c2_b']}

def reference(x, L0_conv_gamma, L0_conv_beta, L0_conv_W_in, L0_conv_conv_w, L0_conv_conv_b, L0_conv_W_xproj, L0_conv_W_dt, L0_conv_b_dt, L0_conv_A_log, L0_conv_D, L0_conv_W_out, L1_conv_bn_gamma, L1_conv_bn_beta, L1_conv_qkv_w, L1_conv_qkv_b, L1_conv_dm_w, L1_conv_dm_b, L1_conv_rel_bias, L1_conv_proj_w, L1_conv_proj_b, L1_conv_c1_w, L1_conv_c1_b, L1_conv_c2_w, L1_conv_c2_b):
    import jax
    import jax.numpy as jnp

    def _L0_conv_ref(x, gamma, beta, W_in, conv_w, conv_b, W_xproj, W_dt, b_dt, A_log, D, W_out):
        import jax, jax.numpy as jnp
        import numpy as np
        D_MODEL = 96
        D_STATE = 16
        D_CONV = 4
        EXPAND = 2
        D_INNER = EXPAND * D_MODEL
        DT_RANK = (D_MODEL + 15) // 16
        B_SZ, H_IMG, W_IMG = (4, 32, 32)
        LN_EPS = 1e-05

        def _mamba(x, W_in, conv_w, conv_b, W_xproj, W_dt, b_dt, A_log, D, W_out):
            Bb, L, _ = x.shape
            xz = x @ W_in
            xr, z = jnp.split(xz, 2, axis=-1)
            xc = jnp.transpose(xr, (0, 2, 1))
            xc = jax.lax.conv_general_dilated(xc, conv_w[:, None, :], (1,), [(D_CONV - 1, 0)], dimension_numbers=('NCH', 'OIH', 'NCH'), feature_group_count=D_INNER)
            xr = jax.nn.silu(jnp.transpose(xc + conv_b[None, :, None], (0, 2, 1)))
            dbl = xr @ W_xproj
            dt = jax.nn.softplus(dbl[..., :DT_RANK] @ W_dt + b_dt)
            Bm = dbl[..., DT_RANK:DT_RANK + D_STATE]
            Cm = dbl[..., DT_RANK + D_STATE:]
            A = -jnp.exp(A_log)

            def step(h, inp):
                dt_t, B_t, C_t, x_t = inp
                h = jnp.exp(dt_t[:, :, None] * A) * h + (dt_t * x_t)[:, :, None] * B_t[:, None, :]
                y_t = jnp.einsum('ben,bn->be', h, C_t)
                return (h, y_t)
            h0 = jnp.zeros((Bb, D_INNER, D_STATE), x.dtype)
            xs = (dt.transpose(1, 0, 2), Bm.transpose(1, 0, 2), Cm.transpose(1, 0, 2), xr.transpose(1, 0, 2))
            _, ys = jax.lax.scan(step, h0, xs)
            y = ys.transpose(1, 0, 2) + xr * D
            y = y * jax.nn.silu(z)
            return y @ W_out
        Bb, C, Hh, Ww = x.shape
        x_flat = x.reshape(Bb, C, Hh * Ww).transpose(0, 2, 1)
        mu = x_flat.mean(-1, keepdims=True)
        var = ((x_flat - mu) ** 2).mean(-1, keepdims=True)
        x_norm = (x_flat - mu) * jax.lax.rsqrt(var + LN_EPS) * gamma + beta
        x_in = jnp.concatenate([x_norm, x_norm[:, ::-1]], axis=0)
        out2 = _mamba(x_in, W_in, conv_w, conv_b, W_xproj, W_dt, b_dt, A_log, D, W_out)
        out_fwd, out_rev = (out2[:Bb], out2[Bb:, ::-1])
        out = (out_fwd + out_rev) * 0.5 + x_flat
        return out.transpose(0, 2, 1).reshape(Bb, C, Hh, Ww)

    def _L1_conv_ref(x, bn_gamma, bn_beta, qkv_w, qkv_b, dm_w, dm_b, rel_bias, proj_w, proj_b, c1_w, c1_b, c2_w, c2_b):
        import jax, jax.numpy as jnp
        import numpy as np
        DIM = 96
        HEADS = 6
        HD = DIM // HEADS
        WIN = 7
        K = WIN * WIN
        B, H, W = (4, 56, 56)
        EPS = 1e-05
        PAD = WIN // 2

        def _conv1x1(x, w, b):
            return jnp.einsum('bchw,oc->bohw', x, w) + b[None, :, None, None]
        Bx, C, Hx, Wx = x.shape
        shortcut = x
        mean = jnp.mean(x, axis=(0, 2, 3), keepdims=True)
        var = jnp.var(x, axis=(0, 2, 3), keepdims=True)
        xn = (x - mean) * jax.lax.rsqrt(var + EPS)
        xn = xn * bn_gamma[None, :, None, None] + bn_beta[None, :, None, None]
        qkv = _conv1x1(xn, qkv_w, qkv_b).reshape(Bx, 3, HEADS, HD, Hx, Wx)
        q, k, v = (qkv[:, 0], qkv[:, 1], qkv[:, 2])
        scale = HD ** (-0.5)
        qk = jnp.concatenate([(q * scale).reshape(Bx * HEADS, HD, Hx, Wx), k.reshape(Bx * HEADS, HD, Hx, Wx)], axis=1)
        attn = jax.lax.conv_general_dilated(qk, dm_w, (1, 1), [(PAD, PAD), (PAD, PAD)], dimension_numbers=('NCHW', 'OIHW', 'NCHW')) + dm_b[None, :, None, None]
        attn = attn.reshape(Bx, HEADS, K, Hx, Wx)
        attn = attn + rel_bias.T[None, :, :, None, None]
        attn = jax.nn.softmax(attn, axis=2)
        patches = jax.lax.conv_general_dilated_patches(v.reshape(Bx * HEADS, HD, Hx, Wx), (WIN, WIN), (1, 1), [(PAD, PAD), (PAD, PAD)], dimension_numbers=('NCHW', 'OIHW', 'NCHW'))
        patches = patches.reshape(Bx, HEADS, HD, K, Hx, Wx)
        out = jnp.einsum('bnckhw,bnkhw->bnchw', patches, attn).reshape(Bx, C, Hx, Wx)
        out = _conv1x1(out, proj_w, proj_b)
        x1 = shortcut + out
        h = _conv1x1(x1, c1_w, c1_b)
        h = jax.nn.gelu(h, approximate=False)
        h = _conv1x1(h, c2_w, c2_b)
        return x1 + h

    def _gn(v, G=32, eps=1e-05):
        B_, C_, H_, W_ = v.shape
        g = v.reshape(B_, G, C_ // G, H_, W_)
        m = jnp.mean(g, axis=(2, 3, 4), keepdims=True)
        s = jnp.var(g, axis=(2, 3, 4), keepdims=True)
        return ((g - m) / jnp.sqrt(s + eps)).reshape(v.shape)

    def _ln_c(v, eps=1e-06):
        m = jnp.mean(v, axis=1, keepdims=True)
        s = jnp.var(v, axis=1, keepdims=True)
        return (v - m) / jnp.sqrt(s + eps)

    def _ln_t(v, eps=1e-05):
        m = jnp.mean(v, axis=-1, keepdims=True)
        s = jnp.var(v, axis=-1, keepdims=True)
        return (v - m) / jnp.sqrt(s + eps)

    def _to_tokens(v):
        B_, C_, H_, W_ = v.shape
        return v.reshape(B_, C_, H_ * W_).transpose(0, 2, 1)

    def _from_tokens(t, like):
        B_, C_, H_, W_ = like.shape
        return t.transpose(0, 2, 1).reshape(B_, C_, H_, W_)
    x = _L0_conv_ref(x, L0_conv_gamma, L0_conv_beta, L0_conv_W_in, L0_conv_conv_w, L0_conv_conv_b, L0_conv_W_xproj, L0_conv_W_dt, L0_conv_b_dt, L0_conv_A_log, L0_conv_D, L0_conv_W_out)
    x = _L1_conv_ref(x, L1_conv_bn_gamma, L1_conv_bn_beta, L1_conv_qkv_w, L1_conv_qkv_b, L1_conv_dm_w, L1_conv_dm_b, L1_conv_rel_bias, L1_conv_proj_w, L1_conv_proj_b, L1_conv_c1_w, L1_conv_c1_b, L1_conv_c2_w, L1_conv_c2_b)
    return x

_drawn_inputs = setup_inputs


def setup_inputs(seed=0):
    import zlib

    import numpy as np

    out = dict(_drawn_inputs(seed))
    spreads = {'L0_conv_gamma': (1.0, 0.6),
     'L0_conv_beta': (0.0, 0.8),
     'L0_conv_conv_b': (0.0, 0.8),
     'L0_conv_b_dt': (-4.600165843963623, 0.6),
     'L0_conv_D': (1.0, 0.6),
     'L1_conv_bn_gamma': (1.0, 0.6),
     'L1_conv_bn_beta': (0.0, 0.8),
     'L1_conv_qkv_b': (0.0, 0.412),
     'L1_conv_dm_b': (0.0, 0.8),
     'L1_conv_proj_b': (0.0, 0.401),
     'L1_conv_c1_b': (0.0, 1.308),
     'L1_conv_c2_b': (0.0, 0.316)}
    factors = {'L0_conv_W_xproj': 8.0,
     'L0_conv_W_dt': 8.0,
     'L0_conv_A_log': 8.0,
     'L1_conv_qkv_w': 8.0,
     'L1_conv_dm_w': 8.0,
     'L1_conv_rel_bias': 41.604,
     'L1_conv_proj_w': 3.295}
    for name, (base, spread) in spreads.items():
        noise = np.random.default_rng([zlib.crc32(name.encode()), seed]).standard_normal(out[name].shape)
        drawn = base * np.exp(spread * noise) if base else spread * noise
        out[name] = jnp.asarray(drawn.astype(out[name].dtype))
    for name, factor in factors.items():
        out[name] = (out[name] * factor).astype(out[name].dtype)
    return out
```

```python
from contextlib import ExitStack

import concourse.bass as bass
from concourse import mybir
import numpy as np

F32 = mybir.dt.float32
BF16 = mybir.dt.bfloat16
ALU = mybir.AluOpType
ACT = mybir.ActivationFunctionType
AX = mybir.AxisListType

B, C, H, W = 4, 96, 32, 32
L = H * W
HALF = L // 2
E_IN, N_ST, RANK, TAPS = 192, 16, 6, 4
PAD = TAPS - 1
E_LO, E_HI = 128, E_IN - 128
GE = 128 // N_ST
UNITS = E_IN // GE
QUADS = UNITS // 4
PHASES = 2 * B
SPAN = L + HALF
PARTS = 3
LN_EPS = 1e-5
SOFTPLUS_LINEAR = 40.0

ORDER = [4 * c + m for m in range(4) for c in range(4)] + [16, 20, 17, 21, 18, 22, 19, 23]

A_RING, H_RING, HC_RING, U_BANKS, D_BANKS = 3, 3, 6, 3, 2
SUM_LAG = 3
LOADS = 16 + 9 + B - 1
SETUP = 8

HEADS, HD, WIN = 6, 16, 7
K2 = WIN * WIN
R = WIN // 2
HP = H + 2 * R
V_ROW = HD * HP
IMAGES = B * HEADS
PAIRS = IMAGES // 2
TILES = IMAGES // 4
X4_ROWS = H + 4
X4_RING = 6
G_BANKS = 4
BN_EPS = 1e-5
BN_VAR, BN_DONE, BN_BIAS = 2 * B + 1, 2 * B + 7, 2 * B + 9
ZEROED = 2
L1_LOADS = 13 + 4 + 2
DVE_ROWS, POOL_ROWS = (0, 1, 2, 3, 4), (5, 6)
PV_STEPS, PP_STEPS = 5 * len(DVE_ROWS) + 1, 5 * len(POOL_ROWS)
MLP_AFTER, MLP_LAST = {7: (0,), 9: (1,)}, (2, 3)
DVE_MLP = {2: (0,), 3: (1,), 5: (2, 3)}
O_AFTER = {1: 0, 2: 1, 4: 2, 5: 3}


def halves(direction):
    return (0, 1) if direction == 0 else (1, 0)


def scan_order(ap, direction):
    return ap if direction == 0 else ap[:, ::-1]


def cols(th, n=HALF):
    return slice(th * n, (th + 1) * n)


def y_steps_before(phase):
    return 3 * (phase // 2)


def mamba(nc, t, x1):
    with ExitStack() as ctx:
        def sb(name, shape, dt=F32):
            return ctx.enter_context(nc.sbuf_tensor(name, shape, dt))

        def ps(name, shape):
            return ctx.enter_context(nc.psum_tensor(name, shape, F32))

        def sem(name):
            return ctx.enter_context(nc.semaphore(name))

        w_in = sb("w_in", [C, 2 * E_IN])
        w_taps = sb("w_taps", [C, TAPS, E_IN])
        w_x = sb("w_x", [128, 2, RANK + 2 * N_ST])
        w_bc = sb("w_bc", [128, 2, 2, N_ST, GE])
        w_dt = sb("w_dt", [RANK, E_IN])
        w_out = sb("w_out", [128, 2, C])
        a_neg = sb("a_neg", [128, UNITS])
        conv_b, b_dt, d_skip = (sb(n, [128, 2]) for n in ("conv_b", "b_dt", "d_skip"))
        norm = sb("norm", [C, 3])
        center = sb("center", [C, 2, C])
        rep = sb("rep", [PARTS * 32, 4, 128], BF16)
        pick = sb("pick", [128, 4, 32])
        xn = sb("xn", [C, PAD + L + PAD])
        t01 = sb("t01", [128, 2 * SPAN])
        t0, t1 = t01[:, 0:SPAN], t01[:, SPAN:2 * SPAN]
        u_parts = t01[:, 0:PARTS * SPAN // 2].bitcast(BF16).rearrange("p (a s) -> p a s", a=PARTS)
        t2, t3, t4 = (sb(f"t{i}", [128, SPAN]) for i in (2, 3, 4))
        conv_w_rows = t2[0:C, 0:TAPS * E_IN].rearrange("p (j e) -> p j e", j=TAPS)
        rep_f = t3[0:PARTS * 32, 0:4 * 128].rearrange("p (q m) -> p q m", q=4)
        xr = sb("xr", [128, 2, SPAN])
        z = sb("z", [128, SPAN])
        y = sb("y", [128, SPAN])
        dt_parts = sb("dt_parts", [128, PARTS, SPAN], BF16)
        dt_st = sb("dt_st", [PARTS * 32, 2, 6, L], BF16)
        u_st = sb("u_st", [PARTS * 32, 2, 6, L], BF16)
        b_rep = sb("b_rep", [128, 2, L])
        c_rep = sb("c_rep", [128, 2, L])
        a = sb("a", [128, A_RING, L])
        h = sb("h", [128, H_RING, L])
        hc = sb("hc", [128, HC_RING, L])
        dt_ps = ps("dt_ps", [128, D_BANKS, HALF])
        u_ps = ps("u_ps", [128, U_BANKS, HALF])
        y_ps = ps("y_ps", [128, 2, HALF])
        f_ps = ps("f_ps", [128, HALF])

        loaded = sem("loaded")
        set_up = sem("set_up")
        a_exp = sem("a_exp")
        job_done = sem("job_done")
        job_read = sem("job_read")
        act_step = sem("act_step")
        pool_step = sem("pool_step")
        dve_step = sem("dve_step")
        dt_stacked = sem("dt_stacked")
        u_stacked = sem("u_stacked")
        dt_spread = sem("dt_spread")
        u_spread = sem("u_spread")
        exp_done = sem("exp_done")
        bu_done = sem("bu_done")
        scanned = sem("scanned")
        hc_done = sem("hc_done")
        summed = sem("summed")
        y_read = sem("y_read")
        y_step = sem("y_step")

        block = ctx.enter_context(nc.Block())

        def ran(phase, k):
            return UNITS * phase + k

        def count(phase, name, seq_of):
            return sum(len(seq_of(p)) for p in range(phase)) + seq_of(phase).index(name) + 1

        def jobs(p):
            head = ["cen0", "cen1", "var0", "var1", "conv0", "conv1", "conv2"]
            if p % 2:
                head = ["conv0", "conv1", "conv2", "z0", "z1", "z2"] + (["out0", "out1"] if p > 1 else [])
            return head + ["dtr", "dt0", "dt1", "dt2", "B0", "B1", "C0", "C1"]

        def act_steps(p):
            return (["zs"] if p % 2 else ["sq0", "sq1", "rs", "xn"]) + ["xr", "e", "ln", "dh", "dm", "uh", "um"]

        def pool_steps(p):
            return ([] if p % 2 else ["xs"]) + ["xm", "y1", "u"]

        def dve_steps(p):
            return ["c", "l", "dt", "dr", "dl", "ur", "ul"]

        def J(p, name):
            return count(p, name, jobs)

        def A(p, name):
            return count(p, name, act_steps)

        def P(p, name):
            return count(p, name, pool_steps)

        def V(p, name):
            return count(p, name, dve_steps)

        ALL_JOBS = J(PHASES - 1, "C1")
        STACK = 16 * PARTS * 8

        @block.sync
        def _(sp):
            loads = [
                (x1[:, 0, :], t["x"][0]), (norm[:, 0:1], t["gamma"]), (norm[:, 1:2], t["beta"]),
                (center[:, :, :], t["center"]), (w_in[:, :], t["W_in"]),
                (conv_w_rows.rearrange("p j e -> p (j e)"), t["conv_w"].to_broadcast([C, TAPS * E_IN])),
                (w_x[:, 0, :], t["W_xproj"][0:E_LO]), (w_x[0:E_HI, 1, :], t["W_xproj"][E_LO:E_IN]),
                (w_x[E_HI:128, 1, :], t["W_xproj"][E_LO:E_IN]),
                (w_dt[:, :], t["W_dt"]), (rep_f, t["rep"]), (pick[:, :, :], t["pick"]),
                (a_neg[:, :], t["A_log"]),
                (w_out[:, 0, :], t["W_out"][0:E_LO]), (w_out[0:E_HI, 1, :], t["W_out"][E_LO:E_IN]),
                (w_out[E_HI:128, 1, :], t["W_out"][E_LO:E_IN]),
            ]
            for column, name in ((conv_b, "conv_b"), (b_dt, "b_dt"), (d_skip, "D")):
                loads += [(column[:, 0:1], t[name][0:E_LO]), (column[0:E_HI, 1:2], t[name][E_LO:E_IN]),
                          (column[E_HI:128, 1:2], t[name][E_LO:E_IN])]
            loads += [(x1[:, b, :], t["x"][b]) for b in range(1, B)]
            assert len(loads) == LOADS
            for dst, src in loads:
                sp.dma_start(dst, src).then_inc(loaded, 16)

            def stack(dst, parts, part, th_done):
                for s in range(4):
                    sp.dma_start(dst[32 * part:32 * part + 32, s, :],
                                 parts[32 * s:32 * s + 32, part, 0:L]).then_inc(th_done, 16)
                for s in range(2):
                    for th in range(2):
                        p = E_HI * th + 32 * s
                        sp.dma_start(dst[32 * part:32 * part + 32, 4 + s, cols(th)],
                                     parts[p:p + 32, part, L:SPAN]).then_inc(th_done, 16)

            for ph in range(PHASES):
                d = ph % 2
                if ph >= 2:
                    sp.wait_ge(u_spread, 2 * ran(ph - 1, 0))
                for dst, parts, done, steps in (
                    (dt_st[:, d], dt_parts, dt_stacked, ((act_step, A(ph, "dh")), (act_step, A(ph, "dm")),
                                                         (dve_step, V(ph, "dl")))),
                    (u_st[:, d], u_parts, u_stacked, ((act_step, A(ph, "uh")), (act_step, A(ph, "um")),
                                                      (dve_step, V(ph, "ul")))),
                ):
                    for part, (made, at) in enumerate(steps):
                        sp.wait_ge(made, at)
                        stack(dst, parts, part, done)

        @block.tensor
        def _(pe):
            def free(job):
                if job > 1:
                    pe.wait_ge(job_read, job - 1)

            def out_job(b, th):
                pe.wait_ge(y_step, 3 * b + 3)
                p = E_HI * th
                pe.matmul(f_ps[0:C, :], w_out[:, 0, :], y[:, cols(th)], start=True, stop=False)
                pe.matmul(f_ps[0:C, :], w_out[p:p + E_HI, 1, :], y[p:p + E_HI, L:SPAN], start=False,
                          stop=True).then_inc(job_done, 1)

            def front(ph, slot):
                d, b = ph % 2, ph // 2
                if d == 0 and slot in (0, 1):
                    free(J(ph, f"cen{slot}"))
                    pe.matmul(f_ps[0:C, :], center[:, 0, :], x1[:, b, cols(slot)], start=True,
                              stop=True).then_inc(job_done, 1)
                if d == 0 and slot in (2, 3):
                    free(J(ph, f"var{slot - 2}"))
                    pe.wait_ge(act_step, A(ph, f"sq{slot - 2}"))
                    pe.matmul(f_ps[0:C, :], center[:, 1, :], t1[0:C, cols(slot - 2)], start=True,
                              stop=True).then_inc(job_done, 1)
                c0 = 0 if d else 5
                shifts = [2 * PAD - j if d else j for j in range(TAPS)]
                if slot in (c0, c0 + 1):
                    th = slot - c0
                    free(J(ph, f"conv{th}"))
                    pe.wait_ge(set_up, SETUP)
                    pe.wait_ge(act_step, A(2 * b, "xn"))
                    for j, s in enumerate(shifts):
                        mm = pe.matmul(f_ps[:, :], w_taps[:, j, 0:E_LO], xn[:, s + th * HALF:s + (th + 1) * HALF],
                                       start=(j == 0), stop=(j == TAPS - 1))
                    mm.then_inc(job_done, 1)
                if slot == c0 + 2:
                    free(J(ph, "conv2"))
                    for j, s in enumerate(shifts):
                        for th in range(2):
                            mm = pe.matmul(f_ps[E_HI * th:E_HI * (th + 1), :], w_taps[:, j, E_LO:E_IN],
                                           xn[:, s + th * HALF:s + (th + 1) * HALF],
                                           start=(j == 0), stop=(j == TAPS - 1))
                    mm.then_inc(job_done, 1)
                if d == 1 and slot in (3, 4):
                    th = slot - 3
                    free(J(ph, f"z{th}"))
                    pe.matmul(f_ps[:, :], w_in[:, E_IN:E_IN + E_LO], xn[:, PAD + th * HALF:PAD + (th + 1) * HALF],
                              start=True, stop=True).then_inc(job_done, 1)
                if d == 1 and slot == 5:
                    free(J(ph, "z2"))
                    for th in range(2):
                        mm = pe.matmul(f_ps[E_HI * th:E_HI * (th + 1), :], w_in[:, E_IN + E_LO:2 * E_IN],
                                       xn[:, PAD + th * HALF:PAD + (th + 1) * HALF], start=True, stop=True)
                    mm.then_inc(job_done, 1)
                if d == 1 and b > 0 and slot in (7, 8):
                    free(J(ph, f"out{slot - 7}"))
                    out_job(b - 1, slot - 7)
                if slot == 9:
                    free(J(ph, "dtr"))
                    pe.wait_ge(act_step, A(ph, "xr"))
                    for th in range(2):
                        p = E_HI * th
                        pe.matmul(f_ps[32 * th:32 * th + RANK, :], w_x[:, 0, 0:RANK], xr[:, d, cols(th)],
                                  start=True, stop=False)
                        mm = pe.matmul(f_ps[32 * th:32 * th + RANK, :], w_x[p:p + E_HI, 1, 0:RANK],
                                       xr[p:p + E_HI, d, L:SPAN], start=False, stop=True)
                    mm.then_inc(job_done, 1)
                if slot in (10, 11):
                    th = slot - 10
                    free(J(ph, f"dt{th}"))
                    pe.matmul(f_ps[:, :], w_dt[:, 0:E_LO], t0[0:RANK, cols(th)], start=True,
                              stop=True).then_inc(job_done, 1)
                if slot == 12:
                    free(J(ph, "dt2"))
                    for th in range(2):
                        mm = pe.matmul(f_ps[E_HI * th:E_HI * (th + 1), :], w_dt[:, E_LO:E_IN],
                                       t0[0:RANK, cols(th)], start=True, stop=True)
                    mm.then_inc(job_done, 1)
                if slot in (13, 14, 15, 16):
                    which, th = (slot - 13) // 2, (slot - 13) % 2
                    p = E_HI * th
                    free(J(ph, f"{'BC'[which]}{th}"))
                    pe.matmul(f_ps[:, :], w_bc[:, 0, which].rearrange("p n e -> p (n e)"), xr[:, d, cols(th)],
                              start=True, stop=False)
                    pe.matmul(f_ps[:, :], w_bc[p:p + E_HI, 1, which].rearrange("p n e -> p (n e)"),
                              xr[p:p + E_HI, d, L:SPAN], start=False, stop=True).then_inc(job_done, 1)

            def spread(ph, k):
                d, g = ph % 2, ORDER[k]
                if k == 0:
                    pe.wait_ge(dt_stacked, STACK * (ph + 1))
                    pe.wait_ge(u_stacked, STACK * (ph + 1))
                for i, th in enumerate(halves(d)):
                    n = 2 * ran(ph, k) + i
                    if n >= D_BANKS:
                        pe.wait_ge(exp_done, n - D_BANKS + 1)
                    pe.matmul(dt_ps[:, n % D_BANKS, :], rep[:, g % 4, :], dt_st[:, d, g // 4, cols(th)],
                              start=True, stop=True).then_inc(dt_spread, 1)
                    if n >= U_BANKS:
                        pe.wait_ge(scanned, n - U_BANKS + 1)
                    pe.matmul(u_ps[:, n % U_BANKS, :], rep[:, g % 4, :], u_st[:, d, g // 4, cols(th)],
                              start=True, stop=True).then_inc(u_spread, 1)

            def sum_states(q):
                ph, m = q // QUADS, q % QUADS
                pe.wait_ge(hc_done, 4 * q + 4)
                y_tile = 2 * ph + (m >= 4)
                if m in (0, 4) and y_tile:
                    pe.wait_ge(y_read, y_tile)
                for th in range(2):
                    for k in range(4 * m, 4 * m + 4):
                        g = ORDER[k]
                        if m < 4:
                            out, first, last = y_ps[32 * (g // 4):32 * (g // 4) + 32, th, :], m == 0, m == 3
                        else:
                            p = 32 * ((g - 16) // 4) + E_HI * th
                            out, first, last = y_ps[p:p + 32, 0, :], g in (16, 20), g in (19, 23)
                        mm = pe.matmul(out, pick[:, g % 4, :], hc[:, ran(ph, k) % HC_RING, cols(th)],
                                       start=first, stop=last)
                mm.then_inc(summed, 1)

            pe.wait_ge(loaded, 16 * LOADS)
            for slot in range(UNITS):
                front(0, slot)
            for ph in range(PHASES):
                for k in range(UNITS):
                    spread(ph, k)
                    if ran(ph, k) % 4 == (3 + SUM_LAG) % 4 and ran(ph, k) >= 3 + SUM_LAG:
                        sum_states((ran(ph, k) - 3 - SUM_LAG) // 4)
                    if ph + 1 < PHASES:
                        front(ph + 1, k)
            sum_states(QUADS * PHASES - 1)
            for th in range(2):
                free(ALL_JOBS + th + 1)
                out_job(B - 1, th)

        @block.scalar
        def _(act):
            def own(ph, name):
                act.wait_ge(act_step, A(ph, name))

            def leave(ph, job, out, src, func=ACT.Identity, **kw):
                act.wait_ge(job_done, J(ph, job))
                nc.scalar.activation(out, src, func, **kw).then_inc(job_read, 1)

            def front(ph, slot):
                d, b = ph % 2, ph // 2
                if slot == 0 and ph > 0:
                    act.wait_ge(u_stacked, STACK * ph)
                    act.wait_ge(dve_step, V(ph - 1, "ul"))
                if d == 0 and slot in (0, 1):
                    th = slot
                    leave(ph, f"cen{th}", t0[0:C, cols(th)], f_ps[0:C, :])
                    act.wait_ge(job_read, J(ph, f"cen{th}"))
                    nc.scalar.activation(t1[0:C, cols(th)], t0[0:C, cols(th)], ACT.Square).then_inc(act_step, 1)
                if d == 0 and slot in (2, 3):
                    th = slot - 2
                    leave(ph, f"var{th}", t2[0:C, cols(th)], f_ps[0:C, :], ACT.Ln, bias=norm[:, 2:3])
                if d == 0 and slot == 3:
                    act.wait_ge(job_read, J(ph, "var1"))
                    nc.scalar.activation(t2[0:C, 0:L], t2[0:C, 0:L], ACT.Exp, scale=-0.5).then_inc(act_step, 1)
                if d == 0 and slot == 4:
                    act.wait_ge(pool_step, P(ph, "xs"))
                    nc.scalar.activation(xn[:, PAD:PAD + L], t1[0:C, 0:L], ACT.Identity, scale=norm[:, 0:1],
                                         bias=norm[:, 1:2]).then_inc(act_step, 1)
                c0 = 0 if d else 5
                if slot in (c0, c0 + 1):
                    th = slot - c0
                    leave(ph, f"conv{th}", t3[:, cols(th)], f_ps[:, :], bias=conv_b[:, 0:1])
                if slot == c0 + 2:
                    leave(ph, "conv2", t3[:, L:SPAN], f_ps[:, :], bias=conv_b[:, 1:2])
                if d == 1 and slot in (3, 4):
                    leave(ph, f"z{slot - 3}", t4[:, cols(slot - 3)], f_ps[:, :])
                if d == 1 and slot == 5:
                    leave(ph, "z2", t4[:, L:SPAN], f_ps[:, :])
                if slot == 8:
                    if ph >= 2:
                        act.wait_ge(y_read, 2 * ph - 2)
                        act.wait_ge(y_step, y_steps_before(ph - 1))
                    if d == 1:
                        act.wait_ge(job_read, J(ph, "z2"))
                        nc.scalar.activation(z[:, :], t4[:, :], ACT.Silu).then_inc(act_step, 1)
                    act.wait_ge(job_read, J(ph, "conv2"))
                    nc.scalar.activation(xr[:, d, :], t3[:, :], ACT.Silu).then_inc(act_step, 1)
                if slot == 9:
                    act.wait_ge(job_done, J(ph, "dtr"))
                    nc.scalar.activation(t0[0:RANK, cols(0)], f_ps[0:RANK, :], ACT.Copy)
                    nc.scalar.activation(t0[0:RANK, cols(1)], f_ps[32:32 + RANK, :], ACT.Copy).then_inc(job_read, 1)
                if slot in (10, 11):
                    leave(ph, f"dt{slot - 10}", t2[:, cols(slot - 10)], f_ps[:, :], bias=b_dt[:, 0:1])
                if slot == 12:
                    leave(ph, "dt2", t2[:, L:SPAN], f_ps[:, :], bias=b_dt[:, 1:2])
                if slot in (13, 14):
                    if ph >= 2 and slot == 13:
                        act.wait_ge(bu_done, 2 * ran(ph - 1, 0))
                    leave(ph, f"B{slot - 13}", b_rep[:, d, cols(slot - 13)], f_ps[:, :])
                if slot == 14:
                    act.wait_ge(pool_step, P(ph, "xm"))
                    nc.scalar.activation(t4[:, :], t3[:, :], ACT.Exp).then_inc(act_step, 1)
                if slot in (15, 16):
                    if ph >= 2 and slot == 15:
                        act.wait_ge(hc_done, ran(ph - 1, 0))
                    leave(ph, f"C{slot - 15}", c_rep[:, d, cols(slot - 15)], f_ps[:, :])
                if slot == 15:
                    act.wait_ge(pool_step, P(ph, "y1"))
                    nc.scalar.activation(t1[:, :], t3[:, :], ACT.Ln).then_inc(act_step, 1)
                if slot == 17:
                    if ph > 0:
                        act.wait_ge(dt_stacked, STACK * ph)
                    act.wait_ge(dve_step, V(ph, "dt"))
                    nc.scalar.activation(dt_parts[:, 0, :], t2[:, :], ACT.Copy).then_inc(act_step, 1)
                if slot == 18:
                    act.wait_ge(dve_step, V(ph, "dr"))
                    nc.scalar.activation(dt_parts[:, 1, :], t1[:, :], ACT.Copy).then_inc(act_step, 1)
                if slot == 19:
                    act.wait_ge(pool_step, P(ph, "u"))
                    act.wait_ge(dve_step, V(ph, "dl"))
                    nc.scalar.activation(u_parts[:, 0, :], t3[:, :], ACT.Copy).then_inc(act_step, 1)
                if slot == 20:
                    act.wait_ge(dve_step, V(ph, "ur"))
                    nc.scalar.activation(u_parts[:, 1, :], t4[:, :], ACT.Copy).then_inc(act_step, 1)

            def decay(ph, k):
                g = ORDER[k]
                for i, th in enumerate(halves(ph % 2)):
                    n = 2 * ran(ph, k) + i
                    act.wait_ge(dt_spread, n + 1)
                    if i == 0 and ran(ph, k) >= A_RING:
                        act.wait_ge(scanned, 2 * (ran(ph, k) - A_RING + 1))
                    nc.scalar.activation(a[:, ran(ph, k) % A_RING, cols(th)], dt_ps[:, n % D_BANKS, :], ACT.Exp,
                                         scale=a_neg[:, g:g + 1]).then_inc(exp_done, 1)

            act.wait_ge(loaded, 16 * LOADS)
            nc.scalar.activation(a_neg[:, :], a_neg[:, :], ACT.Exp).then_inc(a_exp, 1)
            act.wait_ge(set_up, SETUP)
            for slot in range(UNITS):
                front(0, slot)
            for ph in range(PHASES):
                for k in range(UNITS):
                    decay(ph, k)
                    if ph + 1 < PHASES:
                        front(ph + 1, k)

        @block.gpsimd
        def _(pool):
            def front(ph, slot):
                d = ph % 2
                if d == 0 and slot == 3:
                    pool.wait_ge(act_step, A(ph, "rs"))
                    nc.gpsimd.tensor_tensor(t1[0:C, 0:L], t0[0:C, 0:L], t2[0:C, 0:L], ALU.mult).then_inc(pool_step, 1)
                if slot == 12:
                    pool.wait_ge(job_read, J(ph, "dt2"))
                    nc.gpsimd.tensor_scalar(t3[:, :], t2[:, :], SOFTPLUS_LINEAR, None, ALU.min).then_inc(pool_step, 1)
                if slot == 14:
                    pool.wait_ge(act_step, A(ph, "e"))
                    nc.gpsimd.tensor_scalar(t3[:, :], t4[:, :], 1.0, None, ALU.add).then_inc(pool_step, 1)
                if slot == 16:
                    pool.wait_ge(dve_step, V(ph, "dt"))
                    nc.gpsimd.tensor_tensor(t3[:, :], t2[:, :], xr[:, d, :], ALU.mult).then_inc(pool_step, 1)

            def read_out(ph, k):
                n = ran(ph, k)
                pool.wait_ge(scanned, 2 * n + 2)
                if n >= HC_RING:
                    pool.wait_ge(summed, (n - HC_RING) // 4 + 1)
                if k == 0:
                    pool.wait_ge(job_read, J(ph, "C1"))
                nc.gpsimd.tensor_tensor(hc[:, n % HC_RING, :], h[:, n % H_RING, :], c_rep[:, ph % 2, :],
                                        ALU.mult).then_inc(hc_done, 1)

            for slot in range(UNITS):
                front(0, slot)
            for ph in range(PHASES):
                for k in range(UNITS):
                    read_out(ph, k)
                    if ph + 1 < PHASES:
                        front(ph + 1, k)

        @block.vector
        def _(dve):
            def front(ph, slot):
                d, b = ph % 2, ph // 2
                if d == 1 and b > 0 and slot in (7, 8):
                    add_out(b - 1, slot - 7, J(ph, f"out{slot - 7}"))
                if slot == 15:
                    dve.wait_ge(pool_step, P(ph, "y1"))
                    nc.vector.scalar_tensor_tensor(out=t4[:, :], in0=t3[:, :], scalar=-1.0, in1=t4[:, :],
                                                   op0=ALU.add, op1=ALU.subtract).then_inc(dve_step, 1)
                    dve.wait_ge(dve_step, V(ph, "c"))
                    dve.wait_ge(act_step, A(ph, "ln"))
                    nc.vector.tensor_tensor(t1[:, :], t1[:, :], t4[:, :], ALU.subtract).then_inc(dve_step, 1)
                    dve.wait_ge(dve_step, V(ph, "l"))
                    nc.vector.tensor_tensor(t2[:, :], t2[:, :], t1[:, :], ALU.max).then_inc(dve_step, 1)
                if slot == 17:
                    dve.wait_ge(act_step, A(ph, "dh"))
                    nc.vector.tensor_tensor(t1[:, :], t2[:, :], dt_parts[:, 0, :], ALU.subtract).then_inc(dve_step, 1)
                if slot == 18:
                    dve.wait_ge(act_step, A(ph, "dm"))
                    nc.vector.tensor_tensor(dt_parts[:, 2, :], t1[:, :], dt_parts[:, 1, :],
                                            ALU.subtract).then_inc(dve_step, 1)
                if slot == 19:
                    dve.wait_ge(act_step, A(ph, "uh"))
                    nc.vector.tensor_tensor(t4[:, :], t3[:, :], u_parts[:, 0, :], ALU.subtract).then_inc(dve_step, 1)
                if slot == 20:
                    dve.wait_ge(act_step, A(ph, "um"))
                    nc.vector.tensor_tensor(u_parts[:, 2, :], t4[:, :], u_parts[:, 1, :],
                                            ALU.subtract).then_inc(dve_step, 1)

            def add_out(b, th, job):
                dve.wait_ge(job_done, job)
                nc.vector.scalar_tensor_tensor(out=x1[:, b, cols(th)], in0=f_ps[0:C, :], scalar=0.5,
                                               in1=x1[:, b, cols(th)], op0=ALU.mult, op1=ALU.add).then_inc(job_read, 1)

            def take_y(ph, tile):
                d, b = ph % 2, ph // 2
                s = slice(0, L) if tile == 0 else slice(L, SPAN)
                src = y_ps[:, :, :].rearrange("p a n -> p (a n)") if tile == 0 else y_ps[:, 0, :]
                dve.wait_ge(summed, QUADS * ph + (4 if tile == 0 else 6))
                if d == 0:
                    if b > 0 and tile == 0:
                        dve.wait_ge(job_done, J(2 * b + 1, "out1"))
                    nc.vector.scalar_tensor_tensor(out=y[:, s], in0=xr[:, d, s], scalar=d_skip[:, tile:tile + 1],
                                                   in1=src, op0=ALU.mult, op1=ALU.add).then_inc(y_read, 1)
                    return
                dve.wait_ge(y_read, 2 * ph - 1 + tile)
                nc.vector.tensor_tensor(y[:, s], y[:, s], src, ALU.add).then_inc(y_read, 1)
                dve.wait_ge(y_read, 2 * ph + 1 + tile)
                nc.vector.scalar_tensor_tensor(out=y[:, s], in0=xr[:, d, s], scalar=d_skip[:, tile:tile + 1],
                                               in1=y[:, s], op0=ALU.mult, op1=ALU.add).then_inc(y_step, 1)

            def gate(b):
                dve.wait_ge(y_step, 3 * b + 2)
                nc.vector.tensor_tensor(y[:, :], y[:, :], z[:, :], ALU.mult).then_inc(y_step, 1)

            def times_b(ph, k, i):
                n = 2 * ran(ph, k) + i
                th = halves(ph % 2)[i]
                if k == 0 and i == 0:
                    dve.wait_ge(job_read, J(ph, "B1"))
                dve.wait_ge(u_spread, n + 1)
                nc.vector.tensor_tensor(u_ps[:, n % U_BANKS, :], u_ps[:, n % U_BANKS, :],
                                        b_rep[:, ph % 2, cols(th)], ALU.mult).then_inc(bu_done, 1)

            def scan(ph, k, i):
                d, n = ph % 2, 2 * ran(ph, k) + i
                th = halves(d)[i]
                place = ran(ph, k) % H_RING
                before = HALF - 1 if d == 0 else HALF
                dve.wait_ge(exp_done, n + 1)
                dve.wait_ge(bu_done, n + 1)
                if i == 0 and ran(ph, k) >= H_RING:
                    dve.wait_ge(hc_done, ran(ph, k) - H_RING + 1)
                if i == 1:
                    dve.wait_ge(scanned, n)
                nc.vector.tensor_tensor_scan(
                    scan_order(h[:, place, cols(th)], d), scan_order(a[:, ran(ph, k) % A_RING, cols(th)], d),
                    scan_order(u_ps[:, n % U_BANKS, :], d), h[:, place, before:before + 1] if i else 0.0,
                    ALU.mult, ALU.add).then_inc(scanned, 1)

            nc.vector.memset(xn[:, 0:PAD], 0.0)
            nc.vector.memset(xn[:, PAD + L:], 0.0)
            nc.vector.memset(norm[:, 2:3], LN_EPS).then_inc(set_up, 1)
            dve.wait_ge(loaded, 16 * LOADS)
            nc.vector.tensor_tensor(w_taps[:, :, :], conv_w_rows,
                                    w_in[:, 0:E_IN].unsqueeze(1).broadcast_to([C, TAPS, E_IN]), ALU.mult)\
                .then_inc(set_up, 1)
            nc.vector.tensor_copy(rep[:, :, :], rep_f).then_inc(set_up, 1)
            for part in range(2):
                for which in range(2):
                    s = RANK + which * N_ST
                    nc.vector.tensor_copy(w_bc[:, part, which], w_x[:, part, s:s + N_ST].unsqueeze(2)
                                          .broadcast_to([128, N_ST, GE])).then_inc(set_up, 1)
            dve.wait_ge(a_exp, 1)
            nc.vector.tensor_scalar(a_neg[:, :], a_neg[:, :], -1.0, None, ALU.mult).then_inc(set_up, 1)

            for slot in range(UNITS):
                front(0, slot)
            for ph in range(PHASES):
                for k in range(UNITS):
                    if k == 0:
                        times_b(ph, k, 0)
                    times_b(ph, k, 1)
                    scan(ph, k, 0)
                    if k + 1 < UNITS:
                        times_b(ph, k + 1, 0)
                    scan(ph, k, 1)
                    if ph + 1 < PHASES:
                        front(ph + 1, k)
                    if k == 4 and ph > 0:
                        take_y(ph - 1, 1)
                        if ph % 2 == 0:
                            gate(ph // 2 - 1)
                    if k == 20:
                        take_y(ph, 0)
            take_y(PHASES - 1, 1)
            gate(B - 1)
            for th in range(2):
                add_out(B - 1, th, ALL_JOBS + th + 1)
            dve.wait_ge(job_read, ALL_JOBS + 2)


def attention(nc, t, x1, scratch):
    scores_d, v_d, o_d = scratch
    with ExitStack() as ctx:
        def sb(name, shape, dt=F32):
            return ctx.enter_context(nc.sbuf_tensor(name, shape, dt))

        def ps(name, shape):
            return ctx.enter_context(nc.psum_tensor(name, shape, F32))

        def sem(name):
            return ctx.enter_context(nc.semaphore(name))

        qkv_w = sb("qkv_w", [C, 3 * C])
        qkv_s = sb("qkv_s", [C, 3 * C])
        qkv_b = sb("qkv_b", [128, 3])
        qkv_bias = sb("qkv_bias", [128, 3])
        qkv_scale = sb("qkv_scale", [128, 3])
        bn = sb("bn", [C, 3])
        bn_stats = sb("bn_stats", [C, 2 * B, nc.vector.BN_STATS_DIM])
        bn_mv = sb("bn_mv", [C, nc.vector.BN_AGGR_DIM])
        bn_scale, bn_shift = sb("bn_scale", [C, 1]), sb("bn_shift", [C, 1])
        w_up = sb("w_up", [128, WIN, 64])
        w_low = sb("w_low", [96, WIN, 64])
        rel = sb("rel", [128, HEADS // 2])
        dm_b = sb("dm_b", [128, 1])
        proj_w, proj_b = sb("proj_w", [C, C]), sb("proj_b", [C, 1])
        c1_w, c1_b = sb("c1_w", [C, 4 * C]), sb("c1_b", [128, 3])
        c2_w, c2_b = sb("c2_w", [128, 3, C]), sb("c2_b", [C, 1])
        qk = sb("qk", [128, 2, 2, HP, HP])
        v = sb("v", [C, 2, H, HP])
        zeros = sb("zeros", [IMAGES, R * V_ROW])
        x4 = sb("x4", [128, X4_RING, X4_ROWS, HP])
        sc = sb("sc", [128, 2, L])
        at = sb("at", [128, 2, K2, W])
        mx = sb("mx", [128, W])
        den = sb("den", [128, 2, W])
        vw = sb("vw", [128, 2, WIN, HD, HP])
        prod_v = sb("prod_v", [128, WIN, HD, W])
        prod_p = sb("prod_p", [128, WIN, HD, W])
        acc_v = sb("acc_v", [128, HD, W])
        acc_p = sb("acc_p", [128, HD, W])
        o_t = sb("o_t", [128, HD, W])
        o = sb("o", [C, L])
        up = sb("up", [128, 3, L])
        sc_ps = ps("sc_ps", [128, 2, 2, HALF])
        g_ps = ps("g_ps", [128, G_BANKS, HALF])

        loaded = sem("l1_loaded")
        zeroed = sem("zeroed")
        bn_step = sem("bn_step")
        job_done = sem("g_done")
        left_act = sem("left_act")
        left_dve = sem("left_dve")
        x4_in = [sem(f"x4_in{i}") for i in range(X4_RING // 2)]
        scored = sem("scored")
        sc_out = sem("sc_out")
        sc_stored = [sem(f"sc_stored{i}") for i in range(2)]
        sides = sem("sides")
        v_stored = [sem(f"v_stored{b}") for b in range(B)]
        at_in = [sem(f"at_in{i}") for i in range(2)]
        vw_in = [sem(f"vw_in{i}") for i in range(2)]
        soft = sem("soft")
        less = sem("less")
        exped = sem("exped")
        pv = sem("pv")
        pp = sem("pp")
        normed = sem("normed")
        o_stored = sem("o_stored")
        o_in = sem("o_in")
        out_s = sem("out_stored")

        block = ctx.enter_context(nc.Block())

        def job_list():
            seq = [("bias", m) for m in range(3)]
            for b in range(B):
                if b == 0:
                    seq += [("qkv", 0, i) for i in range(6)]
                for p in range(3 * b, 3 * b + 3):
                    if p == 3 * b and b + 1 < B:
                        seq += [("qkv", b + 1, i) for i in range(6)]
                    for m in MLP_AFTER.get(p, ()):
                        seq += [("mlp", m, i) for i in range(10)]
            for m in MLP_LAST:
                seq += [("mlp", m, i) for i in range(10)]
            return {name: n + 1 for n, name in enumerate(seq)}

        JOB = job_list()

        def by_dve(name):
            return name[0] == "bias" or name[0] == "mlp" and name[2] not in range(2, 8)

        def left(eng, name):
            mine = [n for n in JOB if by_dve(n) == by_dve(name)]
            eng.wait_ge(left_dve if by_dve(name) else left_act, mine.index(name) + 1)

        @block.sync
        def _(sp):
            loads = [(qkv_w[:, :], t["qkv_w"]), (qkv_b[:, 0:1], t["qkv_b"][0:128]),
                     (qkv_b[0:64, 1:2], t["qkv_b"][128:192]), (qkv_b[0:C, 2:3], t["qkv_b"][192:288]),
                     (qkv_scale[:, :], t["qkv_scale"]), (bn[:, 0:1], t["bn_gamma"]), (bn[:, 1:2], t["bn_beta"]),
                     (proj_w[:, :], t["proj_w"]), (proj_b[:, :], t["proj_b"]), (c1_w[:, :], t["c1_w"]),
                     (c1_b[:, :], t["c1_b"]), (c2_w[:, :, :], t["c2_w"]), (c2_b[:, :], t["c2_b"])]
            for i in range(2):
                rows = slice(64 * i, 64 * i + K2)
                loads += [(rel[rows, :], t["rel_bias"][:, i::2]), (dm_b[rows, :], t["dm_b"])]
            sp.wait_ge(zeroed, ZEROED)
            loads += [(w_up[:, :, 0:K2], t["dm_w"][0:128]), (w_low[:, :, 0:K2], t["dm_w"][128:224])]
            assert len(loads) == L1_LOADS
            with nc.allow_non_contiguous_dma(reason="small weights"):
                for dst, src in loads:
                    sp.dma_start(dst, src).then_inc(loaded, 16)
            for side in (0, R + H):
                sp.dma_start(v_d[:, side:side + R].rearrange("i r c x -> i (r c x)"), zeros[:, :])\
                    .then_inc(sides, 16)

            def put_x4(p):
                b = p // 3
                if p % 3 == 0:
                    left(sp, ("qkv", b, 3))
                if p >= X4_RING // 2:
                    sp.wait_ge(scored, 2 * (p - X4_RING // 2) + 2)
                for i in range(2):
                    hd = 2 * (p % 3) + i
                    for j in range(4):
                        rows = X4_ROWS if j < 3 else H
                        sp.dma_start(x4[32 * j:32 * j + 32, (2 * p + i) % X4_RING, 0:rows, :],
                                     qk[32 * (hd % 4):32 * (hd % 4) + 32, hd // 4, b % 2, j:j + rows, :])\
                            .then_inc(x4_in[p % (X4_RING // 2)], 16)

            def store_v(b):
                left(sp, ("qkv", b, 5))
                for hd in range(HEADS):
                    sp.dma_start(v_d[HEADS * b + hd, R:R + H].rearrange("y c x -> c y x"),
                                 v[HD * hd:HD * hd + HD, b % 2, :, :]).then_inc(v_stored[b], 16)

            def load_tile(j):
                for i in range(2):
                    sp.wait_ge(sc_stored[i], 32 * (j + 1))
                if j >= 2:
                    sp.wait_ge(pv, PV_STEPS * (j - 1))
                    sp.wait_ge(pp, PP_STEPS * (j - 1))
                for i in range(4):
                    sp.dma_start(at[32 * i:32 * i + 32, j % 2, :, :],
                                 scores_d[4 * j + i].rearrange("k (y x) -> y k x", x=W)).then_inc(at_in[j % 2], 16)
                sp.wait_ge(sides, 32)
                for b in range(4 * j // HEADS, (4 * j + 3) // HEADS + 1):
                    sp.wait_ge(v_stored[b], 16 * HEADS)
                for i in range(4):
                    src = v_d[4 * j + i]
                    win = bass.AP(src.tensor, src.offset, [[V_ROW, H], [1, WIN * V_ROW]])
                    sp.dma_start(vw[32 * i:32 * i + 32, j % 2].rearrange("p r c x -> p (r c x)"), win)\
                        .then_inc(vw_in[j % 2], 16)

            def store_o(j):
                sp.wait_ge(normed, j + 1)
                for i in range(4):
                    sp.dma_start(o_d[4 * j + i].rearrange("c (y x) -> y c x", x=W), o_t[32 * i:32 * i + 32, :, :])\
                        .then_inc(o_stored, 16)

            def load_o(b):
                sp.wait_ge(o_stored, 64 * ((HEADS * b + HEADS - 1) // 4 + 1))
                if b:
                    sp.wait_ge(job_done, JOB["mlp", b - 1, 1])
                sp.dma_start(o[:, :], o_d[HEADS * b:HEADS * (b + 1)].rearrange("i c n -> (i c) n")).then_inc(o_in, 16)

            put_x4(0)
            put_x4(1)
            store_v(0)
            put_x4(2)
            for p in range(PAIRS):
                if p + 3 < PAIRS:
                    put_x4(p + 3)
                if p % 3 == 0 and p // 3 + 1 < B:
                    store_v(p // 3 + 1)
                if p % 2:
                    load_tile(p // 2)
                if p % 2 == 0 and p >= 4:
                    store_o(p // 2 - 2)
                    if p // 2 - 2 in O_AFTER:
                        load_o(O_AFTER[p // 2 - 2])
            for j in range(TILES - 2, TILES):
                store_o(j)
                if j in O_AFTER:
                    load_o(O_AFTER[j])
            for b in range(B):
                for th in range(2):
                    left(sp, ("mlp", b, 8 + th))
                    sp.dma_start(t["out"][b][:, cols(th)], x1[:, b, cols(th)]).then_inc(out_s, 16)
            sp.wait_ge(out_s, 32 * B)
            sp.wait_ge(o_stored, 16 * IMAGES)

        @block.tensor
        def _(pe):
            def free(job):
                if job > G_BANKS:
                    left(pe, list(JOB)[job - G_BANKS - 1])

            def bank(job):
                return g_ps[:, job % G_BANKS, :]

            def qkv(b, i):
                n = JOB["qkv", b, i]
                free(n)
                m, th = i // 2, i % 2
                w = (slice(0, 128), slice(128, 192), slice(192, 288))[m]
                pe.matmul(bank(n)[0:w.stop - w.start, :], qkv_s[:, w], x1[:, b, cols(th)], start=True,
                          stop=True).then_inc(job_done, 1)

            def score(p):
                pe.wait_ge(x4_in[p % 3], 16 * 8 * (p // 3 + 1))
                for th in range(2):
                    if p >= 2:
                        pe.wait_ge(sc_out, 2 * (p - 2) + th + 1)
                    for dx in range(WIN):
                        for w, rows, y0 in ((w_up, 128, 0), (w_low, 96, 4)):
                            for i in range(2):
                                y = 16 * th + y0
                                mm = pe.matmul(sc_ps[64 * i:64 * i + 64, p % 2, th, :], w[:, dx, :],
                                               x4[0:rows, (2 * p + i) % X4_RING, y:y + 16, dx:dx + W],
                                               start=(dx == 0 and y0 == 0), stop=(dx == WIN - 1 and y0 == 4))
                    mm.then_inc(scored, 1)

            def mlp(b, i):
                n = JOB["mlp", b, i]
                free(n)
                if i < 2:
                    if i == 0:
                        pe.wait_ge(o_in, 16 * (b + 1))
                    pe.matmul(bank(n)[0:C, :], proj_w[:, :], o[:, cols(i)], start=True, stop=True)\
                        .then_inc(job_done, 1)
                elif i < 8:
                    m, th = (i - 2) % 3, (i - 2) // 3
                    left(pe, ("mlp", b, th))
                    pe.matmul(bank(n)[:, :], c1_w[:, 128 * m:128 * m + 128], x1[:, b, cols(th)], start=True,
                              stop=True).then_inc(job_done, 1)
                else:
                    th = i - 8
                    left(pe, ("mlp", b, 4 + 3 * th))
                    for m in range(3):
                        mm = pe.matmul(bank(n)[0:C, :], c2_w[:, m, :], up[:, m, cols(th)], start=(m == 0),
                                       stop=(m == 2))
                    mm.then_inc(job_done, 1)

            pe.wait_ge(loaded, 16 * L1_LOADS)
            pe.wait_ge(bn_step, BN_DONE)
            for m, w in enumerate((slice(0, 128), slice(128, 192), slice(192, 288))):
                n = JOB["bias", m]
                pe.matmul(bank(n)[0:w.stop - w.start, 0:1], qkv_w[:, w], bn_shift[:, :], start=True,
                          stop=True).then_inc(job_done, 1)
            for i in range(6):
                qkv(0, i)
            for p in range(PAIRS):
                if p % 3 == 0 and p // 3 + 1 < B:
                    for i in range(6):
                        qkv(p // 3 + 1, i)
                for m in MLP_AFTER.get(p, ()):
                    for i in range(10):
                        mlp(m, i)
                score(p)
            for m in MLP_LAST:
                for i in range(10):
                    mlp(m, i)

        @block.scalar
        def _(act):
            def qkv(b, i):
                n = JOB["qkv", b, i]
                m, th = i // 2, i % 2
                act.wait_ge(job_done, n)
                y0 = 16 * th
                rows = (128, 64, C)[m]
                src = g_ps[0:rows, n % G_BANKS, :].rearrange("p (y x) -> p y x", x=W)
                if m < 2:
                    if b >= 2 and i == 0:
                        for s in x4_in:
                            act.wait_ge(s, 16 * 8 * (b - 1))
                    dst = qk[0:rows, m, b % 2, R + y0:R + y0 + 16, R:R + W]
                else:
                    if b >= 2 and th == 0:
                        act.wait_ge(v_stored[b - 2], 16 * HEADS)
                    dst = v[:, b % 2, y0:y0 + 16, R:R + W]
                nc.scalar.activation(dst, src, ACT.Identity, bias=qkv_bias[0:rows, m:m + 1],
                                     scale=qkv_scale[0:rows, m:m + 1]).then_inc(left_act, 1)

            def store_scores(p):
                for th in range(2):
                    act.wait_ge(scored, 2 * p + th + 1)
                    if p >= 2 and th == 0:
                        act.wait_ge(sc_stored[p % 2], 32 * (p // 2))
                    nc.scalar.activation(sc[:, p % 2, cols(th)], sc_ps[:, p % 2, th, :], ACT.Identity,
                                         bias=rel[:, p % 3:p % 3 + 1]).then_inc(sc_out, 1)
                act.wait_ge(sc_out, 2 * p + 2)
                for i in range(2):
                    act.dma_start(scores_d[2 * p + i], sc[64 * i:64 * i + K2, p % 2, :]).then_inc(sc_stored[p % 2], 16)

            def exps(j):
                act.wait_ge(less, j + 1)
                nc.scalar.activation(at[:, j % 2], at[:, j % 2], ACT.Exp).then_inc(exped, 1)

            def mlp(b):
                for i in range(2, 8):
                    n = JOB["mlp", b, i]
                    m, th = (i - 2) % 3, (i - 2) // 3
                    act.wait_ge(job_done, n)
                    nc.scalar.activation(up[:, m, cols(th)], g_ps[:, n % G_BANKS, :], ACT.Gelu,
                                         bias=c1_b[:, m:m + 1]).then_inc(left_act, 1)

            act.wait_ge(bn_step, BN_VAR)
            nc.scalar.activation(bn_scale[:, :], bn_mv[:, 1:2], ACT.Sqrt, bias=bn[:, 2:3]).then_inc(bn_step, 1)
            act.wait_ge(bn_step, BN_BIAS)
            act.wait_ge(zeroed, ZEROED)
            for i in range(6):
                qkv(0, i)
            for p in range(PAIRS):
                if p % 3 == 0 and p // 3 + 1 < B:
                    for i in range(6):
                        qkv(p // 3 + 1, i)
                for m in MLP_AFTER.get(p, ()):
                    mlp(m)
                store_scores(p)
                if p % 2 == 0 and p:
                    exps(p // 2 - 1)
            exps(TILES - 1)
            for m in MLP_LAST:
                mlp(m)

        def product(engine, j, dy, prod):
            e = at[:, j % 2, WIN * dy:WIN * dy + WIN, :].unsqueeze(2).broadcast_to([128, WIN, HD, W])
            win = vw[:, j % 2, dy]
            shifted = bass.AP(win.tensor, win.offset, [list(win.ap[0]), [1, WIN], [HP, HD], [1, W]])
            return engine.tensor_tensor(prod[:, :, :, :], shifted, e, ALU.mult)

        def fold(engine, eng, s, base, prod, acc, first):
            for n, (lo, hi) in enumerate((((0, 3), (4, 7)), ((0, 2), (2, 4)), ((0, 1), (1, 2)))):
                eng.wait_ge(s, base + n)
                engine.tensor_tensor(prod[:, lo[0]:lo[1]], prod[:, lo[0]:lo[1]], prod[:, hi[0]:hi[1]],
                                     ALU.add).then_inc(s, 1)
            eng.wait_ge(s, base + 3)
            if first:
                engine.tensor_copy(acc[:, :, :], prod[:, 0]).then_inc(s, 1)
            else:
                engine.tensor_tensor(acc[:, :, :], acc[:, :, :], prod[:, 0], ALU.add).then_inc(s, 1)

        @block.gpsimd
        def _(pool):
            nc.gpsimd.memset(zeros[:, :], 0.0)
            nc.gpsimd.memset(qk[:, :, :, :, :], 0.0)
            nc.gpsimd.memset(v[:, :, :, :], 0.0).then_inc(zeroed, 1)
            for j in range(TILES):
                pool.wait_ge(soft, 3 * j + 1)
                pool.wait_ge(at_in[j % 2], 64 * (j // 2 + 1))
                nc.gpsimd.tensor_tensor(at[:, j % 2], at[:, j % 2],
                                        mx[:, :].unsqueeze(1).broadcast_to([128, K2, W]),
                                        ALU.subtract).then_inc(less, 1)
                pool.wait_ge(exped, j + 1)
                pool.wait_ge(vw_in[j % 2], 64 * (j // 2 + 1))
                for n, dy in enumerate(POOL_ROWS):
                    base = PP_STEPS * j + 5 * n
                    if n == 0 and j:
                        pool.wait_ge(normed, j)
                    if base:
                        pool.wait_ge(pp, base)
                    product(nc.gpsimd, j, dy, prod_p).then_inc(pp, 1)
                    fold(nc.gpsimd, pool, pp, base + 1, prod_p, acc_p, n == 0)

        @block.vector
        def _(dve):
            nc.vector.memset(w_up[:, :, :], 0.0)
            nc.vector.memset(w_low[:, :, :], 0.0)
            nc.vector.memset(rel[:, :], 0.0)
            nc.vector.memset(dm_b[:, :], 0.0)
            nc.vector.memset(bn[:, 2:3], BN_EPS).then_inc(zeroed, 1)
            for n in range(2 * B):
                nc.vector.bn_stats(bn_stats[:, n, :], x1[:, n // 2, cols(n % 2)]).then_inc(bn_step, 1)
            dve.wait_ge(bn_step, 2 * B)
            nc.vector.bn_aggr(bn_mv[:, :], bn_stats[:, :, :]).then_inc(bn_step, 1)
            dve.wait_ge(bn_step, BN_VAR + 1)
            nc.vector.reciprocal(bn_scale[:, :], bn_scale[:, :]).then_inc(bn_step, 1)
            dve.wait_ge(loaded, 16 * L1_LOADS)
            dve.wait_ge(bn_step, BN_VAR + 2)
            nc.vector.tensor_tensor(bn_scale[:, :], bn_scale[:, :], bn[:, 0:1], ALU.mult).then_inc(bn_step, 1)
            dve.wait_ge(bn_step, BN_VAR + 3)
            nc.vector.tensor_tensor(bn_shift[:, :], bn_mv[:, 0:1], bn_scale[:, :], ALU.mult).then_inc(bn_step, 1)
            dve.wait_ge(bn_step, BN_VAR + 4)
            nc.vector.tensor_tensor(bn_shift[:, :], bn[:, 1:2], bn_shift[:, :], ALU.subtract).then_inc(bn_step, 1)
            nc.vector.tensor_scalar(qkv_s[:, :], qkv_w[:, :], bn_scale[:, 0:1], None, ALU.mult).then_inc(bn_step, 1)
            nc.vector.tensor_scalar(rel[:, :], rel[:, :], dm_b[:, 0:1], None, ALU.add).then_inc(bn_step, 1)
            for m, rows in enumerate((128, 64, C)):
                n = JOB["bias", m]
                dve.wait_ge(job_done, n)
                nc.vector.scalar_tensor_tensor(out=qkv_bias[0:rows, m:m + 1], in0=g_ps[0:rows, n % G_BANKS, 0:1],
                                               scalar=qkv_b[0:rows, m:m + 1], in1=qkv_scale[0:rows, m:m + 1],
                                               op0=ALU.add, op1=ALU.mult).then_inc(left_dve, 1)
            dve.wait_ge(left_dve, 3)
            nc.vector.memset(mx[:, :], 0.0).then_inc(bn_step, 1)

            def mlp_out(b, i):
                n = JOB["mlp", b, i]
                bias = proj_b if i < 2 else c2_b
                dve.wait_ge(job_done, n)
                if i >= 8:
                    left(dve, ("mlp", b, i - 8))
                nc.vector.scalar_tensor_tensor(out=x1[:, b, cols(i % 2)], in0=g_ps[0:C, n % G_BANKS, :],
                                               scalar=bias[:, 0:1], in1=x1[:, b, cols(i % 2)],
                                               op0=ALU.add, op1=ALU.add).then_inc(left_dve, 1)

            def tile(j):
                dve.wait_ge(at_in[j % 2], 64 * (j // 2 + 1))
                if j:
                    dve.wait_ge(less, j)
                nc.vector.tensor_reduce(mx[:, :], at[:, j % 2].rearrange("p k x -> p x k"), AX.X, ALU.max)\
                    .then_inc(soft, 1)
                dve.wait_ge(exped, j + 1)
                nc.vector.tensor_reduce(den[:, 0, :], at[:, j % 2].rearrange("p k x -> p x k"), AX.X, ALU.add)\
                    .then_inc(soft, 1)
                dve.wait_ge(soft, 3 * j + 2)
                nc.vector.reciprocal(den[:, 1, :], den[:, 0, :]).then_inc(soft, 1)
                dve.wait_ge(vw_in[j % 2], 64 * (j // 2 + 1))
                for n, dy in enumerate(DVE_ROWS):
                    base = PV_STEPS * j + 5 * n
                    if base:
                        dve.wait_ge(pv, base)
                    product(nc.vector, j, dy, prod_v).then_inc(pv, 1)
                    fold(nc.vector, dve, pv, base + 1, prod_v, acc_v, n == 0)
                base = PV_STEPS * j + 5 * len(DVE_ROWS)
                dve.wait_ge(pv, base)
                dve.wait_ge(pp, PP_STEPS * (j + 1))
                nc.vector.tensor_tensor(acc_v[:, :, :], acc_v[:, :, :], acc_p[:, :, :], ALU.add).then_inc(pv, 1)
                dve.wait_ge(pv, base + 1)
                dve.wait_ge(soft, 3 * j + 3)
                if j:
                    dve.wait_ge(o_stored, 64 * j)
                nc.vector.tensor_tensor(o_t[:, :, :], acc_v[:, :, :],
                                        den[:, 1, :].unsqueeze(1).broadcast_to([128, HD, W]),
                                        ALU.mult).then_inc(normed, 1)

            for j in range(TILES):
                tile(j)
                for m in DVE_MLP.get(j, ()):
                    for i in (0, 1, 8, 9):
                        mlp_out(m, i)



def program(nc, t):
    scratch = (nc.dram_tensor("scores_d", (IMAGES, K2, L), F32, kind="Internal").ap(),
               nc.dram_tensor("v_d", (IMAGES, HP, HD, HP), F32, kind="Internal").ap(),
               nc.dram_tensor("o_d", (IMAGES, HD, L), F32, kind="Internal").ap())
    with nc.sbuf_tensor("x1", [C, B, L], F32) as x1:
        mamba(nc, t, x1)
        attention(nc, t, x1, scratch)


def constants():
    center = np.stack([np.eye(C) - 1.0 / C, np.full((C, C), 1.0 / C)], 1)
    rep = np.zeros((PARTS, 32, 4, N_ST, GE))
    pick = np.zeros((N_ST, GE, 4, 32))
    for q in range(4):
        for e in range(GE):
            rep[:, GE * q + e, q, :, e] = 1.0
            pick[:, e, q, GE * q + e] = 1.0
    q_scale = np.ones((128, 3))
    q_scale[:, 0:2] = np.tile(np.repeat([HD ** -0.5, 1.0], HD), 4)[:, None]
    return {"center": center, "rep": rep.reshape(PARTS * 32, 4, 128), "pick": pick.reshape(128, 4, 32),
            "qkv_scale": q_scale}


def kernel(**inputs):
    import concourse.bacc as _bacc
    from concourse.bass_utils import run_bass_kernel_spmd as _run

    g = {k.replace("L0_conv_", "").replace("L1_conv_", ""): np.asarray(v) for k, v in inputs.items()}

    def col(v):
        return v.reshape(-1, 1)

    order = [s * C + hd * HD + c for hd in range(HEADS) for s in range(2) for c in range(HD)] + \
        list(range(2 * C, 3 * C))
    arrays = {
        "x": g["x"].reshape(B, C, L), "gamma": col(g["gamma"]), "beta": col(g["beta"]), "W_in": g["W_in"],
        "conv_w": g["conv_w"].T.reshape(1, TAPS * E_IN), "conv_b": col(g["conv_b"]), "W_xproj": g["W_xproj"],
        "W_dt": g["W_dt"], "b_dt": col(g["b_dt"]), "D": col(g["D"]), "W_out": g["W_out"],
        "A_log": g["A_log"].reshape(UNITS, GE, N_ST).transpose(2, 1, 0).reshape(128, UNITS),
        "bn_gamma": col(g["bn_gamma"]), "bn_beta": col(g["bn_beta"]),
        "qkv_w": g["qkv_w"][order].T, "qkv_b": col(g["qkv_b"][order]),
        "dm_w": g["dm_w"].transpose(2, 1, 3, 0).reshape(WIN * 2 * HD, WIN, K2), "dm_b": col(g["dm_b"]),
        "rel_bias": g["rel_bias"], "proj_w": g["proj_w"].T, "proj_b": col(g["proj_b"]),
        "c1_w": g["c1_w"].T, "c1_b": g["c1_b"].reshape(3, 128).T,
        "c2_w": g["c2_w"].T.reshape(3, 128, C).transpose(1, 0, 2), "c2_b": col(g["c2_b"]),
    }
    arrays.update({k: v.astype(np.float32) for k, v in constants().items()})
    nc = _bacc.Bacc("TRN2", target_bir_lowering=False, num_devices=1)
    t, feed = {}, {}
    for name, v in arrays.items():
        v = np.ascontiguousarray(v)
        feed[f"in_{name}"] = v
        t[name] = nc.dram_tensor(f"in_{name}", v.shape, F32, kind="ExternalInput").ap()
    t["out"] = nc.dram_tensor("out_x", (B, C, L), F32, kind="ExternalOutput").ap()
    program(nc, t)
    r = _run(nc, [feed], core_ids=[0])
    return r.results[0]["out_x"].reshape(B, C, H, W)
```

```python
from contextlib import ExitStack

import concourse.bass as bass
from concourse import mybir
import numpy as np

F32 = mybir.dt.float32
BF16 = mybir.dt.bfloat16
ALU = mybir.AluOpType
ACT = mybir.ActivationFunctionType
AX = mybir.AxisListType

B, C, H, W = 4, 96, 32, 32
L = H * W
HALF = L // 2
E_IN, N_ST, RANK, TAPS = 192, 16, 6, 4
PAD = TAPS - 1
E_LO, E_HI = 128, E_IN - 128
GE = 128 // N_ST
UNITS = E_IN // GE
QUADS = UNITS // 4
PHASES = 2 * B
SPAN = L + HALF
PARTS = 3
LN_EPS = 1e-5

A_RING, H_RING, HC_RING, ST_RING, U_BANKS, D_BANKS = 4, 3, 8, 8, 3, 2
HS = 2 * UNITS
ACT_AHEAD = 2
DT_LEAD, EXP_LEAD = 5, 5
XP = RANK + 2 * N_ST
SUM_AT = 16
CONV_AT, Z_AT, XP_AT, DT_AT = (0, 5, 10), (15, 26, 28), 17, (20, 22, 24)
LN_AT, OUT_AT = (30, 32, 34, 36), (38, 42)
SILU_AT = 15
EXP_AT, ONE_AT, LOG_AT, LOST_AT, LESS_AT, MAX_AT = 26, 24, 29, 27, 26, 30
U_AT = 30
DH_AT, DR_AT, DM_AT, DL_AT = 33, 33, 35, 35
UH_AT, UR_AT, UM_AT, UL_AT = 37, 37, 39, 39
Y0_AT, Y1_AT = 43, 10
LOADS = [4, 6, 10, 9]
SETUP = 5

HEADS, HD, WIN = 6, 16, 7
K2 = WIN * WIN
R = WIN // 2
HP = H + 2 * R
V_ROW = HD * HP
IMAGES = B * HEADS
PAIRS = IMAGES // 2
TILES = IMAGES // 4
X4_ROWS = H + 4
X4_RING = 6
G_BANKS = 4
BN_EPS = 1e-5
BN_VAR, BN_DONE, BN_BIAS = 2 * B + 1, 2 * B + 7, 2 * B + 9
ZEROED = 2
L1_LOADS = 13 + 4 + 2
DVE_ROWS, POOL_ROWS = (0, 1, 2, 3, 4), (5, 6)
PV_STEPS, PP_STEPS = 5 * len(DVE_ROWS) + 1, 5 * len(POOL_ROWS)
MLP_AFTER, MLP_LAST = {}, (0, 1, 2, 3)
DVE_MLP = {(4, 4): ((0, 0),), (5, 0): ((0, 8),), (5, 1): ((1, 0),), (5, 2): ((1, 8),), (5, 3): ((2, 0),),
           (5, 4): ((2, 8),)}
O_AFTER = {1: 0, 2: 1, 4: 2, 5: 3}


def halves(direction):
    return (0, 1) if direction == 0 else (1, 0)


def scan_order(ap, direction):
    return ap if direction == 0 else ap[:, ::-1]


def cols(th, n=HALF):
    return slice(th * n, (th + 1) * n)


def mamba(nc, t, x1, dt_d, u_d):
    with ExitStack() as ctx:
        def sb(name, shape, dt=F32):
            return ctx.enter_context(nc.sbuf_tensor(name, shape, dt))

        def ps(name, shape):
            return ctx.enter_context(nc.psum_tensor(name, shape, F32))

        def sem(name):
            return ctx.enter_context(nc.semaphore(name))

        w_z = sb("w_z", [C, E_IN])
        w_taps = sb("w_taps", [C, TAPS, E_IN])
        w_x = sb("w_x", [128, 2, XP])
        w_dt = sb("w_dt", [RANK, E_IN])
        w_out = sb("w_out", [128, 2, C])
        a_neg = sb("a_neg", [128, UNITS])
        conv_b, b_dt, d_skip = (sb(n, [128, 2]) for n in ("conv_b", "b_dt", "d_skip"))
        norm = sb("norm", [C, 3])
        center = sb("center", [C, 2, C])
        rep = sb("rep", [PARTS * 32, 4, 128], BF16)
        pick = sb("pick", [128, 8, 32])
        xn = sb("xn", [C, PAD + L + PAD])
        xi = xn[:, PAD:PAD + L]
        var = sb("var", [C, L])
        t01 = sb("t01", [128, 2 * SPAN])
        t0, t1 = t01[:, 0:SPAN], t01[:, SPAN:2 * SPAN]
        u_parts = t01[:, 0:PARTS * SPAN // 2].bitcast(BF16).rearrange("p (a s) -> p a s", a=PARTS)
        t2, t3, t4 = (sb(f"t{i}", [128, SPAN]) for i in (2, 3, 4))
        conv_w_rows = t2[0:C, 0:TAPS * E_IN].rearrange("p (j e) -> p j e", j=TAPS)
        w_in = t2[0:C, TAPS * E_IN:(TAPS + 1) * E_IN]
        rep_f = t3[0:PARTS * 32, 0:4 * 128].rearrange("p (q m) -> p q m", q=4)
        dbc = sb("dbc", [XP, L])
        xr = sb("xr", [128, 2, SPAN])
        z = sb("z", [128, SPAN])
        y = sb("y", [128, SPAN])
        dt_parts = sb("dt_parts", [128, PARTS, SPAN], BF16)
        dt_st = sb("dt_st", [PARTS * 32, ST_RING, L], BF16)
        u_st = sb("u_st", [PARTS * 32, ST_RING, L], BF16)
        b_rep = sb("b_rep", [128, 2, L])
        c_rep = sb("c_rep", [128, 2, L])
        a = sb("a", [128, A_RING, L])
        h = sb("h", [128, H_RING, L])
        hc = sb("hc", [128, HC_RING, L])
        dt_ps = ps("dt_ps", [128, D_BANKS, HALF])
        u_ps = ps("u_ps", [128, U_BANKS, HALF])
        y_ps = ps("y_ps", [128, 2, HALF])
        f_ps = ps("f_ps", [128, HALF])

        loaded = [sem(f"loaded{i}") for i in range(4)]
        set_up = sem("set_up")
        a_exp = sem("a_exp")
        job_done = sem("job_done")
        job_read = sem("job_read")
        act_step = sem("act_step")
        act_ln = sem("act_ln")
        pool_ln = sem("pool_ln")
        pool_step = sem("pool_step")
        dve_step = sem("dve_step")
        dt_out = sem("dt_out")
        u_out = sem("u_out")
        dt_stacked = sem("dt_stacked")
        u_stacked = sem("u_stacked")
        b_in = sem("b_in")
        c_in = sem("c_in")
        dt_spread = sem("dt_spread")
        u_spread = sem("u_spread")
        exp_done = sem("exp_done")
        bu_done = sem("bu_done")
        scanned = sem("scanned")
        hc_done = sem("hc_done")
        summed = sem("summed")
        z_ready = sem("z_ready")
        y_read = sem("y_read")
        y_step = sem("y_step")

        block = ctx.enter_context(nc.Block())

        def ran(phase, k):
            return UNITS * phase + k

        def count(phase, name, seq_of):
            return sum(len(seq_of(p)) for p in range(phase)) + seq_of(phase).index(name) + 1

        def jobs(p):
            first = ["cen0", "cen1", "var0", "var1"] if p == 0 else []
            if p % 2 == 0:
                return first + ["conv0", "conv1", "conv2", "xp", "dt0", "dt1", "dt2"]
            return ["conv0", "conv1", "conv2", "z0", "xp", "dt0", "dt1", "dt2", "z1", "z2"] + \
                (["cen0", "cen1", "var0", "var1"] if p + 1 < PHASES else []) + \
                (["out0", "out1"] if p > 1 else [])

        def act_steps(p):
            return ["xr", "e", "ln", "dh", "dm", "uh", "um"]

        def pool_steps(p):
            return ["y1", "l", "u"]

        def dve_steps(p):
            return ["c", "dt", "dr", "dl", "ur", "ul"]

        def J(p, name):
            return count(p, name, jobs)

        def A(p, name):
            return count(p, name, act_steps)

        def P(p, name):
            return count(p, name, pool_steps)

        def V(p, name):
            return count(p, name, dve_steps)

        def ln_front(b):
            return max(2 * b - 1, 0)

        ALL_JOBS = J(PHASES - 1, "out1")
        PARTS_OUT = 16 * PARTS * 2
        STACK = 16 * PARTS
        SPREAD = 16 * GE

        @block.sync
        def _(sp):
            def both(column, name):
                return [(column[:, 0:1], t[name][0:E_LO]), (column[0:E_HI, 1:2], t[name][E_LO:E_IN]),
                        (column[E_HI:128, 1:2], t[name][E_LO:E_IN])]

            groups = [
                [(x1[:, 0, :], t["x"][0]), (center[:, :, :], t["center"]), (norm[:, 0:1], t["gamma"]),
                 (norm[:, 1:2], t["beta"])],
                [(conv_w_rows.rearrange("p j e -> p (j e)"), t["conv_w"].to_broadcast([C, TAPS * E_IN])),
                 (w_in, t["W_in"][:, 0:E_IN]),
                 (w_z[:, :], t["W_in"][:, E_IN:])] + both(conv_b, "conv_b"),
                [(w_x[:, 0, :], t["W_xproj"][0:E_LO]), (w_x[0:E_HI, 1, :], t["W_xproj"][E_LO:E_IN]),
                 (w_x[E_HI:128, 1, :], t["W_xproj"][E_LO:E_IN]), (w_dt[:, :], t["W_dt"]),
                 (rep_f, t["rep"]), (pick[:, :, :], t["pick"]), (a_neg[:, :], t["A_log"])] + both(b_dt, "b_dt"),
                [(w_out[:, 0, :], t["W_out"][0:E_LO]), (w_out[0:E_HI, 1, :], t["W_out"][E_LO:E_IN]),
                 (w_out[E_HI:128, 1, :], t["W_out"][E_LO:E_IN])] + both(d_skip, "D") +
                [(x1[:, b, :], t["x"][b]) for b in range(1, B)],
            ]
            assert [len(g) for g in groups] == LOADS
            for group, done in zip(groups, loaded):
                for dst, src in group:
                    sp.dma_start(dst, src).then_inc(done, 16)

            def store(ph, parts, part, dram, done):
                low, high = dram
                sp.dma_start(low[part], parts[:, part, 0:L]).then_inc(done, 16)
                sp.dma_start(high[part].rearrange("c (h l) -> h c l", h=2), parts[:, part, L:SPAN])\
                    .then_inc(done, 16)

            def stack(ph, dst, dram, done):
                low = dram[0].rearrange("a (r s) l -> (a r) s l", s=4)
                high = dram[1].rearrange("a (r s) l -> (a r) s l", s=2)
                for s in (0, 2):
                    at = (6 * ph + s) % ST_RING
                    sp.dma_start(dst[:, at:at + 2, :], low[:, s:s + 2, :]).then_inc(done, 16)
                at = (6 * ph + 4) % ST_RING
                sp.dma_start(dst[:, at:at + 2, :], high).then_inc(done, 16)

            for ph in range(PHASES):
                sp.wait_ge(job_read, J(ph, "xp"))
                for dst, row, done in ((b_rep, RANK, b_in), (c_rep, RANK + N_ST, c_in)):
                    if ph >= 2:
                        if dst is b_rep:
                            sp.wait_ge(bu_done, 2 * ran(ph - 1, 0))
                        else:
                            sp.wait_ge(hc_done, ran(ph - 1, 0))
                    for e in range(GE):
                        sp.dma_start(dst[N_ST * e:N_ST * (e + 1), ph % 2, :], dbc[row:row + N_ST, :])\
                            .then_inc(done, 16)
                if ph >= 1:
                    sp.wait_ge(u_spread, 2 * ran(ph - 1, 16))
                for dst, parts, dram, stored, done, steps in (
                    (dt_st, dt_parts, dt_d, dt_out, dt_stacked,
                     ((act_step, A(ph, "dh")), (act_step, A(ph, "dm")), (dve_step, V(ph, "dl")))),
                    (u_st, u_parts, u_d, u_out, u_stacked,
                     ((act_step, A(ph, "uh")), (act_step, A(ph, "um")), (dve_step, V(ph, "ul")))),
                ):
                    if ph:
                        sp.wait_ge(done, STACK * ph)
                    for part, (made, at) in enumerate(steps):
                        sp.wait_ge(made, at)
                        store(ph, parts, part, dram, stored)
                    sp.wait_ge(stored, PARTS_OUT * (ph + 1))
                    stack(ph, dst, dram, done)

        @block.tensor
        def _(pe):
            def free(job):
                if job > 1:
                    pe.wait_ge(job_read, job - 1)

            def out_job(b, th, part):
                if part == 0:
                    pe.wait_ge(y_step, 3 * b + 3)
                    pe.matmul(f_ps[0:C, :], w_out[:, 0, :], y[:, cols(th)], start=True, stop=False)
                else:
                    p = E_HI * th
                    pe.matmul(f_ps[0:C, :], w_out[p:p + E_HI, 1, :], y[p:p + E_HI, L:SPAN], start=False,
                              stop=True).then_inc(job_done, 1)

            def layer_norm(b, step):
                ph, th = ln_front(b), step % 2
                free(J(ph, ("cen", "var")[step // 2] + str(th)))
                if step < 2:
                    pe.matmul(f_ps[0:C, :], center[:, 0, :], x1[:, b, cols(th)], start=True,
                              stop=True).then_inc(job_done, 1)
                else:
                    pe.wait_ge(act_ln, 5 * b + th + 1)
                    pe.matmul(f_ps[0:C, :], center[:, 1, :], var[:, cols(th)], start=True,
                              stop=True).then_inc(job_done, 1)

            def front(ph, hs):
                d, b = ph % 2, ph // 2
                shifts = [2 * PAD - j if d else j for j in range(TAPS)]
                for job, at in enumerate(CONV_AT):
                    j = hs - at
                    if not 0 <= j < TAPS:
                        continue
                    if j == 0:
                        free(J(ph, f"conv{job}"))
                        if job == 0:
                            pe.wait_ge(act_ln, 5 * b + 5)
                    for th in ((job,) if job < 2 else (0, 1)):
                        s = shifts[j] + th * HALF
                        out, w = (f_ps[:, :], w_taps[:, j, 0:E_LO]) if job < 2 else \
                            (f_ps[E_HI * th:E_HI * (th + 1), :], w_taps[:, j, E_LO:E_IN])
                        mm = pe.matmul(out, w, xn[:, s:s + HALF], start=(j == 0), stop=(j == TAPS - 1))
                    if j == TAPS - 1:
                        mm.then_inc(job_done, 1)
                if d == 1 and hs in Z_AT[:2]:
                    th = Z_AT.index(hs)
                    free(J(ph, f"z{th}"))
                    pe.matmul(f_ps[:, :], w_z[:, 0:E_LO], xi[:, cols(th)],
                              start=True, stop=True).then_inc(job_done, 1)
                if d == 1 and hs == Z_AT[2]:
                    free(J(ph, "z2"))
                    for th in range(2):
                        mm = pe.matmul(f_ps[E_HI * th:E_HI * (th + 1), :], w_z[:, E_LO:E_IN],
                                       xi[:, cols(th)], start=True, stop=True)
                    mm.then_inc(job_done, 1)
                if hs == XP_AT:
                    free(J(ph, "xp"))
                    pe.wait_ge(act_step, A(ph, "xr"))
                    for th in range(2):
                        pe.matmul(f_ps[64 * th:64 * th + XP, :], w_x[:, 0, :], xr[:, d, cols(th)],
                                  start=True, stop=False)
                if hs == XP_AT + 1:
                    for th in range(2):
                        p = E_HI * th
                        mm = pe.matmul(f_ps[64 * th:64 * th + XP, :], w_x[p:p + E_HI, 1, :],
                                       xr[p:p + E_HI, d, L:SPAN], start=False, stop=True)
                    mm.then_inc(job_done, 1)
                if hs in DT_AT[:2]:
                    th = DT_AT.index(hs)
                    free(J(ph, f"dt{th}"))
                    pe.matmul(f_ps[:, :], w_dt[:, 0:E_LO], dbc[0:RANK, cols(th)], start=True,
                              stop=True).then_inc(job_done, 1)
                if hs == DT_AT[2]:
                    free(J(ph, "dt2"))
                    for th in range(2):
                        mm = pe.matmul(f_ps[E_HI * th:E_HI * (th + 1), :], w_dt[:, E_LO:E_IN],
                                       dbc[0:RANK, cols(th)], start=True, stop=True)
                    mm.then_inc(job_done, 1)
                if d == 1 and b + 1 < B and hs in LN_AT:
                    layer_norm(b + 1, LN_AT.index(hs))
                for th, at in enumerate(OUT_AT):
                    if d == 1 and b > 0 and hs in (at, at + 1):
                        if hs == at:
                            free(J(ph, f"out{th}"))
                        out_job(b - 1, th, hs - at)

            def spread_dt(n):
                ph, hs = n // HS, n % HS
                if ph == PHASES:
                    return
                if hs == 0:
                    pe.wait_ge(dt_stacked, STACK * (ph + 1))
                if n >= D_BANKS:
                    pe.wait_ge(exp_done, n - D_BANKS + 1)
                pe.matmul(dt_ps[:, n % D_BANKS, :], rep[:, hs // 2 % 4, :],
                          dt_st[:, (6 * ph + hs // 8) % ST_RING, cols(halves(ph % 2)[hs % 2])],
                          start=True, stop=True).then_inc(dt_spread, 1)

            def spread_u(n):
                ph, hs = n // HS, n % HS
                if hs == 0:
                    pe.wait_ge(u_stacked, STACK * (ph + 1))
                if n >= U_BANKS:
                    pe.wait_ge(scanned, n - U_BANKS + 1)
                pe.matmul(u_ps[:, n % U_BANKS, :], rep[:, hs // 2 % 4, :],
                          u_st[:, (6 * ph + hs // 8) % ST_RING, cols(halves(ph % 2)[hs % 2])],
                          start=True, stop=True).then_inc(u_spread, 1)

            def sum_states(q, part):
                ph, m = q // QUADS, q % QUADS
                y_tile = 2 * ph + (m >= 4)
                if part == 0:
                    pe.wait_ge(hc_done, 4 * q + 4)
                    if m in (0, 4) and y_tile:
                        pe.wait_ge(y_read, y_tile)
                for i in range(4):
                    if m < 4:
                        u, th, v = i, part, m
                        out, first, last = y_ps[32 * u:32 * u + 32, th, :], m == 0, m == 3
                    else:
                        u, th = 2 * (i % 2) + part, i // 2
                        v = 4 + 2 * (m - 4) + u % 2
                        p = 32 * (u // 2) + E_HI * th
                        out, first, last = y_ps[p:p + 32, 0, :], m == 4 and part == 0, m == 5 and part == 1
                    mm = pe.matmul(out, pick[:, v, :], hc[:, (4 * q + u) % HC_RING, cols(th)],
                                   start=first, stop=last)
                if part:
                    mm.then_inc(summed, 1)

            pe.wait_ge(loaded[0], 16 * LOADS[0])
            for step in range(4):
                layer_norm(0, step)
            pe.wait_ge(loaded[1], 16 * LOADS[1])
            pe.wait_ge(set_up, 3)
            for hs in range(HS):
                if hs == XP_AT:
                    pe.wait_ge(loaded[2], 16 * LOADS[2])
                front(0, hs)
            pe.wait_ge(set_up, SETUP)
            pe.wait_ge(loaded[3], 16 * LOADS[3])
            for n in range(DT_LEAD):
                spread_dt(n)
            for ph in range(PHASES):
                for hs in range(HS):
                    n = HS * ph + hs
                    spread_u(n)
                    q, part = divmod(n - SUM_AT, 8)
                    if q >= 0 and part < 2:
                        sum_states(q, part)
                    if ph + 1 < PHASES:
                        front(ph + 1, hs)
                    spread_dt(n + DT_LEAD)
            for q in range(-(-(HS * PHASES - SUM_AT) // 8), QUADS * PHASES):
                for part in range(2):
                    sum_states(q, part)
            for th in range(2):
                free(ALL_JOBS + th + 1)
                for part in range(2):
                    out_job(B - 1, th, part)

        @block.scalar
        def _(act):
            def leave(ph, job, out, src, func=ACT.Identity, **kw):
                act.wait_ge(job_done, J(ph, job))
                nc.scalar.activation(out, src, func, **kw).then_inc(job_read, 1)

            def layer_norm(b, step):
                ph, th = ln_front(b), step % 2
                if step < 2:
                    if step == 0 and b:
                        act.wait_ge(job_done, J(ph, "z2"))
                    leave(ph, f"cen{th}", xi[:, cols(th)], f_ps[0:C, :])
                    act.wait_ge(job_read, J(ph, f"cen{th}"))
                    nc.scalar.activation(var[:, cols(th)], xi[:, cols(th)], ACT.Square).then_inc(act_ln, 1)
                elif step < 4:
                    leave(ph, f"var{th}", var[:, cols(th)], f_ps[0:C, :])
                elif step == 4:
                    act.wait_ge(job_read, J(ph, "var1"))
                    nc.scalar.activation(var[:, :], var[:, :], ACT.Ln, bias=norm[:, 2:3]).then_inc(act_ln, 1)
                    act.wait_ge(act_ln, 5 * b + 3)
                    nc.scalar.activation(var[:, :], var[:, :], ACT.Exp, scale=-0.5).then_inc(act_ln, 1)
                else:
                    act.wait_ge(pool_ln, b + 1)
                    nc.scalar.activation(xi, xi, ACT.Identity, scale=norm[:, 0:1], bias=norm[:, 1:2])\
                        .then_inc(act_ln, 1)

            def front(ph, hs):
                d, b = ph % 2, ph // 2
                for th in range(2):
                    if hs == CONV_AT[th] + TAPS:
                        if th == 0 and ph:
                            act.wait_ge(pool_step, P(ph - 1, "u"))
                            act.wait_ge(dve_step, V(ph - 1, "ul"))
                        leave(ph, f"conv{th}", t3[:, cols(th)], f_ps[:, :], bias=conv_b[:, 0:1])
                if hs == CONV_AT[2] + TAPS:
                    leave(ph, "conv2", t3[:, L:SPAN], f_ps[:, :], bias=conv_b[:, 1:2])
                if hs == SILU_AT:
                    if ph >= 2 and d == 0:
                        act.wait_ge(y_read, 2 * ph - 2)
                    if ph >= 2 and d == 1:
                        act.wait_ge(y_step, 3 * (b - 1) + 2)
                    act.wait_ge(job_read, J(ph, "conv2"))
                    nc.scalar.activation(xr[:, d, :], t3[:, :], ACT.Silu).then_inc(act_step, 1)
                if d == 1 and hs - 1 in Z_AT[:2]:
                    th = Z_AT.index(hs - 1)
                    if b and not th:
                        act.wait_ge(y_step, 3 * b)
                    leave(ph, f"z{th}", z[:, cols(th)], f_ps[:, :])
                if d == 1 and hs == Z_AT[2] + 1:
                    leave(ph, "z2", z[:, L:SPAN], f_ps[:, :])
                if hs == XP_AT + 2:
                    if ph:
                        act.wait_ge(b_in, SPREAD * ph)
                        act.wait_ge(c_in, SPREAD * ph)
                    act.wait_ge(job_done, J(ph, "xp"))
                    nc.scalar.activation(dbc[:, cols(0)], f_ps[0:XP, :], ACT.Copy)
                    nc.scalar.activation(dbc[:, cols(1)], f_ps[64:64 + XP, :], ACT.Copy).then_inc(job_read, 1)
                if hs - 1 in DT_AT:
                    job = DT_AT.index(hs - 1)
                    to = cols(job)
                    tile = job // 2
                    act.wait_ge(job_done, J(ph, f"dt{job}"))
                    nc.scalar.activation(t2[:, to], f_ps[:, :], ACT.Identity, bias=b_dt[:, tile:tile + 1])
                    nc.scalar.activation(t3[:, to], f_ps[:, :], ACT.Abs, bias=b_dt[:, tile:tile + 1])\
                        .then_inc(job_read, 1)
                if hs == EXP_AT:
                    act.wait_ge(job_read, J(ph, "dt2"))
                    nc.scalar.activation(t4[:, :], t3[:, :], ACT.Exp, scale=-1.0).then_inc(act_step, 1)
                if hs == LOG_AT:
                    if ph:
                        act.wait_ge(u_out, PARTS_OUT * ph)
                    act.wait_ge(pool_step, P(ph, "y1"))
                    nc.scalar.activation(t1[:, :], t3[:, :], ACT.Ln).then_inc(act_step, 1)
                if hs == DH_AT:
                    if ph:
                        act.wait_ge(dt_out, PARTS_OUT * ph)
                    act.wait_ge(dve_step, V(ph, "dt"))
                    nc.scalar.activation(dt_parts[:, 0, :], t2[:, :], ACT.Copy).then_inc(act_step, 1)
                if hs == DM_AT:
                    act.wait_ge(dve_step, V(ph, "dr"))
                    nc.scalar.activation(dt_parts[:, 1, :], t1[:, :], ACT.Copy).then_inc(act_step, 1)
                if hs == UH_AT:
                    act.wait_ge(pool_step, P(ph, "u"))
                    act.wait_ge(dve_step, V(ph, "dl"))
                    nc.scalar.activation(u_parts[:, 0, :], t3[:, :], ACT.Copy).then_inc(act_step, 1)
                if hs == UM_AT:
                    act.wait_ge(dve_step, V(ph, "ur"))
                    nc.scalar.activation(u_parts[:, 1, :], t4[:, :], ACT.Copy).then_inc(act_step, 1)
                steps = [at + 1 for at in LN_AT] + [LN_AT[3] + 2, LN_AT[3] + 6]
                if d == 1 and b + 1 < B and hs in steps:
                    layer_norm(b + 1, steps.index(hs))

            def decay(n):
                ph, hs = n // HS, n % HS
                if ph == PHASES:
                    return
                k, th = n // 2, halves(ph % 2)[hs % 2]
                unit = hs // 2
                act.wait_ge(dt_spread, n + 1)
                if hs % 2 == 0 and k >= A_RING:
                    act.wait_ge(scanned, 2 * (k - A_RING + 1))
                nc.scalar.activation(a[:, k % A_RING, cols(th)], dt_ps[:, n % D_BANKS, :], ACT.Exp,
                                     scale=a_neg[:, unit:unit + 1]).then_inc(exp_done, 1)

            act.wait_ge(loaded[0], 16 * LOADS[0])
            act.wait_ge(set_up, 1)
            for step in range(6):
                layer_norm(0, step)
            act.wait_ge(loaded[1], 16 * LOADS[1])
            act.wait_ge(loaded[2], 16 * LOADS[2])
            nc.scalar.activation(a_neg[:, :], a_neg[:, :], ACT.Exp).then_inc(a_exp, 1)
            act.wait_ge(set_up, SETUP)
            for hs in range(HS):
                front(0, hs)
            for n in range(EXP_LEAD):
                decay(n)
            for ph in range(PHASES):
                for hs in range(HS):
                    decay(HS * ph + hs + EXP_LEAD)
                    if ph + 1 < PHASES:
                        front(ph + 1, hs + ACT_AHEAD)
                    if ph % 2 and hs + ACT_AHEAD == SILU_AT:
                        act.wait_ge(job_read, J(ph, "z2"))
                        nc.scalar.activation(z[:, :], z[:, :], ACT.Silu).then_inc(z_ready, 1)

        @block.gpsimd
        def _(pool):
            def layer_norm(b):
                pool.wait_ge(act_ln, 5 * b + 4)
                nc.gpsimd.tensor_tensor(xi, xi, var[:, :], ALU.mult).then_inc(pool_ln, 1)

            def front(ph, hs):
                d, b = ph % 2, ph // 2
                if hs == ONE_AT:
                    pool.wait_ge(act_step, A(ph, "e"))
                    nc.gpsimd.tensor_scalar(t3[:, :], t4[:, :], 1.0, 1.0, ALU.mult, ALU.add).then_inc(pool_step, 1)
                if hs == LESS_AT:
                    pool.wait_ge(act_step, A(ph, "ln"))
                    pool.wait_ge(dve_step, V(ph, "c"))
                    nc.gpsimd.tensor_tensor(t1[:, :], t1[:, :], t4[:, :], ALU.subtract).then_inc(pool_step, 1)
                if hs == U_AT:
                    pool.wait_ge(dve_step, V(ph, "dt"))
                    nc.gpsimd.tensor_tensor(t3[:, :], t2[:, :], xr[:, d, :], ALU.mult).then_inc(pool_step, 1)
                if d == 1 and b + 1 < B and hs == LN_AT[3] + 1:
                    layer_norm(b + 1)

            def read_out(ph, k):
                n = ran(ph, k)
                pool.wait_ge(scanned, 2 * n + 2)
                if n >= HC_RING:
                    pool.wait_ge(summed, (n - HC_RING) // 4 + 1)
                if k == 0:
                    pool.wait_ge(c_in, SPREAD * (ph + 1))
                nc.gpsimd.tensor_tensor(hc[:, n % HC_RING, :], h[:, n % H_RING, :], c_rep[:, ph % 2, :],
                                        ALU.mult).then_inc(hc_done, 1)

            layer_norm(0)
            for hs in range(HS):
                front(0, hs)
            for ph in range(PHASES):
                for k in range(UNITS):
                    read_out(ph, k)
                    if ph + 1 < PHASES:
                        front(ph + 1, 2 * k)
                        front(ph + 1, 2 * k + 1)

        @block.vector
        def _(dve):
            def front(ph, hs):
                d, b = ph % 2, ph // 2
                if hs == LOST_AT:
                    dve.wait_ge(pool_step, P(ph, "y1"))
                    nc.vector.scalar_tensor_tensor(out=t4[:, :], in0=t3[:, :], scalar=-1.0, in1=t4[:, :],
                                                   op0=ALU.add, op1=ALU.subtract).then_inc(dve_step, 1)
                if hs == MAX_AT:
                    dve.wait_ge(pool_step, P(ph, "l"))
                    nc.vector.scalar_tensor_tensor(out=t2[:, :], in0=t2[:, :], scalar=0.0, in1=t1[:, :],
                                                   op0=ALU.max, op1=ALU.add).then_inc(dve_step, 1)
                for th, at in enumerate(OUT_AT):
                    if d == 1 and b > 0 and hs == at + 2:
                        add_out(b - 1, th, J(ph, f"out{th}"))
                if hs == DR_AT:
                    dve.wait_ge(act_step, A(ph, "dh"))
                    nc.vector.tensor_tensor(t1[:, :], t2[:, :], dt_parts[:, 0, :], ALU.subtract).then_inc(dve_step, 1)
                if hs == DL_AT:
                    dve.wait_ge(act_step, A(ph, "dm"))
                    nc.vector.tensor_tensor(dt_parts[:, 2, :], t1[:, :], dt_parts[:, 1, :],
                                            ALU.subtract).then_inc(dve_step, 1)
                if hs == UR_AT:
                    dve.wait_ge(act_step, A(ph, "uh"))
                    nc.vector.tensor_tensor(t4[:, :], t3[:, :], u_parts[:, 0, :], ALU.subtract).then_inc(dve_step, 1)
                if hs == UL_AT:
                    dve.wait_ge(act_step, A(ph, "um"))
                    nc.vector.tensor_tensor(u_parts[:, 2, :], t4[:, :], u_parts[:, 1, :],
                                            ALU.subtract).then_inc(dve_step, 1)

            def add_out(b, th, job):
                dve.wait_ge(job_done, job)
                nc.vector.scalar_tensor_tensor(out=x1[:, b, cols(th)], in0=f_ps[0:C, :], scalar=0.5,
                                               in1=x1[:, b, cols(th)], op0=ALU.mult, op1=ALU.add).then_inc(job_read, 1)

            def take_y(ph, tile):
                d, b = ph % 2, ph // 2
                s = slice(0, L) if tile == 0 else slice(L, SPAN)
                src = y_ps[:, :, :].rearrange("p a n -> p (a n)") if tile == 0 else y_ps[:, 0, :]
                dve.wait_ge(summed, QUADS * ph + (4 if tile == 0 else 6))
                if d == 0:
                    if b > 0 and tile == 0:
                        dve.wait_ge(job_done, J(2 * b + 1, "out1"))
                    nc.vector.scalar_tensor_tensor(out=y[:, s], in0=xr[:, d, s], scalar=d_skip[:, tile:tile + 1],
                                                   in1=src, op0=ALU.mult, op1=ALU.add).then_inc(y_read, 1)
                    return
                dve.wait_ge(y_read, 2 * ph - 1 + tile)
                nc.vector.tensor_tensor(y[:, s], y[:, s], src, ALU.add).then_inc(y_read, 1)
                dve.wait_ge(y_read, 2 * ph + 1 + tile)
                nc.vector.scalar_tensor_tensor(out=y[:, s], in0=xr[:, d, s], scalar=d_skip[:, tile:tile + 1],
                                               in1=y[:, s], op0=ALU.mult, op1=ALU.add).then_inc(y_step, 1)

            def gate(b):
                dve.wait_ge(y_step, 3 * b + 2)
                dve.wait_ge(z_ready, b + 1)
                nc.vector.tensor_tensor(y[:, :], y[:, :], z[:, :], ALU.mult).then_inc(y_step, 1)

            def times_b(n):
                ph, hs = n // HS, n % HS
                if ph == PHASES:
                    return
                if hs == 0:
                    dve.wait_ge(b_in, SPREAD * (ph + 1))
                dve.wait_ge(u_spread, n + 1)
                nc.vector.tensor_tensor(u_ps[:, n % U_BANKS, :], u_ps[:, n % U_BANKS, :],
                                        b_rep[:, ph % 2, cols(halves(ph % 2)[hs % 2])], ALU.mult).then_inc(bu_done, 1)

            def scan(n):
                ph, i = n // HS, n % 2
                d, k = ph % 2, n // 2
                th = halves(d)[i]
                place = k % H_RING
                before = HALF - 1 if d == 0 else HALF
                dve.wait_ge(exp_done, n + 1)
                dve.wait_ge(bu_done, n + 1)
                if i == 0 and k >= H_RING:
                    dve.wait_ge(hc_done, k - H_RING + 1)
                if i == 1:
                    dve.wait_ge(scanned, n)
                nc.vector.tensor_tensor_scan(
                    scan_order(h[:, place, cols(th)], d), scan_order(a[:, k % A_RING, cols(th)], d),
                    scan_order(u_ps[:, n % U_BANKS, :], d), h[:, place, before:before + 1] if i else 0.0,
                    ALU.mult, ALU.add).then_inc(scanned, 1)

            nc.vector.memset(xn[:, 0:PAD], 0.0)
            nc.vector.memset(xn[:, PAD + L:], 0.0)
            nc.vector.memset(norm[:, 2:3], LN_EPS).then_inc(set_up, 1)
            dve.wait_ge(loaded[1], 16 * LOADS[1])
            for part in range(2):
                j = slice(2 * part, 2 * part + 2)
                nc.vector.tensor_tensor(w_taps[:, j, :], conv_w_rows[:, j, :],
                                        w_in.unsqueeze(1).broadcast_to([C, 2, E_IN]), ALU.mult)\
                    .then_inc(set_up, 1)
            dve.wait_ge(loaded[2], 16 * LOADS[2])
            nc.vector.tensor_copy(rep[:, :, :], rep_f).then_inc(set_up, 1)
            dve.wait_ge(a_exp, 1)
            nc.vector.tensor_scalar(a_neg[:, :], a_neg[:, :], -1.0, None, ALU.mult).then_inc(set_up, 1)

            for hs in range(HS):
                front(0, hs)
            times_b(0)
            for ph in range(PHASES):
                for hs in range(HS):
                    n = HS * ph + hs
                    times_b(n + 1)
                    scan(n)
                    if ph + 1 < PHASES:
                        front(ph + 1, hs)
                    if hs == Y1_AT and ph > 0:
                        take_y(ph - 1, 1)
                        if ph % 2 == 0:
                            gate(ph // 2 - 1)
                    if hs == Y0_AT:
                        take_y(ph, 0)
            take_y(PHASES - 1, 1)
            gate(B - 1)
            for th in range(2):
                add_out(B - 1, th, ALL_JOBS + th + 1)
            dve.wait_ge(job_read, ALL_JOBS + 2)


def attention(nc, t, x1, scratch):
    scores_d, v_d, o_d = scratch
    with ExitStack() as ctx:
        def sb(name, shape, dt=F32):
            return ctx.enter_context(nc.sbuf_tensor(name, shape, dt))

        def ps(name, shape):
            return ctx.enter_context(nc.psum_tensor(name, shape, F32))

        def sem(name):
            return ctx.enter_context(nc.semaphore(name))

        qkv_w = sb("qkv_w", [C, 3 * C])
        qkv_s = sb("qkv_s", [C, 3 * C])
        qkv_b = sb("qkv_b", [128, 3])
        qkv_bias = sb("qkv_bias", [128, 3])
        qkv_scale = sb("qkv_scale", [128, 3])
        bn = sb("bn", [C, 3])
        bn_stats = sb("bn_stats", [C, 2 * B, nc.vector.BN_STATS_DIM])
        bn_mv = sb("bn_mv", [C, nc.vector.BN_AGGR_DIM])
        bn_scale, bn_shift = sb("bn_scale", [C, 1]), sb("bn_shift", [C, 1])
        w_up = sb("w_up", [128, WIN, 64])
        w_low = sb("w_low", [96, WIN, 64])
        rel = sb("rel", [128, HEADS // 2])
        dm_b = sb("dm_b", [128, 1])
        proj_w, proj_b = sb("proj_w", [C, C]), sb("proj_b", [C, 1])
        c1_w, c1_b = sb("c1_w", [C, 4 * C]), sb("c1_b", [128, 3])
        c2_w, c2_b = sb("c2_w", [128, 3, C]), sb("c2_b", [C, 1])
        qk = sb("qk", [128, 2, 2, HP, HP])
        v = sb("v", [C, 2, H, HP])
        zeros = sb("zeros", [IMAGES, R * V_ROW])
        x4 = sb("x4", [128, X4_RING, X4_ROWS, HP])
        sc = sb("sc", [128, 2, L])
        at = sb("at", [128, 2, K2, W])
        mx = sb("mx", [128, W])
        den = sb("den", [128, 2, W])
        vw = sb("vw", [128, 2, WIN, HD, HP])
        prod_v = sb("prod_v", [128, WIN, HD, W])
        prod_p = sb("prod_p", [128, WIN, HD, W])
        acc_v = sb("acc_v", [128, HD, W])
        acc_p = sb("acc_p", [128, HD, W])
        o_t = sb("o_t", [128, HD, W])
        o = sb("o", [C, L])
        up = sb("up", [128, 3, L])
        sc_ps = ps("sc_ps", [128, 2, 2, HALF])
        g_ps = ps("g_ps", [128, G_BANKS, HALF])

        loaded = sem("l1_loaded")
        zeroed = sem("zeroed")
        bn_step = sem("bn_step")
        job_done = sem("g_done")
        left_act = sem("left_act")
        left_dve = sem("left_dve")
        x4_in = [sem(f"x4_in{i}") for i in range(X4_RING // 2)]
        scored = sem("scored")
        sc_out = sem("sc_out")
        sc_stored = [sem(f"sc_stored{i}") for i in range(2)]
        sides = sem("sides")
        v_stored = [sem(f"v_stored{b}") for b in range(B)]
        at_in = [sem(f"at_in{i}") for i in range(2)]
        vw_in = [sem(f"vw_in{i}") for i in range(2)]
        soft = sem("soft")
        less = sem("less")
        exped = sem("exped")
        pv = sem("pv")
        pp = sem("pp")
        normed = sem("normed")
        o_stored = sem("o_stored")
        o_in = sem("o_in")
        out_s = sem("out_stored")

        block = ctx.enter_context(nc.Block())

        def job_list():
            seq = [("bias", m) for m in range(3)]
            for b in range(B):
                if b == 0:
                    seq += [("qkv", 0, i) for i in range(6)]
                for p in range(3 * b, 3 * b + 3):
                    if p == 3 * b and b + 1 < B:
                        seq += [("qkv", b + 1, i) for i in range(6)]
                    for m in MLP_AFTER.get(p, ()):
                        seq += [("mlp", m, i) for i in range(10)]
            for m in MLP_LAST:
                seq += [("mlp", m, i) for i in range(10)]
            return {name: n + 1 for n, name in enumerate(seq)}

        JOB = job_list()

        def by_dve(name):
            return name[0] == "bias" or name[0] == "mlp" and name[2] not in range(2, 8)

        def left(eng, name):
            mine = [n for n in JOB if by_dve(n) == by_dve(name)]
            eng.wait_ge(left_dve if by_dve(name) else left_act, mine.index(name) + 1)

        @block.sync
        def _(sp):
            loads = [(qkv_w[:, :], t["qkv_w"]), (qkv_b[:, 0:1], t["qkv_b"][0:128]),
                     (qkv_b[0:64, 1:2], t["qkv_b"][128:192]), (qkv_b[0:C, 2:3], t["qkv_b"][192:288]),
                     (qkv_scale[:, :], t["qkv_scale"]), (bn[:, 0:1], t["bn_gamma"]), (bn[:, 1:2], t["bn_beta"]),
                     (proj_w[:, :], t["proj_w"]), (proj_b[:, :], t["proj_b"]), (c1_w[:, :], t["c1_w"]),
                     (c1_b[:, :], t["c1_b"]), (c2_w[:, :, :], t["c2_w"]), (c2_b[:, :], t["c2_b"])]
            for i in range(2):
                rows = slice(64 * i, 64 * i + K2)
                loads += [(rel[rows, :], t["rel_bias"][:, i::2]), (dm_b[rows, :], t["dm_b"])]
            sp.wait_ge(zeroed, ZEROED)
            loads += [(w_up[:, :, 0:K2], t["dm_w"][0:128]), (w_low[:, :, 0:K2], t["dm_w"][128:224])]
            assert len(loads) == L1_LOADS
            with nc.allow_non_contiguous_dma(reason="small weights"):
                for dst, src in loads:
                    sp.dma_start(dst, src).then_inc(loaded, 16)
            for side in (0, R + H):
                sp.dma_start(v_d[:, side:side + R].rearrange("i r c x -> i (r c x)"), zeros[:, :])\
                    .then_inc(sides, 16)

            def put_x4(p):
                b = p // 3
                if p % 3 == 0:
                    left(sp, ("qkv", b, 3))
                if p >= X4_RING // 2:
                    sp.wait_ge(scored, 2 * (p - X4_RING // 2) + 2)
                for i in range(2):
                    hd = 2 * (p % 3) + i
                    for j in range(4):
                        rows = X4_ROWS if j < 3 else H
                        sp.dma_start(x4[32 * j:32 * j + 32, (2 * p + i) % X4_RING, 0:rows, :],
                                     qk[32 * (hd % 4):32 * (hd % 4) + 32, hd // 4, b % 2, j:j + rows, :])\
                            .then_inc(x4_in[p % (X4_RING // 2)], 16)

            def store_v(b):
                left(sp, ("qkv", b, 5))
                for hd in range(HEADS):
                    sp.dma_start(v_d[HEADS * b + hd, R:R + H].rearrange("y c x -> c y x"),
                                 v[HD * hd:HD * hd + HD, b % 2, :, :]).then_inc(v_stored[b], 16)

            def load_tile(j):
                for i in range(2):
                    sp.wait_ge(sc_stored[i], 32 * (j + 1))
                if j >= 2:
                    sp.wait_ge(pv, PV_STEPS * (j - 1))
                    sp.wait_ge(pp, PP_STEPS * (j - 1))
                for i in range(4):
                    sp.dma_start(at[32 * i:32 * i + 32, j % 2, :, :],
                                 scores_d[4 * j + i].rearrange("k (y x) -> y k x", x=W)).then_inc(at_in[j % 2], 16)
                sp.wait_ge(sides, 32)
                for b in range(4 * j // HEADS, (4 * j + 3) // HEADS + 1):
                    sp.wait_ge(v_stored[b], 16 * HEADS)
                for i in range(4):
                    src = v_d[4 * j + i]
                    win = bass.AP(src.tensor, src.offset, [[V_ROW, H], [1, WIN * V_ROW]])
                    sp.dma_start(vw[32 * i:32 * i + 32, j % 2].rearrange("p r c x -> p (r c x)"), win)\
                        .then_inc(vw_in[j % 2], 16)

            def store_o(j):
                sp.wait_ge(normed, j + 1)
                for i in range(4):
                    sp.dma_start(o_d[4 * j + i].rearrange("c (y x) -> y c x", x=W), o_t[32 * i:32 * i + 32, :, :])\
                        .then_inc(o_stored, 16)

            def load_o(b):
                sp.wait_ge(o_stored, 64 * ((HEADS * b + HEADS - 1) // 4 + 1))
                if b:
                    sp.wait_ge(job_done, JOB["mlp", b - 1, 1])
                sp.dma_start(o[:, :], o_d[HEADS * b:HEADS * (b + 1)].rearrange("i c n -> (i c) n")).then_inc(o_in, 16)

            put_x4(0)
            put_x4(1)
            store_v(0)
            put_x4(2)
            for p in range(PAIRS):
                if p + 3 < PAIRS:
                    put_x4(p + 3)
                if p % 3 == 0 and p // 3 + 1 < B:
                    store_v(p // 3 + 1)
                if p % 2:
                    load_tile(p // 2)
                if p % 2 == 0 and p >= 4:
                    store_o(p // 2 - 2)
                    if O_AFTER.get(p // 2 - 2) == 0:
                        load_o(0)
            load_o(1)
            for j in range(TILES - 2, TILES):
                store_o(j)
                if j in O_AFTER:
                    load_o(O_AFTER[j])
            for b in range(B):
                for th in range(2):
                    left(sp, ("mlp", b, 8 + th))
                    sp.dma_start(t["out"][b][:, cols(th)], x1[:, b, cols(th)]).then_inc(out_s, 16)
            sp.wait_ge(out_s, 32 * B)
            sp.wait_ge(o_stored, 16 * IMAGES)

        @block.tensor
        def _(pe):
            def free(job):
                if job > G_BANKS:
                    left(pe, list(JOB)[job - G_BANKS - 1])

            def bank(job):
                return g_ps[:, job % G_BANKS, :]

            def qkv(b, i):
                n = JOB["qkv", b, i]
                free(n)
                m, th = i // 2, i % 2
                w = (slice(0, 128), slice(128, 192), slice(192, 288))[m]
                pe.matmul(bank(n)[0:w.stop - w.start, :], qkv_s[:, w], x1[:, b, cols(th)], start=True,
                          stop=True).then_inc(job_done, 1)

            def score(p):
                pe.wait_ge(x4_in[p % 3], 16 * 8 * (p // 3 + 1))
                for th in range(2):
                    if p >= 2:
                        pe.wait_ge(sc_out, 2 * (p - 2) + th + 1)
                    for dx in range(WIN):
                        for w, rows, y0 in ((w_up, 128, 0), (w_low, 96, 4)):
                            for i in range(2):
                                y = 16 * th + y0
                                mm = pe.matmul(sc_ps[64 * i:64 * i + 64, p % 2, th, :], w[:, dx, :],
                                               x4[0:rows, (2 * p + i) % X4_RING, y:y + 16, dx:dx + W],
                                               start=(dx == 0 and y0 == 0), stop=(dx == WIN - 1 and y0 == 4))
                    mm.then_inc(scored, 1)

            def mlp(b, i):
                n = JOB["mlp", b, i]
                free(n)
                if i < 2:
                    if i == 0:
                        pe.wait_ge(o_in, 16 * (b + 1))
                    pe.matmul(bank(n)[0:C, :], proj_w[:, :], o[:, cols(i)], start=True, stop=True)\
                        .then_inc(job_done, 1)
                elif i < 8:
                    m, th = (i - 2) % 3, (i - 2) // 3
                    left(pe, ("mlp", b, th))
                    pe.matmul(bank(n)[:, :], c1_w[:, 128 * m:128 * m + 128], x1[:, b, cols(th)], start=True,
                              stop=True).then_inc(job_done, 1)
                else:
                    th = i - 8
                    left(pe, ("mlp", b, 4 + 3 * th))
                    for m in range(3):
                        mm = pe.matmul(bank(n)[0:C, :], c2_w[:, m, :], up[:, m, cols(th)], start=(m == 0),
                                       stop=(m == 2))
                    mm.then_inc(job_done, 1)

            pe.wait_ge(loaded, 16 * L1_LOADS)
            pe.wait_ge(bn_step, BN_DONE)
            for m, w in enumerate((slice(0, 128), slice(128, 192), slice(192, 288))):
                n = JOB["bias", m]
                pe.matmul(bank(n)[0:w.stop - w.start, 0:1], qkv_w[:, w], bn_shift[:, :], start=True,
                          stop=True).then_inc(job_done, 1)
            for i in range(6):
                qkv(0, i)
            for p in range(PAIRS):
                if p % 3 == 0 and p // 3 + 1 < B:
                    for i in range(6):
                        qkv(p // 3 + 1, i)
                for m in MLP_AFTER.get(p, ()):
                    for i in range(10):
                        mlp(m, i)
                score(p)
            for m in MLP_LAST:
                for i in range(10):
                    mlp(m, i)

        @block.scalar
        def _(act):
            def qkv(b, i):
                n = JOB["qkv", b, i]
                m, th = i // 2, i % 2
                act.wait_ge(job_done, n)
                y0 = 16 * th
                rows = (128, 64, C)[m]
                src = g_ps[0:rows, n % G_BANKS, :].rearrange("p (y x) -> p y x", x=W)
                if m < 2:
                    if b >= 2 and i == 0:
                        for s in x4_in:
                            act.wait_ge(s, 16 * 8 * (b - 1))
                    dst = qk[0:rows, m, b % 2, R + y0:R + y0 + 16, R:R + W]
                else:
                    if b >= 2 and th == 0:
                        act.wait_ge(v_stored[b - 2], 16 * HEADS)
                    dst = v[:, b % 2, y0:y0 + 16, R:R + W]
                nc.scalar.activation(dst, src, ACT.Identity, bias=qkv_bias[0:rows, m:m + 1],
                                     scale=qkv_scale[0:rows, m:m + 1]).then_inc(left_act, 1)

            def store_scores(p):
                for th in range(2):
                    act.wait_ge(scored, 2 * p + th + 1)
                    if p >= 2 and th == 0:
                        act.wait_ge(sc_stored[p % 2], 32 * (p // 2))
                    nc.scalar.activation(sc[:, p % 2, cols(th)], sc_ps[:, p % 2, th, :], ACT.Identity,
                                         bias=rel[:, p % 3:p % 3 + 1]).then_inc(sc_out, 1)
                act.wait_ge(sc_out, 2 * p + 2)
                for i in range(2):
                    act.dma_start(scores_d[2 * p + i], sc[64 * i:64 * i + K2, p % 2, :]).then_inc(sc_stored[p % 2], 16)

            def exps(j):
                act.wait_ge(less, j + 1)
                nc.scalar.activation(at[:, j % 2], at[:, j % 2], ACT.Exp).then_inc(exped, 1)

            def mlp(b):
                for i in range(2, 8):
                    n = JOB["mlp", b, i]
                    m, th = (i - 2) % 3, (i - 2) // 3
                    act.wait_ge(job_done, n)
                    nc.scalar.activation(up[:, m, cols(th)], g_ps[:, n % G_BANKS, :], ACT.Gelu,
                                         bias=c1_b[:, m:m + 1]).then_inc(left_act, 1)

            act.wait_ge(bn_step, BN_VAR)
            nc.scalar.activation(bn_scale[:, :], bn_mv[:, 1:2], ACT.Sqrt, bias=bn[:, 2:3]).then_inc(bn_step, 1)
            act.wait_ge(bn_step, BN_BIAS)
            act.wait_ge(zeroed, ZEROED)
            for i in range(6):
                qkv(0, i)
            for p in range(PAIRS):
                if p % 3 == 0 and p // 3 + 1 < B:
                    for i in range(6):
                        qkv(p // 3 + 1, i)
                for m in MLP_AFTER.get(p, ()):
                    mlp(m)
                store_scores(p)
                if p % 2 == 0 and p:
                    exps(p // 2 - 1)
            exps(TILES - 1)
            for m in MLP_LAST:
                mlp(m)

        def product(engine, j, dy, prod):
            e = at[:, j % 2, WIN * dy:WIN * dy + WIN, :].unsqueeze(2).broadcast_to([128, WIN, HD, W])
            win = vw[:, j % 2, dy]
            shifted = bass.AP(win.tensor, win.offset, [list(win.ap[0]), [1, WIN], [HP, HD], [1, W]])
            return engine.tensor_tensor(prod[:, :, :, :], shifted, e, ALU.mult)

        def fold(engine, eng, s, base, prod, acc, first):
            for n, (lo, hi) in enumerate((((0, 3), (4, 7)), ((0, 2), (2, 4)), ((0, 1), (1, 2)))):
                eng.wait_ge(s, base + n)
                engine.tensor_tensor(prod[:, lo[0]:lo[1]], prod[:, lo[0]:lo[1]], prod[:, hi[0]:hi[1]],
                                     ALU.add).then_inc(s, 1)
            eng.wait_ge(s, base + 3)
            if first:
                engine.tensor_copy(acc[:, :, :], prod[:, 0]).then_inc(s, 1)
            else:
                engine.tensor_tensor(acc[:, :, :], acc[:, :, :], prod[:, 0], ALU.add).then_inc(s, 1)

        @block.gpsimd
        def _(pool):
            nc.gpsimd.memset(zeros[:, :], 0.0)
            nc.gpsimd.memset(qk[:, :, :, :, :], 0.0)
            nc.gpsimd.memset(v[:, :, :, :], 0.0).then_inc(zeroed, 1)
            for j in range(TILES):
                pool.wait_ge(soft, 3 * j + 1)
                pool.wait_ge(at_in[j % 2], 64 * (j // 2 + 1))
                nc.gpsimd.tensor_tensor(at[:, j % 2], at[:, j % 2],
                                        mx[:, :].unsqueeze(1).broadcast_to([128, K2, W]),
                                        ALU.subtract).then_inc(less, 1)
                pool.wait_ge(exped, j + 1)
                pool.wait_ge(vw_in[j % 2], 64 * (j // 2 + 1))
                for n, dy in enumerate(POOL_ROWS):
                    base = PP_STEPS * j + 5 * n
                    if n == 0 and j:
                        pool.wait_ge(normed, j)
                    if base:
                        pool.wait_ge(pp, base)
                    product(nc.gpsimd, j, dy, prod_p).then_inc(pp, 1)
                    fold(nc.gpsimd, pool, pp, base + 1, prod_p, acc_p, n == 0)

        @block.vector
        def _(dve):
            nc.vector.memset(w_up[:, :, :], 0.0)
            nc.vector.memset(w_low[:, :, :], 0.0)
            nc.vector.memset(rel[:, :], 0.0)
            nc.vector.memset(dm_b[:, :], 0.0)
            nc.vector.memset(bn[:, 2:3], BN_EPS).then_inc(zeroed, 1)
            for n in range(2 * B):
                nc.vector.bn_stats(bn_stats[:, n, :], x1[:, n // 2, cols(n % 2)]).then_inc(bn_step, 1)
            dve.wait_ge(bn_step, 2 * B)
            nc.vector.bn_aggr(bn_mv[:, :], bn_stats[:, :, :]).then_inc(bn_step, 1)
            dve.wait_ge(bn_step, BN_VAR + 1)
            nc.vector.reciprocal(bn_scale[:, :], bn_scale[:, :]).then_inc(bn_step, 1)
            dve.wait_ge(loaded, 16 * L1_LOADS)
            dve.wait_ge(bn_step, BN_VAR + 2)
            nc.vector.tensor_tensor(bn_scale[:, :], bn_scale[:, :], bn[:, 0:1], ALU.mult).then_inc(bn_step, 1)
            dve.wait_ge(bn_step, BN_VAR + 3)
            nc.vector.tensor_tensor(bn_shift[:, :], bn_mv[:, 0:1], bn_scale[:, :], ALU.mult).then_inc(bn_step, 1)
            dve.wait_ge(bn_step, BN_VAR + 4)
            nc.vector.tensor_tensor(bn_shift[:, :], bn[:, 1:2], bn_shift[:, :], ALU.subtract).then_inc(bn_step, 1)
            nc.vector.tensor_scalar(qkv_s[:, :], qkv_w[:, :], bn_scale[:, 0:1], None, ALU.mult).then_inc(bn_step, 1)
            nc.vector.tensor_scalar(rel[:, :], rel[:, :], dm_b[:, 0:1], None, ALU.add).then_inc(bn_step, 1)
            for m, rows in enumerate((128, 64, C)):
                n = JOB["bias", m]
                dve.wait_ge(job_done, n)
                nc.vector.scalar_tensor_tensor(out=qkv_bias[0:rows, m:m + 1], in0=g_ps[0:rows, n % G_BANKS, 0:1],
                                               scalar=qkv_b[0:rows, m:m + 1], in1=qkv_scale[0:rows, m:m + 1],
                                               op0=ALU.add, op1=ALU.mult).then_inc(left_dve, 1)
            dve.wait_ge(left_dve, 3)
            nc.vector.memset(mx[:, :], 0.0).then_inc(bn_step, 1)

            def mlp_out(b, i):
                n = JOB["mlp", b, i]
                bias = proj_b if i < 2 else c2_b
                dve.wait_ge(job_done, n)
                if i >= 8:
                    left(dve, ("mlp", b, i - 8))
                nc.vector.scalar_tensor_tensor(out=x1[:, b, cols(i % 2)], in0=g_ps[0:C, n % G_BANKS, :],
                                               scalar=bias[:, 0:1], in1=x1[:, b, cols(i % 2)],
                                               op0=ALU.add, op1=ALU.add).then_inc(left_dve, 1)

            def maximum(j):
                dve.wait_ge(at_in[j % 2], 64 * (j // 2 + 1))
                if j:
                    dve.wait_ge(less, j)
                nc.vector.tensor_reduce(mx[:, :], at[:, j % 2].rearrange("p k x -> p x k"), AX.X, ALU.max)\
                    .then_inc(soft, 1)

            def tile(j):
                dve.wait_ge(exped, j + 1)
                nc.vector.tensor_reduce(den[:, 0, :], at[:, j % 2].rearrange("p k x -> p x k"), AX.X, ALU.add)\
                    .then_inc(soft, 1)
                dve.wait_ge(soft, 3 * j + 2)
                nc.vector.reciprocal(den[:, 1, :], den[:, 0, :]).then_inc(soft, 1)
                dve.wait_ge(vw_in[j % 2], 64 * (j // 2 + 1))
                for n, dy in enumerate(DVE_ROWS):
                    base = PV_STEPS * j + 5 * n
                    if n == len(DVE_ROWS) - 1 and j + 1 < TILES:
                        maximum(j + 1)
                    for m, i in DVE_MLP.get((j, n), ()):
                        mlp_out(m, i)
                        mlp_out(m, i + 1)
                    if base:
                        dve.wait_ge(pv, base)
                    product(nc.vector, j, dy, prod_v).then_inc(pv, 1)
                    fold(nc.vector, dve, pv, base + 1, prod_v, acc_v, n == 0)
                base = PV_STEPS * j + 5 * len(DVE_ROWS)
                dve.wait_ge(pv, base)
                dve.wait_ge(pp, PP_STEPS * (j + 1))
                nc.vector.tensor_tensor(acc_v[:, :, :], acc_v[:, :, :], acc_p[:, :, :], ALU.add).then_inc(pv, 1)
                dve.wait_ge(pv, base + 1)
                dve.wait_ge(soft, 3 * j + 3)
                if j:
                    dve.wait_ge(o_stored, 64 * j)
                nc.vector.tensor_tensor(o_t[:, :, :], acc_v[:, :, :],
                                        den[:, 1, :].unsqueeze(1).broadcast_to([128, HD, W]),
                                        ALU.mult).then_inc(normed, 1)

            maximum(0)
            for j in range(TILES):
                tile(j)
            for i in (0, 1, 8, 9):
                mlp_out(B - 1, i)



def parts_in_dram(nc):
    return [tuple(nc.dram_tensor(f"{n}_{m}", (PARTS, c, L), BF16, kind="Internal").ap()
                  for m, c in (("low", E_LO), ("high", E_HI))) for n in ("dt", "u")]


def program(nc, t):
    scratch = (nc.dram_tensor("scores_d", (IMAGES, K2, L), F32, kind="Internal").ap(),
               nc.dram_tensor("v_d", (IMAGES, HP, HD, HP), F32, kind="Internal").ap(),
               nc.dram_tensor("o_d", (IMAGES, HD, L), F32, kind="Internal").ap())
    with nc.sbuf_tensor("x1", [C, B, L], F32) as x1:
        mamba(nc, t, x1, *parts_in_dram(nc))
        attention(nc, t, x1, scratch)


def constants():
    center = np.stack([np.eye(C) - 1.0 / C, np.full((C, C), 1.0 / C)], 1)
    rep = np.zeros((PARTS, 32, 4, GE, N_ST))
    pick = np.zeros((GE, N_ST, 8, 32))
    for e in range(GE):
        for q in range(4):
            rep[:, GE * q + e, q, e, :] = 1.0
            pick[e, :, q, 4 * e + q] = 1.0
            pick[e, :, 4 + q, 16 * (q % 2) + 2 * e + q // 2] = 1.0
    q_scale = np.ones((128, 3))
    q_scale[:, 0:2] = np.tile(np.repeat([HD ** -0.5, 1.0], HD), 4)[:, None]
    return {"center": center, "rep": rep.reshape(PARTS * 32, 4, 128), "pick": pick.reshape(128, 8, 32),
            "qkv_scale": q_scale}


def by_unit(v):
    low = v[:E_LO].reshape(4, GE, 4, N_ST).transpose(1, 3, 2, 0).reshape(128, 16)
    high = v[E_LO:].reshape(4, GE, 2, N_ST).transpose(1, 3, 2, 0).reshape(128, 8)
    return np.concatenate([low, high], 1)


def kernel(**inputs):
    import concourse.bacc as _bacc
    from concourse.bass_utils import run_bass_kernel_spmd as _run

    g = {k.replace("L0_conv_", "").replace("L1_conv_", ""): np.asarray(v) for k, v in inputs.items()}

    def col(v):
        return v.reshape(-1, 1)

    order = [s * C + hd * HD + c for hd in range(HEADS) for s in range(2) for c in range(HD)] + \
        list(range(2 * C, 3 * C))
    arrays = {
        "x": g["x"].reshape(B, C, L), "gamma": col(g["gamma"]), "beta": col(g["beta"]), "W_in": g["W_in"],
        "conv_w": g["conv_w"].T.reshape(1, TAPS * E_IN), "conv_b": col(g["conv_b"]), "W_xproj": g["W_xproj"],
        "W_dt": g["W_dt"], "b_dt": col(g["b_dt"]), "D": col(g["D"]), "W_out": g["W_out"],
        "A_log": by_unit(g["A_log"]),
        "bn_gamma": col(g["bn_gamma"]), "bn_beta": col(g["bn_beta"]),
        "qkv_w": g["qkv_w"][order].T, "qkv_b": col(g["qkv_b"][order]),
        "dm_w": g["dm_w"].transpose(2, 1, 3, 0).reshape(WIN * 2 * HD, WIN, K2), "dm_b": col(g["dm_b"]),
        "rel_bias": g["rel_bias"], "proj_w": g["proj_w"].T, "proj_b": col(g["proj_b"]),
        "c1_w": g["c1_w"].T, "c1_b": g["c1_b"].reshape(3, 128).T,
        "c2_w": g["c2_w"].T.reshape(3, 128, C).transpose(1, 0, 2), "c2_b": col(g["c2_b"]),
    }
    arrays.update({k: v.astype(np.float32) for k, v in constants().items()})
    nc = _bacc.Bacc("TRN2", target_bir_lowering=False, num_devices=1)
    t, feed = {}, {}
    for name, v in arrays.items():
        v = np.ascontiguousarray(v)
        feed[f"in_{name}"] = v
        t[name] = nc.dram_tensor(f"in_{name}", v.shape, F32, kind="ExternalInput").ap()
    t["out"] = nc.dram_tensor("out_x", (B, C, L), F32, kind="ExternalOutput").ap()
    program(nc, t)
    r = _run(nc, [feed], core_ids=[0])
    return r.results[0]["out_x"].reshape(B, C, H, W)
```

```python
from contextlib import ExitStack

import concourse.bass as bass
from concourse import mybir
import numpy as np

F32 = mybir.dt.float32
BF16 = mybir.dt.bfloat16
ALU = mybir.AluOpType
ACT = mybir.ActivationFunctionType
AX = mybir.AxisListType

B, C, H, W = 4, 96, 32, 32
L = H * W
HALF = L // 2
E_IN, N_ST, RANK, TAPS = 192, 16, 6, 4
PAD = TAPS - 1
E_LO, E_HI = 128, E_IN - 128
GE = 128 // N_ST
UNITS = E_IN // GE
QUADS = UNITS // 4
PHASES = 2 * B
SPAN = L + HALF
PARTS = 3
LN_EPS = 1e-5

A_RING, H_RING, HC_RING, ST_RING, U_BANKS, D_BANKS = 4, 3, 8, 8, 3, 2
HS = 2 * UNITS
ACT_AHEAD = 2
DT_LEAD, EXP_LEAD = 5, 5
XP = RANK + 2 * N_ST
SUM_AT = 16
CONV_AT, Z_AT, XP_AT, DT_AT = (0, 4, 10), (15, 26, 27), 17, (20, 22, 24)
LN_AT, OUT_AT = (30, 32, 33, 35), (38, 42)
SILU_AT = 16
EXP_AT, ONE_AT, LOG_AT, LOST_AT, LESS_AT, MAX_AT = 26, 25, 29, 28, 26, 30
U_AT = 30
DH_AT, DR_AT, DM_AT, DL_AT = 32, 32, 35, 34
UH_AT, UR_AT, UM_AT, UL_AT = 37, 37, 39, 39
Y0_AT, Y1_AT = 42, 10
LOADS = [4, 6, 10, 9]
SETUP = 5

HEADS, HD, WIN = 6, 16, 7
K2 = WIN * WIN
R = WIN // 2
HP = H + 2 * R
V_ROW = HD * HP
IMAGES = B * HEADS
PAIRS = IMAGES // 2
TILES = IMAGES // 4
X4_ROWS = H + 4
X4_RING = 6
G_BANKS = 4
BN_EPS = 1e-5
BN_VAR, BN_DONE = 2 * B + 1, 2 * B + 7
L1_LOADS = [7, 12]
DVE_ROWS = (5, 5, 5, 5, 5, 4)
DVE_MLP = {(4, 4): ((0, 0),), (5, 0): ((0, 8),), (5, 1): ((1, 0),), (5, 2): ((1, 8), (2, 0)), (5, 3): ((2, 8),)}
LAST_TILE = [(HEADS * b + HEADS - 1) // 4 for b in range(B)]


def halves(direction):
    return (0, 1) if direction == 0 else (1, 0)


def scan_order(ap, direction):
    return ap if direction == 0 else ap[:, ::-1]


def cols(th, n=HALF):
    return slice(th * n, (th + 1) * n)


def mamba(nc, t, x1, dt_d, u_d):
    with ExitStack() as ctx:
        def sb(name, shape, dt=F32):
            return ctx.enter_context(nc.sbuf_tensor(name, shape, dt))

        def ps(name, shape):
            return ctx.enter_context(nc.psum_tensor(name, shape, F32))

        def sem(name):
            return ctx.enter_context(nc.semaphore(name))

        w_z = sb("w_z", [C, E_IN])
        w_taps = sb("w_taps", [C, TAPS, E_IN])
        w_x = sb("w_x", [128, 2, XP])
        w_dt = sb("w_dt", [RANK, E_IN])
        w_out = sb("w_out", [128, 2, C])
        a_neg = sb("a_neg", [128, UNITS])
        conv_b, b_dt, d_skip = (sb(n, [128, 2]) for n in ("conv_b", "b_dt", "d_skip"))
        norm = sb("norm", [C, 3])
        center = sb("center", [C, 2, C])
        rep = sb("rep", [PARTS * 32, 4, 128], BF16)
        pick = sb("pick", [128, 8, 32])
        xn = sb("xn", [C, PAD + L + PAD])
        xi = xn[:, PAD:PAD + L]
        var = sb("var", [C, L])
        t01 = sb("t01", [128, 2 * SPAN])
        t0, t1 = t01[:, 0:SPAN], t01[:, SPAN:2 * SPAN]
        u_parts = t01[:, 0:PARTS * SPAN // 2].bitcast(BF16).rearrange("p (a s) -> p a s", a=PARTS)
        t2, t3, t4 = (sb(f"t{i}", [128, SPAN]) for i in (2, 3, 4))
        conv_w_rows = t2[0:C, 0:TAPS * E_IN].rearrange("p (j e) -> p j e", j=TAPS)
        w_in = t2[0:C, TAPS * E_IN:(TAPS + 1) * E_IN]
        rep_f = t3[0:PARTS * 32, 0:4 * 128].rearrange("p (q m) -> p q m", q=4)
        dbc = sb("dbc", [XP, L])
        xr = sb("xr", [128, 2, SPAN])
        z = sb("z", [128, SPAN])
        y = sb("y", [128, SPAN])
        dt_parts = sb("dt_parts", [128, PARTS, SPAN], BF16)
        dt_st = sb("dt_st", [PARTS * 32, ST_RING, L], BF16)
        u_st = sb("u_st", [PARTS * 32, ST_RING, L], BF16)
        b_rep = sb("b_rep", [128, 2, L])
        c_rep = sb("c_rep", [128, 2, L])
        a = sb("a", [128, A_RING, L])
        h = sb("h", [128, H_RING, L])
        hc = sb("hc", [128, HC_RING, L])
        dt_ps = ps("dt_ps", [128, D_BANKS, HALF])
        u_ps = ps("u_ps", [128, U_BANKS, HALF])
        y_ps = ps("y_ps", [128, 2, HALF])
        f_ps = ps("f_ps", [128, HALF])

        loaded = [sem(f"loaded{i}") for i in range(4)]
        set_up = sem("set_up")
        a_exp = sem("a_exp")
        job_done = sem("job_done")
        job_read = sem("job_read")
        act_step = sem("act_step")
        act_ln = sem("act_ln")
        normalised = sem("normalised")
        pool_step = sem("pool_step")
        dve_step = sem("dve_step")
        dt_out = sem("dt_out")
        u_out = sem("u_out")
        dt_stacked = [sem(f"dt_stacked{i}") for i in range(2)]
        u_stacked = [sem(f"u_stacked{i}") for i in range(2)]
        b_in = sem("b_in")
        c_in = sem("c_in")
        dt_spread = sem("dt_spread")
        u_spread = sem("u_spread")
        exp_done = sem("exp_done")
        bu_done = sem("bu_done")
        scanned = sem("scanned")
        hc_done = sem("hc_done")
        summed = sem("summed")
        z_ready = sem("z_ready")
        y_read = sem("y_read")
        y_step = sem("y_step")

        block = ctx.enter_context(nc.Block())

        def ran(phase, k):
            return UNITS * phase + k

        def count(phase, name, seq_of):
            return sum(len(seq_of(p)) for p in range(phase)) + seq_of(phase).index(name) + 1

        def jobs(p):
            first = ["cen0", "cen1", "var0", "var1"] if p == 0 else []
            if p % 2 == 0:
                return first + ["conv0", "conv1", "conv2", "xp", "dt0", "dt1", "dt2"]
            return ["conv0", "conv1", "conv2", "z0", "xp", "dt0", "dt1", "dt2", "z1", "z2"] + \
                (["cen0", "cen1", "var0", "var1"] if p + 1 < PHASES else []) + \
                (["out0", "out1"] if p > 1 else [])

        def act_steps(p):
            return ["xr", "e", "ln", "dh", "dm", "uh", "um"]

        def pool_steps(p):
            return ["y1", "l", "u"]

        def dve_steps(p):
            return ["c", "dt", "dr", "dl", "ur", "ul"]

        def J(p, name):
            return count(p, name, jobs)

        def A(p, name):
            return count(p, name, act_steps)

        def P(p, name):
            return count(p, name, pool_steps)

        def V(p, name):
            return count(p, name, dve_steps)

        def ln_front(b):
            return max(2 * b - 1, 0)

        def bank(p, name):
            n = J(p, name)
            return (f_ps[:, :], y_ps[:, 0, :], y_ps[:, 1, :])[n % 3] if n <= len(jobs(0)) else f_ps[:, :]

        ALL_JOBS = J(PHASES - 1, "out1")
        PARTS_OUT = 16 * PARTS * 2
        STACK = (16, 32)
        SPREAD = 16 * GE

        @block.sync
        def _(sp):
            def both(column, name):
                return [(column[:, 0:1], t[name][0:E_LO]), (column[0:E_HI, 1:2], t[name][E_LO:E_IN]),
                        (column[E_HI:128, 1:2], t[name][E_LO:E_IN])]

            groups = [
                [(x1[:, 0, :], t["x"][0]), (center[:, :, :], t["center"]), (norm[:, 0:1], t["gamma"]),
                 (norm[:, 1:2], t["beta"])],
                [(conv_w_rows.rearrange("p j e -> p (j e)"), t["conv_w"].to_broadcast([C, TAPS * E_IN])),
                 (w_in, t["W_in"][:, 0:E_IN]),
                 (w_z[:, :], t["W_in"][:, E_IN:])] + both(conv_b, "conv_b"),
                [(w_x[:, 0, :], t["W_xproj"][0:E_LO]), (w_x[0:E_HI, 1, :], t["W_xproj"][E_LO:E_IN]),
                 (w_x[E_HI:128, 1, :], t["W_xproj"][E_LO:E_IN]), (w_dt[:, :], t["W_dt"]),
                 (rep_f, t["rep"]), (pick[:, :, :], t["pick"]), (a_neg[:, :], t["A_log"])] + both(b_dt, "b_dt"),
                [(w_out[:, 0, :], t["W_out"][0:E_LO]), (w_out[0:E_HI, 1, :], t["W_out"][E_LO:E_IN]),
                 (w_out[E_HI:128, 1, :], t["W_out"][E_LO:E_IN])] + both(d_skip, "D") +
                [(x1[:, b, :], t["x"][b]) for b in range(1, B)],
            ]
            assert [len(g) for g in groups] == LOADS
            for group, done in zip(groups, loaded):
                for dst, src in group:
                    sp.dma_start(dst, src).then_inc(done, 16)

            def store(ph, parts, part, dram, done):
                low, high = dram
                sp.dma_start(low[part], parts[:, part, 0:L]).then_inc(done, 16)
                sp.dma_start(high[part].rearrange("c (h l) -> h c l", h=2), parts[:, part, L:SPAN])\
                    .then_inc(done, 16)

            def stack(ph, dst, dram, done):
                low = dram[0].rearrange("a (r s) l -> (a r) s l", s=4)
                high = dram[1].rearrange("a (r s) l -> (a r) s l", s=2)
                for s in (0, 2):
                    at = (6 * ph + s) % ST_RING
                    sp.dma_start(dst[:, at:at + 2, :], low[:, s:s + 2, :]).then_inc(done[s // 2], 16)
                at = (6 * ph + 4) % ST_RING
                sp.dma_start(dst[:, at:at + 2, :], high).then_inc(done[1], 16)

            for ph in range(PHASES):
                sp.wait_ge(job_read, J(ph, "xp"))
                for dst, row, done in ((b_rep, RANK, b_in), (c_rep, RANK + N_ST, c_in)):
                    if ph >= 2:
                        if dst is b_rep:
                            sp.wait_ge(bu_done, 2 * ran(ph - 1, 0))
                        else:
                            sp.wait_ge(hc_done, ran(ph - 1, 0))
                    for e in range(GE):
                        sp.dma_start(dst[N_ST * e:N_ST * (e + 1), ph % 2, :], dbc[row:row + N_ST, :])\
                            .then_inc(done, 16)
                if ph >= 1:
                    sp.wait_ge(u_spread, 2 * ran(ph - 1, 16))
                for dst, parts, dram, stored, done, steps in (
                    (dt_st, dt_parts, dt_d, dt_out, dt_stacked,
                     ((act_step, A(ph, "dh")), (act_step, A(ph, "dm")), (dve_step, V(ph, "dl")))),
                    (u_st, u_parts, u_d, u_out, u_stacked,
                     ((act_step, A(ph, "uh")), (act_step, A(ph, "um")), (dve_step, V(ph, "ul")))),
                ):
                    if ph:
                        for i in range(2):
                            sp.wait_ge(done[i], STACK[i] * ph)
                    for part, (made, at) in enumerate(steps):
                        sp.wait_ge(made, at)
                        store(ph, parts, part, dram, stored)
                    sp.wait_ge(stored, PARTS_OUT * (ph + 1))
                    stack(ph, dst, dram, done)

        @block.tensor
        def _(pe):
            def free(job):
                back = 3 if job <= len(jobs(0)) else 1
                if job > back:
                    pe.wait_ge(job_read, job - back)

            def out_job(b, th, part):
                if part == 0:
                    pe.wait_ge(y_step, 3 * b + 3)
                    pe.matmul(f_ps[0:C, :], w_out[:, 0, :], y[:, cols(th)], start=True, stop=False)
                else:
                    p = E_HI * th
                    pe.matmul(f_ps[0:C, :], w_out[p:p + E_HI, 1, :], y[p:p + E_HI, L:SPAN], start=False,
                              stop=True).then_inc(job_done, 1)

            def layer_norm(b, step):
                ph, th = ln_front(b), step % 2
                name = ("cen", "var")[step // 2] + str(th)
                ln_ps = bank(ph, name)
                free(J(ph, name))
                if step < 2:
                    pe.matmul(ln_ps[0:C, :], center[:, 0, :], x1[:, b, cols(th)], start=True,
                              stop=True).then_inc(job_done, 1)
                else:
                    pe.wait_ge(act_ln, 5 * b + th + 1)
                    pe.matmul(ln_ps[0:C, :], center[:, 1, :], var[:, cols(th)], start=True,
                              stop=True).then_inc(job_done, 1)

            def front(ph, hs):
                d, b = ph % 2, ph // 2
                shifts = [2 * PAD - j if d else j for j in range(TAPS)]
                for job, at in enumerate(CONV_AT):
                    j = hs - at
                    if not 0 <= j < TAPS:
                        continue
                    conv_ps = bank(ph, f"conv{job}")
                    if j == 0:
                        free(J(ph, f"conv{job}"))
                        if job == 0:
                            pe.wait_ge(act_ln, 5 * b + 5)
                    for th in ((job,) if job < 2 else (0, 1)):
                        s = shifts[j] + th * HALF
                        out, w = (conv_ps, w_taps[:, j, 0:E_LO]) if job < 2 else \
                            (conv_ps[E_HI * th:E_HI * (th + 1), :], w_taps[:, j, E_LO:E_IN])
                        mm = pe.matmul(out, w, xn[:, s:s + HALF], start=(j == 0), stop=(j == TAPS - 1))
                    if j == TAPS - 1:
                        mm.then_inc(job_done, 1)
                if d == 1 and hs in Z_AT[:2]:
                    th = Z_AT.index(hs)
                    free(J(ph, f"z{th}"))
                    pe.matmul(f_ps[:, :], w_z[:, 0:E_LO], xi[:, cols(th)],
                              start=True, stop=True).then_inc(job_done, 1)
                if d == 1 and hs == Z_AT[2]:
                    free(J(ph, "z2"))
                    for th in range(2):
                        mm = pe.matmul(f_ps[E_HI * th:E_HI * (th + 1), :], w_z[:, E_LO:E_IN],
                                       xi[:, cols(th)], start=True, stop=True)
                    mm.then_inc(job_done, 1)
                if hs == XP_AT:
                    free(J(ph, "xp"))
                    pe.wait_ge(act_step, A(ph, "xr"))
                    for th in range(2):
                        pe.matmul(bank(ph, "xp")[64 * th:64 * th + XP, :], w_x[:, 0, :], xr[:, d, cols(th)],
                                  start=True, stop=False)
                if hs == XP_AT + 1:
                    for th in range(2):
                        p = E_HI * th
                        mm = pe.matmul(bank(ph, "xp")[64 * th:64 * th + XP, :], w_x[p:p + E_HI, 1, :],
                                       xr[p:p + E_HI, d, L:SPAN], start=False, stop=True)
                    mm.then_inc(job_done, 1)
                if hs in DT_AT[:2]:
                    th = DT_AT.index(hs)
                    free(J(ph, f"dt{th}"))
                    pe.wait_ge(job_read, J(ph, "xp"))
                    pe.matmul(bank(ph, f"dt{th}"), w_dt[:, 0:E_LO], dbc[0:RANK, cols(th)], start=True,
                              stop=True).then_inc(job_done, 1)
                if hs == DT_AT[2]:
                    free(J(ph, "dt2"))
                    for th in range(2):
                        mm = pe.matmul(bank(ph, "dt2")[E_HI * th:E_HI * (th + 1), :], w_dt[:, E_LO:E_IN],
                                       dbc[0:RANK, cols(th)], start=True, stop=True)
                    mm.then_inc(job_done, 1)
                if d == 1 and b + 1 < B and hs in LN_AT:
                    layer_norm(b + 1, LN_AT.index(hs))
                for th, at in enumerate(OUT_AT):
                    if d == 1 and b > 0 and hs in (at, at + 1):
                        if hs == at:
                            free(J(ph, f"out{th}"))
                        out_job(b - 1, th, hs - at)

            def spread_dt(n):
                ph, hs = n // HS, n % HS
                if ph == PHASES:
                    return
                if hs in (0, 16):
                    pe.wait_ge(dt_stacked[hs // 16], STACK[hs // 16] * (ph + 1))
                if n >= D_BANKS:
                    pe.wait_ge(exp_done, n - D_BANKS + 1)
                pe.matmul(dt_ps[:, n % D_BANKS, :], rep[:, hs // 2 % 4, :],
                          dt_st[:, (6 * ph + hs // 8) % ST_RING, cols(halves(ph % 2)[hs % 2])],
                          start=True, stop=True).then_inc(dt_spread, 1)

            def spread_u(n):
                ph, hs = n // HS, n % HS
                if hs in (0, 16):
                    pe.wait_ge(u_stacked[hs // 16], STACK[hs // 16] * (ph + 1))
                if n >= U_BANKS:
                    pe.wait_ge(scanned, n - U_BANKS + 1)
                pe.matmul(u_ps[:, n % U_BANKS, :], rep[:, hs // 2 % 4, :],
                          u_st[:, (6 * ph + hs // 8) % ST_RING, cols(halves(ph % 2)[hs % 2])],
                          start=True, stop=True).then_inc(u_spread, 1)

            def sum_states(q, part):
                ph, m = q // QUADS, q % QUADS
                y_tile = 2 * ph + (m >= 4)
                if part == 0:
                    pe.wait_ge(hc_done, 4 * q + 4)
                    if m in (0, 4) and y_tile:
                        pe.wait_ge(y_read, y_tile)
                for i in range(4):
                    if m < 4:
                        u, th, v = i, part, m
                        out, first, last = y_ps[32 * u:32 * u + 32, th, :], m == 0, m == 3
                    else:
                        u, th = 2 * (i % 2) + part, i // 2
                        v = 4 + 2 * (m - 4) + u % 2
                        p = 32 * (u // 2) + E_HI * th
                        out, first, last = y_ps[p:p + 32, 0, :], m == 4 and part == 0, m == 5 and part == 1
                    mm = pe.matmul(out, pick[:, v, :], hc[:, (4 * q + u) % HC_RING, cols(th)],
                                   start=first, stop=last)
                if part:
                    mm.then_inc(summed, 1)

            pe.wait_ge(loaded[0], 16 * LOADS[0])
            for step in range(4):
                layer_norm(0, step)
            pe.wait_ge(loaded[1], 16 * LOADS[1])
            pe.wait_ge(set_up, 3)
            for hs in range(HS):
                if hs == XP_AT:
                    pe.wait_ge(loaded[2], 16 * LOADS[2])
                front(0, hs)
            pe.wait_ge(set_up, SETUP)
            pe.wait_ge(loaded[3], 16 * LOADS[3])
            for n in range(DT_LEAD):
                spread_dt(n)
            for ph in range(PHASES):
                for hs in range(HS):
                    n = HS * ph + hs
                    spread_u(n)
                    q, part = divmod(n - SUM_AT, 8)
                    if q >= 0 and part < 2:
                        sum_states(q, part)
                    if ph + 1 < PHASES:
                        front(ph + 1, hs)
                    spread_dt(n + DT_LEAD)
            for q in range(-(-(HS * PHASES - SUM_AT) // 8), QUADS * PHASES):
                for part in range(2):
                    sum_states(q, part)
            for th in range(2):
                free(ALL_JOBS + th + 1)
                for part in range(2):
                    out_job(B - 1, th, part)

        @block.scalar
        def _(act):
            def leave(ph, job, out, src, func=ACT.Identity, **kw):
                act.wait_ge(job_done, J(ph, job))
                nc.scalar.activation(out, src, func, **kw).then_inc(job_read, 1)

            def layer_norm(b, step):
                ph, th = ln_front(b), step % 2
                if step < 2:
                    if step == 0 and b:
                        act.wait_ge(job_done, J(ph, "z2"))
                    leave(ph, f"cen{th}", xi[:, cols(th)], bank(ph, f"cen{th}")[0:C, :])
                    act.wait_ge(job_read, J(ph, f"cen{th}"))
                    nc.scalar.activation(var[:, cols(th)], xi[:, cols(th)], ACT.Square).then_inc(act_ln, 1)
                elif step < 4:
                    leave(ph, f"var{th}", var[:, cols(th)], bank(ph, f"var{th}")[0:C, :])
                elif step == 4:
                    act.wait_ge(job_read, J(ph, "var1"))
                    nc.scalar.activation(var[:, :], var[:, :], ACT.Ln, bias=norm[:, 2:3]).then_inc(act_ln, 1)
                    act.wait_ge(act_ln, 5 * b + 3)
                    nc.scalar.activation(var[:, :], var[:, :], ACT.Exp, scale=-0.5).then_inc(act_ln, 1)
                else:
                    act.wait_ge(normalised, b + 1)
                    nc.scalar.activation(xi, xi, ACT.Identity, scale=norm[:, 0:1], bias=norm[:, 1:2])\
                        .then_inc(act_ln, 1)

            def front(ph, hs):
                d, b = ph % 2, ph // 2
                for th in range(2):
                    if hs == CONV_AT[th] + TAPS:
                        if th == 0 and ph:
                            act.wait_ge(pool_step, P(ph - 1, "u"))
                            act.wait_ge(dve_step, V(ph - 1, "ul"))
                        leave(ph, f"conv{th}", t3[:, cols(th)], bank(ph, f"conv{th}"), bias=conv_b[:, 0:1])
                if hs == CONV_AT[2] + TAPS:
                    leave(ph, "conv2", t3[:, L:SPAN], bank(ph, "conv2"), bias=conv_b[:, 1:2])
                if hs == SILU_AT:
                    if ph >= 2 and d == 0:
                        act.wait_ge(y_read, 2 * ph - 2)
                    if ph >= 2 and d == 1:
                        act.wait_ge(y_step, 3 * (b - 1) + 2)
                    act.wait_ge(job_read, J(ph, "conv2"))
                    nc.scalar.activation(xr[:, d, :], t3[:, :], ACT.Silu).then_inc(act_step, 1)
                if d == 1 and hs - 1 in Z_AT[:2]:
                    th = Z_AT.index(hs - 1)
                    if b and not th:
                        act.wait_ge(y_step, 3 * b)
                    leave(ph, f"z{th}", z[:, cols(th)], f_ps[:, :])
                if d == 1 and hs == Z_AT[2] + 1:
                    leave(ph, "z2", z[:, L:SPAN], f_ps[:, :])
                if hs == XP_AT + 2:
                    if ph:
                        act.wait_ge(b_in, SPREAD * ph)
                        act.wait_ge(c_in, SPREAD * ph)
                    act.wait_ge(job_done, J(ph, "xp"))
                    nc.scalar.activation(dbc[:, cols(0)], bank(ph, "xp")[0:XP, :], ACT.Copy)
                    nc.scalar.activation(dbc[:, cols(1)], bank(ph, "xp")[64:64 + XP, :], ACT.Copy).then_inc(job_read, 1)
                if hs - 1 in DT_AT:
                    job = DT_AT.index(hs - 1)
                    to = cols(job)
                    tile = job // 2
                    act.wait_ge(job_done, J(ph, f"dt{job}"))
                    nc.scalar.activation(t2[:, to], bank(ph, f"dt{job}"), ACT.Identity, bias=b_dt[:, tile:tile + 1])
                    nc.scalar.activation(t3[:, to], bank(ph, f"dt{job}"), ACT.Abs, bias=b_dt[:, tile:tile + 1])\
                        .then_inc(job_read, 1)
                if hs == EXP_AT:
                    act.wait_ge(job_read, J(ph, "dt2"))
                    nc.scalar.activation(t4[:, :], t3[:, :], ACT.Exp, scale=-1.0).then_inc(act_step, 1)
                if hs == LOG_AT:
                    if ph:
                        act.wait_ge(u_out, PARTS_OUT * ph)
                    act.wait_ge(pool_step, P(ph, "y1"))
                    nc.scalar.activation(t1[:, :], t3[:, :], ACT.Ln).then_inc(act_step, 1)
                if hs == DH_AT:
                    if ph:
                        act.wait_ge(dt_out, PARTS_OUT * ph)
                    act.wait_ge(dve_step, V(ph, "dt"))
                    nc.scalar.activation(dt_parts[:, 0, :], t2[:, :], ACT.Copy).then_inc(act_step, 1)
                if hs == DM_AT:
                    act.wait_ge(dve_step, V(ph, "dr"))
                    nc.scalar.activation(dt_parts[:, 1, :], t4[:, :], ACT.Copy).then_inc(act_step, 1)
                if hs == UH_AT:
                    act.wait_ge(pool_step, P(ph, "u"))
                    act.wait_ge(dve_step, V(ph, "dt"))
                    nc.scalar.activation(u_parts[:, 0, :], t3[:, :], ACT.Copy).then_inc(act_step, 1)
                if hs == UM_AT:
                    act.wait_ge(dve_step, V(ph, "ur"))
                    nc.scalar.activation(u_parts[:, 1, :], t2[:, :], ACT.Copy).then_inc(act_step, 1)
                steps = [at + 1 for at in LN_AT] + [LN_AT[3] + 2, LN_AT[3] + 6]
                if d == 1 and b + 1 < B and hs in steps:
                    layer_norm(b + 1, steps.index(hs))

            def decay(n):
                ph, hs = n // HS, n % HS
                if ph == PHASES:
                    return
                k, th = n // 2, halves(ph % 2)[hs % 2]
                unit = hs // 2
                act.wait_ge(dt_spread, n + 1)
                if hs % 2 == 0 and k >= A_RING:
                    act.wait_ge(scanned, 2 * (k - A_RING + 1))
                nc.scalar.activation(a[:, k % A_RING, cols(th)], dt_ps[:, n % D_BANKS, :], ACT.Exp,
                                     scale=a_neg[:, unit:unit + 1]).then_inc(exp_done, 1)

            act.wait_ge(loaded[0], 16 * LOADS[0])
            act.wait_ge(set_up, 1)
            for step in range(6):
                layer_norm(0, step)
            act.wait_ge(loaded[1], 16 * LOADS[1])
            act.wait_ge(loaded[2], 16 * LOADS[2])
            nc.scalar.activation(a_neg[:, :], a_neg[:, :], ACT.Exp).then_inc(a_exp, 1)
            act.wait_ge(set_up, SETUP)
            for hs in range(HS):
                front(0, hs)
            for n in range(EXP_LEAD):
                decay(n)
            for ph in range(PHASES):
                for hs in range(HS):
                    decay(HS * ph + hs + EXP_LEAD)
                    if ph + 1 < PHASES:
                        front(ph + 1, hs + ACT_AHEAD)
                    if ph % 2 and hs + ACT_AHEAD == SILU_AT:
                        act.wait_ge(job_read, J(ph, "z2"))
                        nc.scalar.activation(z[:, :], z[:, :], ACT.Silu).then_inc(z_ready, 1)

        def layer_norm_scale(engine, eng, b):
            eng.wait_ge(act_ln, 5 * b + 4)
            engine.tensor_tensor(xi, xi, var[:, :], ALU.mult).then_inc(normalised, 1)

        def log_corrected(engine, eng, ph):
            eng.wait_ge(act_step, A(ph, "ln"))
            eng.wait_ge(dve_step, V(ph, "c"))
            engine.tensor_tensor(t1[:, :], t1[:, :], t4[:, :], ALU.subtract).then_inc(pool_step, 1)

        def dt_times_x(engine, eng, ph):
            eng.wait_ge(dve_step, V(ph, "dt"))
            engine.tensor_tensor(t3[:, :], t2[:, :], xr[:, ph % 2, :], ALU.mult).then_inc(pool_step, 1)

        @block.gpsimd
        def _(pool):
            def front(ph, hs):
                d, b = ph % 2, ph // 2
                if hs == ONE_AT:
                    pool.wait_ge(act_step, A(ph, "e"))
                    nc.gpsimd.tensor_scalar(t3[:, :], t4[:, :], 1.0, 1.0, ALU.mult, ALU.add).then_inc(pool_step, 1)
                if hs == LESS_AT and ph:
                    log_corrected(nc.gpsimd, pool, ph)
                if hs == U_AT and ph:
                    dt_times_x(nc.gpsimd, pool, ph)
                if d == 1 and b + 1 < B and hs == LN_AT[3] + 1:
                    layer_norm_scale(nc.gpsimd, pool, b + 1)

            def read_out(ph, k):
                n = ran(ph, k)
                pool.wait_ge(scanned, 2 * n + 2)
                if n >= HC_RING:
                    pool.wait_ge(summed, (n - HC_RING) // 4 + 1)
                if k == 0:
                    pool.wait_ge(c_in, SPREAD * (ph + 1))
                nc.gpsimd.tensor_tensor(hc[:, n % HC_RING, :], h[:, n % H_RING, :], c_rep[:, ph % 2, :],
                                        ALU.mult).then_inc(hc_done, 1)

            for hs in range(HS):
                front(0, hs)
            for ph in range(PHASES):
                for k in range(UNITS):
                    read_out(ph, k)
                    if ph + 1 < PHASES:
                        front(ph + 1, 2 * k)
                        front(ph + 1, 2 * k + 1)

        @block.vector
        def _(dve):
            def front(ph, hs):
                d, b = ph % 2, ph // 2
                if hs == LOST_AT:
                    dve.wait_ge(pool_step, P(ph, "y1"))
                    nc.vector.scalar_tensor_tensor(out=t4[:, :], in0=t3[:, :], scalar=-1.0, in1=t4[:, :],
                                                   op0=ALU.add, op1=ALU.subtract).then_inc(dve_step, 1)
                if hs == LESS_AT + 2 and ph == 0:
                    log_corrected(nc.vector, dve, ph)
                if hs == MAX_AT:
                    dve.wait_ge(pool_step, P(ph, "l"))
                    nc.vector.scalar_tensor_tensor(out=t2[:, :], in0=t2[:, :], scalar=0.0, in1=t1[:, :],
                                                   op0=ALU.max, op1=ALU.add).then_inc(dve_step, 1)
                if hs == MAX_AT + 1 and ph == 0:
                    dt_times_x(nc.vector, dve, ph)
                for th, at in enumerate(OUT_AT):
                    if d == 1 and b > 0 and hs == at + 2:
                        add_out(b - 1, th, J(ph, f"out{th}"))
                if hs == DR_AT:
                    dve.wait_ge(act_step, A(ph, "dh"))
                    nc.vector.tensor_tensor(t4[:, :], t2[:, :], dt_parts[:, 0, :], ALU.subtract).then_inc(dve_step, 1)
                if hs == DL_AT:
                    dve.wait_ge(act_step, A(ph, "dm"))
                    nc.vector.tensor_tensor(dt_parts[:, 2, :], t4[:, :], dt_parts[:, 1, :],
                                            ALU.subtract).then_inc(dve_step, 1)
                if hs == UR_AT:
                    dve.wait_ge(act_step, A(ph, "uh"))
                    nc.vector.tensor_tensor(t2[:, :], t3[:, :], u_parts[:, 0, :], ALU.subtract).then_inc(dve_step, 1)
                if hs == UL_AT:
                    dve.wait_ge(act_step, A(ph, "um"))
                    nc.vector.tensor_tensor(u_parts[:, 2, :], t2[:, :], u_parts[:, 1, :],
                                            ALU.subtract).then_inc(dve_step, 1)

            def add_out(b, th, job):
                dve.wait_ge(job_done, job)
                nc.vector.scalar_tensor_tensor(out=x1[:, b, cols(th)], in0=f_ps[0:C, :], scalar=0.5,
                                               in1=x1[:, b, cols(th)], op0=ALU.mult, op1=ALU.add).then_inc(job_read, 1)

            def take_y(ph, tile):
                d, b = ph % 2, ph // 2
                s = slice(0, L) if tile == 0 else slice(L, SPAN)
                src = y_ps[:, :, :].rearrange("p a n -> p (a n)") if tile == 0 else y_ps[:, 0, :]
                dve.wait_ge(summed, QUADS * ph + (4 if tile == 0 else 6))
                if d == 0:
                    if b > 0 and tile == 0:
                        dve.wait_ge(job_done, J(2 * b + 1, "out1"))
                    nc.vector.scalar_tensor_tensor(out=y[:, s], in0=xr[:, d, s], scalar=d_skip[:, tile:tile + 1],
                                                   in1=src, op0=ALU.mult, op1=ALU.add).then_inc(y_read, 1)
                    return
                dve.wait_ge(y_read, 2 * ph - 1 + tile)
                nc.vector.tensor_tensor(y[:, s], y[:, s], src, ALU.add).then_inc(y_read, 1)
                dve.wait_ge(y_read, 2 * ph + 1 + tile)
                nc.vector.scalar_tensor_tensor(out=y[:, s], in0=xr[:, d, s], scalar=d_skip[:, tile:tile + 1],
                                               in1=y[:, s], op0=ALU.mult, op1=ALU.add).then_inc(y_step, 1)

            def gate(b):
                dve.wait_ge(y_step, 3 * b + 2)
                dve.wait_ge(z_ready, b + 1)
                nc.vector.tensor_tensor(y[:, :], y[:, :], z[:, :], ALU.mult).then_inc(y_step, 1)

            def times_b(n):
                ph, hs = n // HS, n % HS
                if ph == PHASES:
                    return
                if hs == 0:
                    dve.wait_ge(b_in, SPREAD * (ph + 1))
                dve.wait_ge(u_spread, n + 1)
                nc.vector.tensor_tensor(u_ps[:, n % U_BANKS, :], u_ps[:, n % U_BANKS, :],
                                        b_rep[:, ph % 2, cols(halves(ph % 2)[hs % 2])], ALU.mult).then_inc(bu_done, 1)

            def scan(n):
                ph, i = n // HS, n % 2
                d, k = ph % 2, n // 2
                th = halves(d)[i]
                place = k % H_RING
                before = HALF - 1 if d == 0 else HALF
                dve.wait_ge(exp_done, n + 1)
                dve.wait_ge(bu_done, n + 1)
                if i == 0 and k >= H_RING:
                    dve.wait_ge(hc_done, k - H_RING + 1)
                if i == 1:
                    dve.wait_ge(scanned, n)
                nc.vector.tensor_tensor_scan(
                    scan_order(h[:, place, cols(th)], d), scan_order(a[:, k % A_RING, cols(th)], d),
                    scan_order(u_ps[:, n % U_BANKS, :], d), h[:, place, before:before + 1] if i else 0.0,
                    ALU.mult, ALU.add).then_inc(scanned, 1)

            nc.vector.memset(xn[:, 0:PAD], 0.0)
            nc.vector.memset(xn[:, PAD + L:], 0.0)
            nc.vector.memset(norm[:, 2:3], LN_EPS).then_inc(set_up, 1)
            dve.wait_ge(loaded[1], 16 * LOADS[1])
            for part in range(2):
                j = slice(2 * part, 2 * part + 2)
                nc.vector.tensor_tensor(w_taps[:, j, :], conv_w_rows[:, j, :],
                                        w_in.unsqueeze(1).broadcast_to([C, 2, E_IN]), ALU.mult)\
                    .then_inc(set_up, 1)
            dve.wait_ge(loaded[2], 16 * LOADS[2])
            nc.vector.tensor_copy(rep[:, :, :], rep_f).then_inc(set_up, 1)
            layer_norm_scale(nc.vector, dve, 0)
            dve.wait_ge(a_exp, 1)
            nc.vector.tensor_scalar(a_neg[:, :], a_neg[:, :], -1.0, None, ALU.mult).then_inc(set_up, 1)

            for hs in range(HS):
                front(0, hs)
            times_b(0)
            for ph in range(PHASES):
                for hs in range(HS):
                    n = HS * ph + hs
                    times_b(n + 1)
                    scan(n)
                    if ph + 1 < PHASES:
                        front(ph + 1, hs)
                    if hs == Y1_AT and ph > 0:
                        take_y(ph - 1, 1)
                        if ph % 2 == 0:
                            gate(ph // 2 - 1)
                    if hs == Y0_AT:
                        take_y(ph, 0)
            take_y(PHASES - 1, 1)
            gate(B - 1)
            for th in range(2):
                add_out(B - 1, th, ALL_JOBS + th + 1)
            dve.wait_ge(job_read, ALL_JOBS + 2)


def attention(nc, t, x1, scratch):
    scores_d, v_d, o_d = scratch
    with ExitStack() as ctx:
        def sb(name, shape, dt=F32):
            return ctx.enter_context(nc.sbuf_tensor(name, shape, dt))

        def ps(name, shape):
            return ctx.enter_context(nc.psum_tensor(name, shape, F32))

        def sem(name):
            return ctx.enter_context(nc.semaphore(name))

        qkv_w = sb("qkv_w", [C, 3 * C])
        qkv_s = sb("qkv_s", [C, 3 * C])
        qkv_b = sb("qkv_b", [128, 3])
        qkv_bias = sb("qkv_bias", [128, 3])
        qkv_scale = sb("qkv_scale", [128, 3])
        bn = sb("bn", [C, 3])
        bn_stats = sb("bn_stats", [C, 2 * B, nc.vector.BN_STATS_DIM])
        bn_mv = sb("bn_mv", [C, nc.vector.BN_AGGR_DIM])
        bn_scale, bn_shift = sb("bn_scale", [C, 1]), sb("bn_shift", [C, 1])
        w_up = sb("w_up", [128, WIN, 64])
        w_low = sb("w_low", [96, WIN, 64])
        rel = sb("rel", [128, HEADS // 2])
        dm_b = sb("dm_b", [128, 1])
        proj_w, proj_b = sb("proj_w", [C, C]), sb("proj_b", [C, 1])
        c1_w, c1_b = sb("c1_w", [C, 4 * C]), sb("c1_b", [128, 3])
        c2_w, c2_b = sb("c2_w", [128, 3, C]), sb("c2_b", [C, 1])
        qk = sb("qk", [128, 2, 2, HP, HP])
        v = sb("v", [C, 2, H, HP])
        zeros = sb("zeros", [IMAGES, R * V_ROW])
        x4 = sb("x4", [128, X4_RING, X4_ROWS, HP])
        sc = sb("sc", [128, 2, L])
        at = sb("at", [128, 2, K2, W])
        mx = sb("mx", [128, W])
        den = sb("den", [128, 2, W])
        vw = sb("vw", [128, 2, WIN, HD, HP])
        prod_v = sb("prod_v", [128, WIN, HD, W])
        prod_p = sb("prod_p", [128, WIN, HD, W])
        acc_v = sb("acc_v", [128, HD, W])
        acc_p = sb("acc_p", [128, HD, W])
        o_t = sb("o_t", [128, HD, W])
        o = sb("o", [C, L])
        up = sb("up", [128, 3, L])
        sc_ps = ps("sc_ps", [128, 2, 2, HALF])
        g_ps = ps("g_ps", [128, G_BANKS, HALF])

        loaded = [sem(f"l1_loaded{i}") for i in range(2)]
        padded = sem("padded")
        zeroed = sem("zeroed")
        bn_step = sem("bn_step")
        rel_ready = sem("rel_ready")
        job_done = sem("g_done")
        left_act = sem("left_act")
        left_dve = sem("left_dve")
        x4_in = [sem(f"x4_in{i}") for i in range(X4_RING // 2)]
        scored = sem("scored")
        sc_out = sem("sc_out")
        sc_stored = [sem(f"sc_stored{i}") for i in range(2)]
        sides = sem("sides")
        v_stored = [sem(f"v_stored{b}") for b in range(B)]
        at_in = [sem(f"at_in{i}") for i in range(2)]
        vw_in = [sem(f"vw_in{i}") for i in range(2)]
        soft = sem("soft")
        less = sem("less")
        exped = sem("exped")
        pv = sem("pv")
        pp = sem("pp")
        normed = sem("normed")
        o_stored = sem("o_stored")
        o_in = sem("o_in")
        out_s = sem("out_stored")

        block = ctx.enter_context(nc.Block())

        def pv_before(j):
            return sum(5 * n for n in DVE_ROWS[:j])

        def pp_before(j):
            return sum(5 * (WIN - n) - 1 for n in DVE_ROWS[:j])

        def job_list():
            seq = [("bias", m) for m in range(3)]
            for b in range(B):
                if b == 0:
                    seq += [("qkv", 0, i) for i in range(6)]
                for p in range(3 * b, 3 * b + 3):
                    if p == 3 * b and b + 1 < B:
                        seq += [("qkv", b + 1, i) for i in range(6)]
            seq += [("mlp", b, i) for b in range(B) for i in range(10)]
            return {name: n + 1 for n, name in enumerate(seq)}

        JOB = job_list()

        def by_dve(name):
            return name[0] == "bias" or name[0] == "mlp" and name[2] not in range(2, 8)

        def left(eng, name):
            mine = [n for n in JOB if by_dve(n) == by_dve(name)]
            eng.wait_ge(left_dve if by_dve(name) else left_act, mine.index(name) + 1)

        @block.sync
        def _(sp):
            first = [(qkv_w[:, :], t["qkv_w"]), (qkv_b[:, 0:1], t["qkv_b"][0:128]),
                     (qkv_b[0:64, 1:2], t["qkv_b"][128:192]), (qkv_b[0:C, 2:3], t["qkv_b"][192:288]),
                     (qkv_scale[:, :], t["qkv_scale"]), (bn[:, 0:1], t["bn_gamma"]), (bn[:, 1:2], t["bn_beta"])]
            second = [(w_up[:, :, 0:K2], t["dm_w"][0:128]), (w_low[:, :, 0:K2], t["dm_w"][128:224])]
            for i in range(2):
                rows = slice(64 * i, 64 * i + K2)
                second += [(rel[rows, :], t["rel_bias"][:, i::2]), (dm_b[rows, :], t["dm_b"])]
            second += [(proj_w[:, :], t["proj_w"]), (proj_b[:, :], t["proj_b"]), (c1_w[:, :], t["c1_w"]),
                       (c1_b[:, :], t["c1_b"]), (c2_w[:, :, :], t["c2_w"]), (c2_b[:, :], t["c2_b"])]
            assert [len(first), len(second)] == L1_LOADS
            with nc.allow_non_contiguous_dma(reason="small weights"):
                for loads, done in zip((first, second), loaded):
                    for dst, src in loads:
                        sp.dma_start(dst, src).then_inc(done, 16)
                    if loads is first:
                        sp.wait_ge(padded, 1)
            sp.wait_ge(zeroed, 2)
            for side in (0, R + H):
                sp.dma_start(v_d[:, side:side + R].rearrange("i r c x -> i (r c x)"), zeros[:, :])\
                    .then_inc(sides, 16)

            def put_x4(p):
                b = p // 3
                if p % 3 == 0:
                    left(sp, ("qkv", b, 3))
                if p >= X4_RING // 2:
                    sp.wait_ge(scored, 2 * (p - X4_RING // 2) + 2)
                for i in range(2):
                    hd = 2 * (p % 3) + i
                    for j in range(4):
                        rows = X4_ROWS if j < 3 else H
                        sp.dma_start(x4[32 * j:32 * j + 32, (2 * p + i) % X4_RING, 0:rows, :],
                                     qk[32 * (hd % 4):32 * (hd % 4) + 32, hd // 4, b % 2, j:j + rows, :])\
                            .then_inc(x4_in[p % (X4_RING // 2)], 16)

            def store_v(b):
                left(sp, ("qkv", b, 5))
                for hd in range(HEADS):
                    sp.dma_start(v_d[HEADS * b + hd, R:R + H].rearrange("y c x -> c y x"),
                                 v[HD * hd:HD * hd + HD, b % 2, :, :]).then_inc(v_stored[b], 16)

            def load_tile(j):
                for i in range(2):
                    sp.wait_ge(sc_stored[i], 32 * (j + 1))
                if j >= 2:
                    sp.wait_ge(pv, pv_before(j - 1))
                    sp.wait_ge(pp, pp_before(j - 1))
                for i in range(4):
                    sp.dma_start(at[32 * i:32 * i + 32, j % 2, :, :],
                                 scores_d[4 * j + i].rearrange("k (y x) -> y k x", x=W)).then_inc(at_in[j % 2], 16)
                sp.wait_ge(sides, 32)
                for b in range(4 * j // HEADS, (4 * j + 3) // HEADS + 1):
                    sp.wait_ge(v_stored[b], 16 * HEADS)
                for i in range(4):
                    src = v_d[4 * j + i]
                    win = bass.AP(src.tensor, src.offset, [[V_ROW, H], [1, WIN * V_ROW]])
                    sp.dma_start(vw[32 * i:32 * i + 32, j % 2].rearrange("p r c x -> p (r c x)"), win)\
                        .then_inc(vw_in[j % 2], 16)

            def store_o(j):
                sp.wait_ge(normed, j + 1)
                for i in range(4):
                    sp.dma_start(o_d[4 * j + i].rearrange("c (y x) -> y c x", x=W), o_t[32 * i:32 * i + 32, :, :])\
                        .then_inc(o_stored, 16)

            def load_o(b):
                sp.wait_ge(o_stored, 64 * ((HEADS * b + HEADS - 1) // 4 + 1))
                if b:
                    sp.wait_ge(job_done, JOB["mlp", b - 1, 1])
                sp.dma_start(o[:, :], o_d[HEADS * b:HEADS * (b + 1)].rearrange("i c n -> (i c) n")).then_inc(o_in, 16)

            put_x4(0)
            put_x4(1)
            store_v(0)
            put_x4(2)
            for p in range(PAIRS):
                if p + 3 < PAIRS:
                    put_x4(p + 3)
                if p % 3 == 0 and p // 3 + 1 < B:
                    store_v(p // 3 + 1)
                if p % 2:
                    load_tile(p // 2)
                if p % 2 == 0 and p >= 4:
                    store_o(p // 2 - 2)
                    if p // 2 - 2 == LAST_TILE[0]:
                        load_o(0)
            load_o(1)
            for j in range(TILES - 2, TILES):
                store_o(j)
                load_o(LAST_TILE.index(j))
            for b in range(B):
                for th in range(2):
                    left(sp, ("mlp", b, 8 + th))
                    sp.dma_start(t["out"][b][:, cols(th)], x1[:, b, cols(th)]).then_inc(out_s, 16)
            sp.wait_ge(out_s, 32 * B)
            sp.wait_ge(o_stored, 16 * IMAGES)

        @block.tensor
        def _(pe):
            def free(job):
                if job > G_BANKS:
                    left(pe, list(JOB)[job - G_BANKS - 1])

            def bank(job):
                return g_ps[:, job % G_BANKS, :]

            def qkv(b, i):
                n = JOB["qkv", b, i]
                free(n)
                m, th = i // 2, i % 2
                w = (slice(0, 128), slice(128, 192), slice(192, 288))[m]
                pe.matmul(bank(n)[0:w.stop - w.start, :], qkv_s[:, w], x1[:, b, cols(th)], start=True,
                          stop=True).then_inc(job_done, 1)

            def score(p):
                pe.wait_ge(x4_in[p % 3], 16 * 8 * (p // 3 + 1))
                for th in range(2):
                    if p >= 2:
                        pe.wait_ge(sc_out, 2 * (p - 2) + th + 1)
                    for dx in range(WIN):
                        for w, rows, y0 in ((w_up, 128, 0), (w_low, 96, 4)):
                            for i in range(2):
                                y = 16 * th + y0
                                mm = pe.matmul(sc_ps[64 * i:64 * i + 64, p % 2, th, :], w[:, dx, :],
                                               x4[0:rows, (2 * p + i) % X4_RING, y:y + 16, dx:dx + W],
                                               start=(dx == 0 and y0 == 0), stop=(dx == WIN - 1 and y0 == 4))
                    mm.then_inc(scored, 1)

            def mlp(b, i):
                n = JOB["mlp", b, i]
                free(n)
                if i < 2:
                    if i == 0:
                        pe.wait_ge(o_in, 16 * (b + 1))
                    pe.matmul(bank(n)[0:C, :], proj_w[:, :], o[:, cols(i)], start=True, stop=True)\
                        .then_inc(job_done, 1)
                elif i < 8:
                    m, th = (i - 2) % 3, (i - 2) // 3
                    left(pe, ("mlp", b, th))
                    pe.matmul(bank(n)[:, :], c1_w[:, 128 * m:128 * m + 128], x1[:, b, cols(th)], start=True,
                              stop=True).then_inc(job_done, 1)
                else:
                    th = i - 8
                    left(pe, ("mlp", b, 4 + 3 * th))
                    for m in range(3):
                        mm = pe.matmul(bank(n)[0:C, :], c2_w[:, m, :], up[:, m, cols(th)], start=(m == 0),
                                       stop=(m == 2))
                    mm.then_inc(job_done, 1)

            pe.wait_ge(loaded[0], 16 * L1_LOADS[0])
            pe.wait_ge(bn_step, BN_DONE)
            for m, w in enumerate((slice(0, 128), slice(128, 192), slice(192, 288))):
                n = JOB["bias", m]
                pe.matmul(bank(n)[0:w.stop - w.start, 0:1], qkv_w[:, w], bn_shift[:, :], start=True,
                          stop=True).then_inc(job_done, 1)
            for i in range(6):
                qkv(0, i)
            pe.wait_ge(loaded[1], 16 * L1_LOADS[1])
            for p in range(PAIRS):
                if p % 3 == 0 and p // 3 + 1 < B:
                    for i in range(6):
                        qkv(p // 3 + 1, i)
                score(p)
            for b in range(B):
                for i in range(10):
                    mlp(b, i)

        @block.scalar
        def _(act):
            def qkv(b, i):
                n = JOB["qkv", b, i]
                m, th = i // 2, i % 2
                act.wait_ge(job_done, n)
                y0 = 16 * th
                rows = (128, 64, C)[m]
                src = g_ps[0:rows, n % G_BANKS, :].rearrange("p (y x) -> p y x", x=W)
                if m < 2:
                    if b >= 2 and i == 0:
                        for s in x4_in:
                            act.wait_ge(s, 16 * 8 * (b - 1))
                    dst = qk[0:rows, m, b % 2, R + y0:R + y0 + 16, R:R + W]
                else:
                    if b >= 2 and th == 0:
                        act.wait_ge(v_stored[b - 2], 16 * HEADS)
                    dst = v[:, b % 2, y0:y0 + 16, R:R + W]
                nc.scalar.activation(dst, src, ACT.Identity, bias=qkv_bias[0:rows, m:m + 1],
                                     scale=qkv_scale[0:rows, m:m + 1]).then_inc(left_act, 1)

            def store_scores(p):
                if p == 0:
                    act.wait_ge(rel_ready, 1)
                for th in range(2):
                    act.wait_ge(scored, 2 * p + th + 1)
                    if p >= 2 and th == 0:
                        act.wait_ge(sc_stored[p % 2], 32 * (p // 2))
                    nc.scalar.activation(sc[:, p % 2, cols(th)], sc_ps[:, p % 2, th, :], ACT.Identity,
                                         bias=rel[:, p % 3:p % 3 + 1]).then_inc(sc_out, 1)
                act.wait_ge(sc_out, 2 * p + 2)
                for i in range(2):
                    act.dma_start(scores_d[2 * p + i], sc[64 * i:64 * i + K2, p % 2, :]).then_inc(sc_stored[p % 2], 16)

            def exps(j):
                act.wait_ge(less, j + 1)
                nc.scalar.activation(at[:, j % 2], at[:, j % 2], ACT.Exp).then_inc(exped, 1)

            def mlp(b):
                for i in range(2, 8):
                    n = JOB["mlp", b, i]
                    m, th = (i - 2) % 3, (i - 2) // 3
                    act.wait_ge(job_done, n)
                    nc.scalar.activation(up[:, m, cols(th)], g_ps[:, n % G_BANKS, :], ACT.Gelu,
                                         bias=c1_b[:, m:m + 1]).then_inc(left_act, 1)

            act.wait_ge(bn_step, BN_VAR)
            nc.scalar.activation(bn_scale[:, :], bn_mv[:, 1:2], ACT.Sqrt, bias=bn[:, 2:3]).then_inc(bn_step, 1)
            act.wait_ge(left_dve, 3)
            act.wait_ge(zeroed, 1)
            for i in range(6):
                qkv(0, i)
            for p in range(PAIRS):
                if p % 3 == 0 and p // 3 + 1 < B:
                    for i in range(6):
                        qkv(p // 3 + 1, i)
                if p % 2 == 0 and p:
                    exps(p // 2 - 1)
                store_scores(p)
            exps(TILES - 1)
            for b in range(B):
                mlp(b)

        def product(engine, j, dy, prod):
            e = at[:, j % 2, WIN * dy:WIN * dy + WIN, :].unsqueeze(2).broadcast_to([128, WIN, HD, W])
            win = vw[:, j % 2, dy]
            shifted = bass.AP(win.tensor, win.offset, [list(win.ap[0]), [1, WIN], [HP, HD], [1, W]])
            return engine.tensor_tensor(prod[:, :, :, :], shifted, e, ALU.mult)

        def fold(engine, eng, s, base, prod, acc, first):
            for n, (lo, hi) in enumerate((((0, 3), (4, 7)), ((0, 2), (2, 4)))):
                eng.wait_ge(s, base + n)
                engine.tensor_tensor(prod[:, lo[0]:lo[1]], prod[:, lo[0]:lo[1]], prod[:, hi[0]:hi[1]],
                                     ALU.add).then_inc(s, 1)
            eng.wait_ge(s, base + 2)
            if first:
                engine.tensor_tensor(acc[:, :, :], prod[:, 0], prod[:, 1], ALU.add).then_inc(s, 1)
                return
            engine.tensor_tensor(prod[:, 0], prod[:, 0], prod[:, 1], ALU.add).then_inc(s, 1)
            eng.wait_ge(s, base + 3)
            engine.tensor_tensor(acc[:, :, :], acc[:, :, :], prod[:, 0], ALU.add).then_inc(s, 1)

        @block.gpsimd
        def _(pool):
            nc.gpsimd.memset(qk[:, :, :, :, :], 0.0)
            nc.gpsimd.memset(v[:, :, :, :], 0.0).then_inc(zeroed, 1)
            nc.gpsimd.memset(zeros[:, :], 0.0).then_inc(zeroed, 1)
            for j in range(TILES):
                pool.wait_ge(soft, 3 * j + 1)
                pool.wait_ge(at_in[j % 2], 64 * (j // 2 + 1))
                nc.gpsimd.tensor_tensor(at[:, j % 2], at[:, j % 2],
                                        mx[:, :].unsqueeze(1).broadcast_to([128, K2, W]),
                                        ALU.subtract).then_inc(less, 1)
                pool.wait_ge(exped, j + 1)
                pool.wait_ge(vw_in[j % 2], 64 * (j // 2 + 1))
                for n, dy in enumerate(range(DVE_ROWS[j], WIN)):
                    base = pp_before(j) + max(5 * n - 1, 0)
                    if n == 0 and j:
                        pool.wait_ge(normed, j)
                    if base:
                        pool.wait_ge(pp, base)
                    product(nc.gpsimd, j, dy, prod_p).then_inc(pp, 1)
                    fold(nc.gpsimd, pool, pp, base + 1, prod_p, acc_p, n == 0)

        @block.vector
        def _(dve):
            nc.vector.memset(w_up[:, :, :], 0.0)
            nc.vector.memset(w_low[:, :, :], 0.0)
            nc.vector.memset(rel[:, :], 0.0)
            nc.vector.memset(dm_b[:, :], 0.0)
            nc.vector.memset(bn[:, 2:3], BN_EPS).then_inc(padded, 1)
            for n in range(2 * B):
                nc.vector.bn_stats(bn_stats[:, n, :], x1[:, n // 2, cols(n % 2)]).then_inc(bn_step, 1)
            dve.wait_ge(bn_step, 2 * B)
            nc.vector.bn_aggr(bn_mv[:, :], bn_stats[:, :, :]).then_inc(bn_step, 1)
            dve.wait_ge(bn_step, BN_VAR + 1)
            nc.vector.reciprocal(bn_scale[:, :], bn_scale[:, :]).then_inc(bn_step, 1)
            dve.wait_ge(loaded[0], 16 * L1_LOADS[0])
            dve.wait_ge(bn_step, BN_VAR + 2)
            nc.vector.tensor_tensor(bn_scale[:, :], bn_scale[:, :], bn[:, 0:1], ALU.mult).then_inc(bn_step, 1)
            dve.wait_ge(bn_step, BN_VAR + 3)
            nc.vector.tensor_tensor(bn_shift[:, :], bn_mv[:, 0:1], bn_scale[:, :], ALU.mult).then_inc(bn_step, 1)
            dve.wait_ge(bn_step, BN_VAR + 4)
            nc.vector.tensor_tensor(bn_shift[:, :], bn[:, 1:2], bn_shift[:, :], ALU.subtract).then_inc(bn_step, 1)
            nc.vector.tensor_scalar(qkv_s[:, :], qkv_w[:, :], bn_scale[:, 0:1], None, ALU.mult).then_inc(bn_step, 1)
            for m, rows in enumerate((128, 64, C)):
                n = JOB["bias", m]
                dve.wait_ge(job_done, n)
                nc.vector.scalar_tensor_tensor(out=qkv_bias[0:rows, m:m + 1], in0=g_ps[0:rows, n % G_BANKS, 0:1],
                                               scalar=qkv_b[0:rows, m:m + 1], in1=qkv_scale[0:rows, m:m + 1],
                                               op0=ALU.add, op1=ALU.mult).then_inc(left_dve, 1)
            dve.wait_ge(loaded[1], 16 * L1_LOADS[1])
            nc.vector.tensor_scalar(rel[:, :], rel[:, :], dm_b[:, 0:1], None, ALU.add).then_inc(rel_ready, 1)

            def mlp_out(b, i):
                n = JOB["mlp", b, i]
                bias = proj_b if i < 2 else c2_b
                dve.wait_ge(job_done, n)
                if i >= 8:
                    left(dve, ("mlp", b, i - 8))
                nc.vector.scalar_tensor_tensor(out=x1[:, b, cols(i % 2)], in0=g_ps[0:C, n % G_BANKS, :],
                                               scalar=bias[:, 0:1], in1=x1[:, b, cols(i % 2)],
                                               op0=ALU.add, op1=ALU.add).then_inc(left_dve, 1)

            def maximum(j):
                dve.wait_ge(at_in[j % 2], 64 * (j // 2 + 1))
                if j:
                    dve.wait_ge(less, j)
                nc.vector.tensor_reduce(mx[:, :], at[:, j % 2].rearrange("p k x -> p x k"), AX.X, ALU.max)\
                    .then_inc(soft, 1)

            def tile(j):
                dve.wait_ge(exped, j + 1)
                nc.vector.tensor_reduce(den[:, 0, :], at[:, j % 2].rearrange("p k x -> p x k"), AX.X, ALU.add)\
                    .then_inc(soft, 1)
                dve.wait_ge(soft, 3 * j + 2)
                nc.vector.reciprocal(den[:, 1, :], den[:, 0, :]).then_inc(soft, 1)
                dve.wait_ge(vw_in[j % 2], 64 * (j // 2 + 1))
                for n, dy in enumerate(range(DVE_ROWS[j])):
                    base = pv_before(j) + max(5 * n - 1, 0)
                    if n == DVE_ROWS[j] - 1 and j + 1 < TILES:
                        maximum(j + 1)
                    for m, i in DVE_MLP.get((j, n), ()):
                        mlp_out(m, i)
                        mlp_out(m, i + 1)
                    if base:
                        dve.wait_ge(pv, base)
                    product(nc.vector, j, dy, prod_v).then_inc(pv, 1)
                    fold(nc.vector, dve, pv, base + 1, prod_v, acc_v, n == 0)
                base = pv_before(j + 1) - 1
                dve.wait_ge(pv, base)
                dve.wait_ge(pp, pp_before(j + 1))
                nc.vector.tensor_tensor(acc_v[:, :, :], acc_v[:, :, :], acc_p[:, :, :], ALU.add).then_inc(pv, 1)
                dve.wait_ge(pv, base + 1)
                dve.wait_ge(soft, 3 * j + 3)
                if j:
                    dve.wait_ge(o_stored, 64 * j)
                nc.vector.tensor_tensor(o_t[:, :, :], acc_v[:, :, :],
                                        den[:, 1, :].unsqueeze(1).broadcast_to([128, HD, W]),
                                        ALU.mult).then_inc(normed, 1)

            maximum(0)
            for j in range(TILES):
                tile(j)
            for i in (0, 1, 8, 9):
                mlp_out(B - 1, i)



def parts_in_dram(nc):
    return [tuple(nc.dram_tensor(f"{n}_{m}", (PARTS, c, L), BF16, kind="Internal").ap()
                  for m, c in (("low", E_LO), ("high", E_HI))) for n in ("dt", "u")]


def program(nc, t):
    scratch = (nc.dram_tensor("scores_d", (IMAGES, K2, L), F32, kind="Internal").ap(),
               nc.dram_tensor("v_d", (IMAGES, HP, HD, HP), F32, kind="Internal").ap(),
               nc.dram_tensor("o_d", (IMAGES, HD, L), F32, kind="Internal").ap())
    with nc.sbuf_tensor("x1", [C, B, L], F32) as x1:
        mamba(nc, t, x1, *parts_in_dram(nc))
        attention(nc, t, x1, scratch)


def constants():
    center = np.stack([np.eye(C) - 1.0 / C, np.full((C, C), 1.0 / C)], 1)
    rep = np.zeros((PARTS, 32, 4, GE, N_ST))
    pick = np.zeros((GE, N_ST, 8, 32))
    for e in range(GE):
        for q in range(4):
            rep[:, GE * q + e, q, e, :] = 1.0
            pick[e, :, q, 4 * e + q] = 1.0
            pick[e, :, 4 + q, 16 * (q % 2) + 2 * e + q // 2] = 1.0
    q_scale = np.ones((128, 3))
    q_scale[:, 0:2] = np.tile(np.repeat([HD ** -0.5, 1.0], HD), 4)[:, None]
    return {"center": center, "rep": rep.reshape(PARTS * 32, 4, 128), "pick": pick.reshape(128, 8, 32),
            "qkv_scale": q_scale}


def by_unit(v):
    low = v[:E_LO].reshape(4, GE, 4, N_ST).transpose(1, 3, 2, 0).reshape(128, 16)
    high = v[E_LO:].reshape(4, GE, 2, N_ST).transpose(1, 3, 2, 0).reshape(128, 8)
    return np.concatenate([low, high], 1)


def kernel(**inputs):
    import concourse.bacc as _bacc
    from concourse.bass_utils import run_bass_kernel_spmd as _run

    g = {k.replace("L0_conv_", "").replace("L1_conv_", ""): np.asarray(v) for k, v in inputs.items()}

    def col(v):
        return v.reshape(-1, 1)

    order = [s * C + hd * HD + c for hd in range(HEADS) for s in range(2) for c in range(HD)] + \
        list(range(2 * C, 3 * C))
    arrays = {
        "x": g["x"].reshape(B, C, L), "gamma": col(g["gamma"]), "beta": col(g["beta"]), "W_in": g["W_in"],
        "conv_w": g["conv_w"].T.reshape(1, TAPS * E_IN), "conv_b": col(g["conv_b"]), "W_xproj": g["W_xproj"],
        "W_dt": g["W_dt"], "b_dt": col(g["b_dt"]), "D": col(g["D"]), "W_out": g["W_out"],
        "A_log": by_unit(g["A_log"]),
        "bn_gamma": col(g["bn_gamma"]), "bn_beta": col(g["bn_beta"]),
        "qkv_w": g["qkv_w"][order].T, "qkv_b": col(g["qkv_b"][order]),
        "dm_w": g["dm_w"].transpose(2, 1, 3, 0).reshape(WIN * 2 * HD, WIN, K2), "dm_b": col(g["dm_b"]),
        "rel_bias": g["rel_bias"], "proj_w": g["proj_w"].T, "proj_b": col(g["proj_b"]),
        "c1_w": g["c1_w"].T, "c1_b": g["c1_b"].reshape(3, 128).T,
        "c2_w": g["c2_w"].T.reshape(3, 128, C).transpose(1, 0, 2), "c2_b": col(g["c2_b"]),
    }
    arrays.update({k: v.astype(np.float32) for k, v in constants().items()})
    nc = _bacc.Bacc("TRN2", target_bir_lowering=False, num_devices=1)
    t, feed = {}, {}
    for name, v in arrays.items():
        v = np.ascontiguousarray(v)
        feed[f"in_{name}"] = v
        t[name] = nc.dram_tensor(f"in_{name}", v.shape, F32, kind="ExternalInput").ap()
    t["out"] = nc.dram_tensor("out_x", (B, C, L), F32, kind="ExternalOutput").ap()
    program(nc, t)
    r = _run(nc, [feed], core_ids=[0])
    return r.results[0]["out_x"].reshape(B, C, H, W)
```
